# Optimizing a Trainium2 kernel written in Bass

```python
import numpy as np
import jax
import jax.numpy as jnp

def _softmax(x, axis=-1):
    return jax.nn.softmax(x, axis=axis)

def _gelu(x):
    return jax.nn.gelu(x, approximate=True)

def _silu(x):
    return jax.nn.silu(x)

def _sigmoid(x):
    return jax.nn.sigmoid(x)

def _layernorm(x, axis=-1, eps=1e-05):
    m = jnp.mean(x, axis=axis, keepdims=True)
    v = jnp.var(x, axis=axis, keepdims=True)
    return (x - m) / jnp.sqrt(v + eps)

def _scatter_add(tgt, idx, src, axis=0):
    return tgt.at[idx].add(src)

def _segment_sum(src, seg, n):
    return jax.ops.segment_sum(src, seg, n)
kernel_name = 'mk_adj_ffn_d1_adj_r2_a2069b'

def setup_inputs(seed: int=0):
    np.random.seed(seed)
    _w = jnp.asarray

    def _rec_inputs():
        import jax
        import jax.numpy as jnp
        _gk = jax.random.key(seed)
        x = -0.0005207 + 1.001 * jax.random.normal(jax.random.fold_in(_gk, 1), (4096, 128), jnp.float32)
        _a = jax.random.bernoulli(jax.random.fold_in(_gk, 2), 0.000488281, (4096, 4096))
        adj = _a.astype(jnp.int32)
        return (x, adj)
    x, adj = _rec_inputs()

    def _L0_gnn_setup():
        import jax, jax.numpy as jnp
        import numpy as np
        MIN_NORM = 1e-15
        EPS = 1e-07
        MASK_FILL = -9000000000000000.0

        def logmap0(x, c):
            K = 1.0 / c
            sqrtK = K ** 0.5
            y = x[:, 1:]
            y_norm = jnp.clip(jnp.linalg.norm(y, axis=-1, keepdims=True), MIN_NORM)
            theta = jnp.clip(x[:, :1] / sqrtK, 1.0 + EPS)
            res = sqrtK * jnp.arccosh(theta) * y / y_norm
            return jnp.concatenate([jnp.zeros_like(x[:, :1]), res], axis=1)

        def proj(x, c):
            K = 1.0 / c
            y = x[:, 1:]
            x0 = jnp.sqrt(K + jnp.sum(y * y, axis=-1, keepdims=True))
            return jnp.concatenate([x0, y], axis=1)

        def expmap0(u, c):
            K = 1.0 / c
            sqrtK = K ** 0.5
            x = u[:, 1:]
            x_norm = jnp.clip(jnp.linalg.norm(x, axis=-1, keepdims=True), MIN_NORM)
            theta = x_norm / sqrtK
            res = jnp.concatenate([sqrtK * jnp.cosh(theta), sqrtK * jnp.sinh(theta) * x / x_norm], axis=1)
            return proj(res, c)
        key = jax.random.key(seed)
        k1, k2, k3, k4, k5 = jax.random.split(key, 5)
        N, D_in, D_out = (4096, 128, 128)
        x = jax.random.normal(k1, (N, D_in), dtype=jnp.float32)
        adj = jax.random.randint(k2, (N, N), 0, 2, dtype=jnp.int32)
        W_gcn = jax.random.normal(k3, (D_in - 1, D_out - 1), dtype=jnp.float32)
        std_w = 1.414 * (2.0 / (D_out + D_out)) ** 0.5
        W_att = jax.random.normal(k4, (D_out, D_out), dtype=jnp.float32) * std_w
        std_a = 1.414 * (2.0 / (2 * D_out + 1)) ** 0.5
        a_att = jax.random.normal(k5, (2 * D_out, 1), dtype=jnp.float32) * std_a
        return {'x': x, 'adj': adj, 'k': 1, 'W_gcn': W_gcn, 'W_att': W_att, 'a_att': a_att}
    _L0_gnn_all = _L0_gnn_setup()
    _L0_gnn_in = {k: v for k, v in _L0_gnn_all.items() if k in ('W_gcn', 'W_att', 'a_att')}
    del _L0_gnn_all

    def _L0_ffn_setup():
        import jax, jax.numpy as jnp
        import numpy as np
        TOP_K = 2
        key = jax.random.key(seed)
        ks = jax.random.split(key, 4)
        B, L, D, H, E = (8, 2048, 128, 512, 8)
        s = 0.02
        return {'x': jax.random.normal(ks[0], (B, L, D), jnp.float32), 'Wg': jax.random.normal(ks[1], (D, E), jnp.float32) * s, 'bg': jnp.zeros((E,), jnp.float32), 'W1': jax.random.normal(ks[2], (E, D, H), jnp.float32) * s, 'b1': jnp.zeros((E, H), jnp.float32), 'W2': jax.random.normal(ks[3], (E, H, D), jnp.float32) * s, 'b2': jnp.zeros((E, D), jnp.float32)}
    _L0_ffn_all = _L0_ffn_setup()
    _L0_ffn_in = {k: v for k, v in _L0_ffn_all.items() if k in ('Wg', 'bg', 'W1', 'b1', 'W2', 'b2')}
    del _L0_ffn_all
    return {'x': x, 'adj': adj, 'L0_gnn_W_gcn': _L0_gnn_in['W_gcn'], 'L0_gnn_W_att': _L0_gnn_in['W_att'], 'L0_gnn_a_att': _L0_gnn_in['a_att'], 'L0_ffn_Wg': _L0_ffn_in['Wg'], 'L0_ffn_bg': _L0_ffn_in['bg'], 'L0_ffn_W1': _L0_ffn_in['W1'], 'L0_ffn_b1': _L0_ffn_in['b1'], 'L0_ffn_W2': _L0_ffn_in['W2'], 'L0_ffn_b2': _L0_ffn_in['b2']}

def reference(x, adj, L0_gnn_W_gcn, L0_gnn_W_att, L0_gnn_a_att, L0_ffn_Wg, L0_ffn_bg, L0_ffn_W1, L0_ffn_b1, L0_ffn_W2, L0_ffn_b2):
    import jax
    import jax.numpy as jnp

    def _L0_gnn_ref(x, adj, k, W_gcn, W_att, a_att):
        import jax, jax.numpy as jnp
        import numpy as np
        MIN_NORM = 1e-15
        EPS = 1e-07
        MASK_FILL = -9000000000000000.0

        def logmap0(x, c):
            K = 1.0 / c
            sqrtK = K ** 0.5
            y = x[:, 1:]
            y_norm = jnp.clip(jnp.linalg.norm(y, axis=-1, keepdims=True), MIN_NORM)
            theta = jnp.clip(x[:, :1] / sqrtK, 1.0 + EPS)
            res = sqrtK * jnp.arccosh(theta) * y / y_norm
            return jnp.concatenate([jnp.zeros_like(x[:, :1]), res], axis=1)

        def proj(x, c):
            K = 1.0 / c
            y = x[:, 1:]
            x0 = jnp.sqrt(K + jnp.sum(y * y, axis=-1, keepdims=True))
            return jnp.concatenate([x0, y], axis=1)

        def expmap0(u, c):
            K = 1.0 / c
            sqrtK = K ** 0.5
            x = u[:, 1:]
            x_norm = jnp.clip(jnp.linalg.norm(x, axis=-1, keepdims=True), MIN_NORM)
            theta = x_norm / sqrtK
            res = jnp.concatenate([sqrtK * jnp.cosh(theta), sqrtK * jnp.sinh(theta) * x / x_norm], axis=1)
            return proj(res, c)
        c = float(k)
        N = x.shape[0]
        logx = logmap0(x, c)
        Wx = logx[:, 1:] @ W_gcn
        tmp = jnp.concatenate([jnp.zeros((N, 1), x.dtype), Wx], axis=1)
        fun7 = proj(expmap0(tmp, c), c)
        h_in = logmap0(fun7, c)
        h = h_in @ W_att
        F_ = h.shape[1]
        e = h @ a_att[:F_] + (h @ a_att[F_:]).T
        att = jnp.where(adj > 0, e, MASK_FILL)
        att = jax.nn.softmax(att, axis=1)
        h_prime = att @ h
        emb = jax.nn.elu(h_prime)
        emb = proj(emb, c)
        out = expmap0(jax.nn.sigmoid(logmap0(emb, c)), c)
        return out

    def _L0_ffn_ref(x, Wg, bg, W1, b1, W2, b2):
        import jax, jax.numpy as jnp
        import numpy as np
        TOP_K = 2
        B, L, D = x.shape
        E = W1.shape[0]
        xf = x.reshape(-1, D)
        gate_logits = xf @ Wg + bg
        top_w, top_i = jax.lax.top_k(gate_logits, TOP_K)
        top_w = jax.nn.softmax(top_w, axis=-1)
        w_dense = jnp.sum(jax.nn.one_hot(top_i, E, dtype=xf.dtype) * top_w[..., None], axis=1)
        out = jnp.zeros_like(xf)
        for e in range(E):
            h = jax.nn.gelu(xf @ W1[e] + b1[e], approximate=False)
            out = out + w_dense[:, e:e + 1] * (h @ W2[e] + b2[e])
        return out.reshape(B, L, D)
    x = x + _L0_gnn_ref(_layernorm(x, axis=-1), adj, 1, L0_gnn_W_gcn, L0_gnn_W_att, L0_gnn_a_att)
    x = x + _L0_ffn_ref(_layernorm(x, axis=-1)[None], L0_ffn_Wg, L0_ffn_bg, L0_ffn_W1, L0_ffn_b1, L0_ffn_W2, L0_ffn_b2)[0]
    return x

_drawn_inputs = setup_inputs


def setup_inputs(seed=0):
    import zlib

    import numpy as np

    out = dict(_drawn_inputs(seed))
    spreads = {'L0_ffn_bg': (0.0, 0.8), 'L0_ffn_b1': (0.0, 0.8), 'L0_ffn_b2': (0.0, 2.0)}
    factors = {'L0_ffn_Wg': 8.0, 'L0_ffn_W1': 8.0, 'L0_ffn_W2': 8.0}
    for name, (base, spread) in spreads.items():
        noise = np.random.default_rng([zlib.crc32(name.encode()), seed]).standard_normal(out[name].shape)
        drawn = base * np.exp(spread * noise) if base else spread * noise
        out[name] = jnp.asarray(drawn.astype(out[name].dtype))
    for name, factor in factors.items():
        out[name] = (out[name] * factor).astype(out[name].dtype)
    return out
```

```python
from contextlib import ExitStack

import numpy as np

import concourse.bass as bass
from concourse import mybir

F32 = mybir.dt.float32
BF16 = mybir.dt.bfloat16
I32 = mybir.dt.int32
U32 = mybir.dt.uint32
ALU = mybir.AluOpType
ACT = mybir.ActivationFunctionType
AX_X = mybir.AxisListType.X

P = 128
N = 4096
D = 128
NT = N // P
GB = 4
NB = NT // GB
DC = D - 1
G = D + 1
E = 8
H = 512
HK = H // P
TOP = 2
REGION = N + P
SLOTS = 72
SPARE = SLOTS - TOP * N // P
ROW = D + 2
LN_EPS = 1e-5
THETA_MIN = float(np.float32(1.0 + 1e-7))
CL = THETA_MIN ** 2 - 1.0
ROOT_CL = CL ** 0.5
NORM2_MIN = 1e-30
SPREAD_MAX = 50.0
LN_SCALE = 2.0 ** 36
HALF_LN_SCALE = 18.0 * float(np.log(2.0))
CH = NT // 4
PARTS = sorted(((p, c) for p in range(3) for c in range(4)), key=lambda pc: (pc[0] + pc[1], pc[0]))


class Steps:

    def __init__(self, eng, sem, start=0):
        self.eng, self.sem, self.base, self.n = eng, sem, start, 0

    def value(self):
        return self.base + self.n

    def did(self, ins):
        ins.then_inc(self.sem, 1)
        self.n += 1

    def settle(self):
        self.eng.wait_ge(self.sem, self.base + self.n)

    def step(self, ins):
        self.did(ins)
        self.settle()



def gnn_moe_kernel(nc, x_rows, xT_in, adjT, wg_in, wgT_in, wa_in, waT_in, a2_in,
                   gate_in, bg_in, w1_in, b1_in, w2_in, b2_in, out):
    disp = nc.dram_tensor("disp", [E * REGION + SPARE * P, ROW], F32).ap()
    unit = nc.dram_tensor("unit", [P, (2 * NT - 1) * P], I32).ap()
    planes = nc.dram_tensor("planes", [TOP * N + (E + SPARE) * P, D], F32).ap()
    with ExitStack() as ctx:
        def sb(name, shape, dt=F32):
            return ctx.enter_context(nc.sbuf_tensor(name, shape, dt))

        def sem(name):
            return ctx.enter_context(nc.semaphore(name))

        x = sb("x", [P, NT, D])
        hb = sb("hb", [P, NT * G])
        h3 = hb[:].rearrange("p (t g) -> p t g", g=G)
        b1b = hb[:, 0:E * H]
        gb = sb("gb", [P, NT * 3 * G], BF16)
        g = gb[:].rearrange("p (t a b) -> p t a b", a=3, b=G)
        w1 = sb("w1", [P, E * H])
        w2 = sb("w2", [P, E * HK * P])
        b2b = sb("b2b", [P, E * D])
        raw = sb("raw", [P, 4, N], I32)
        mask = sb("mask", [P, 2, N], BF16)
        xT = mask[:].rearrange("p a n -> p (a n)").bitcast(F32)
        rawf = raw[:].bitcast(F32).rearrange("p a n -> p (a n)")
        ident = sb("ident", [P, P])
        ones = sb("ones", [2, P])
        center = sb("center", [P, P])
        ltri = sb("ltri", [P, P], BF16)
        onesb = sb("onesb", [P, P], BF16)
        gatew = sb("gatew", [P, E])
        bgb = sb("bgb", [P, E])
        iota8 = sb("iota8", [P, E])
        region0 = sb("region0", [P, E])
        tokid = sb("tokid", [P, NT])
        ia = sb("ia", [P, SLOTS], I32)
        slotno = sb("slotno", [P, SLOTS])
        nhalf = sb("nhalf", [P, 1])
        sqj = sb("sqj", [P, 4, D])
        tk = sb("tk", [P, GB, G])
        ta = sb("ta", [P, GB, G])
        ty = sb("ty", [P, GB, D])
        te = sb("te", [P, GB, D])
        xlT = sb("xlT", [P, GB * P])
        xrow = sb("xrow", [P, 2, GB, TOP, ROW])
        hsum = sb("hsum", [P, G])
        vc = sb("vc", [P, 256])
        vec = sb("vec", [P, 28, NT])
        vt = sb("vt", [P, 3, NT])
        bv = sb("bv", [P, 29, GB])
        bt = sb("bt", [P, 3, GB])
        lg = sb("lg", [P, GB, E])
        top = sb("top", [P, GB, 8])
        idx = sb("idx", [P, GB, 8], U32)
        idxf = sb("idxf", [P, TOP, GB])
        onehot = sb("onehot", [P, TOP, GB, E])
        both = sb("both", [P, GB * E], BF16)
        run = sb("run", [P, GB + 1, E])
        rowid = sb("rowid", [P, GB, E])
        pick = sb("pick", [P, TOP * GB, E])
        slotf = sb("slotf", [P, TOP * GB])
        slot = sb("slot", [P, TOP * GB], U32)
        mm = sb("mm", [P, 8])
        flagi = sb("flagi", [P, 1], I32)
        padid = sb("padid", [P, E], U32)
        tabs = sb("tabs", [P, 3, SLOTS])
        tabi = sb("tabi", [P, 2, SLOTS], I32)
        cnt = sb("cnt", [P, 5, E])
        cnti = sb("cnti", [P, 2, E], I32)
        yid = sb("yid", [P, 4], U32)
        still = sb("still", [P, 6])
        pre = rawf[:, 3 * N:4 * N]
        wgT, waq, waT, a2, vraw = pre[:, 0:128], pre[:, 128:257], pre[:, 257:384], pre[:, 384:385], pre[:, 385:641]
        xc = pre[:, 1024:3072].rearrange("p (a t d) -> p a t d", a=2, d=D)
        cmpb = rawf[:, 8192:8192 + SLOTS * E].rearrange("p (s e) -> p s e", e=E)
        pad = rawf[:, 9216:9216 + E * ROW].rearrange("p (e r) -> p e r", r=ROW)
        sc_row, ex_row = (rawf[:, k * N:(k + 1) * N] for k in (1, 2))
        grp = rawf[:, 3 * N:3 * N + 5 * P].rearrange("p (a i) -> p a i", i=P)
        onesf, part_max, diag, row_max, h_sum = (grp[:, i, :] for i in range(5))
        gres = gb[:].bitcast(F32)[:, 0:N].rearrange("p (t d) -> p t d", d=D)
        xs = rawf[:, 0:8 * ROW].rearrange("p (s r) -> p s r", r=ROW)
        xsT = rawf[:, 2048:2048 + 4 * P].rearrange("p (s r) -> p s r", r=P)
        hs = rawf[:, 4096:4096 + 2 * H].rearrange("p (s r) -> p s r", r=H)
        hg = rawf[:, 5120:5120 + 2 * H].rearrange("p (s r) -> p s r", r=H)
        hT = rawf[:, 6144:6144 + 2 * H].rearrange("p (s r) -> p s r", r=H)
        ya = rawf[:, 7168:7168 + 2 * D].rearrange("p (s r) -> p s r", r=D)
        ys = rawf[:, 7424:7424 + 4 * D].rearrange("p (s r) -> p s r", r=D)
        yplane = [rawf[:, k * N:(k + 1) * N].rearrange("p (t d) -> p t d", d=D) for k in range(TOP)]
        spare = w1[:, 0:SPARE * ROW].rearrange("p (e r) -> p e r", r=ROW)

        ps = [ctx.enter_context(nc.psum_tensor(f"ps{i}", [P, 512], F32)) for i in range(8)]

        s_small = sem("small_weights_in")
        s_x = [sem(f"x_in{c}") for c in range(4)]
        s_xT = [sem(f"xT_in{c}") for c in range(4)]
        s_adj = [sem(f"adj_in{i}") for i in range(4)]
        s_w = sem("expert_weights_in")
        s_b1 = sem("b1_in")
        s_const = sem("constants")
        s_cdve = sem("centre_matrix")
        s_pc = sem("pool_steps")
        s_vs = sem("dve_steps")
        s_as = sem("act_steps")
        s_pw = sem("weight_products")
        s_pwc = sem("weight_products_copied")
        s_ft = sem("feature_products")
        s_fcd = sem("feature_rows_copied")
        s_fca = sem("feature_squares")
        s_xc = sem("centred")
        s_sq = sem("centred_squared")
        s_sqd = sem("squares_summed")
        s_va = sem("vectors_for_act")
        s_av = sem("vectors_from_act")
        s_al = sem("alpha_ready")
        s_u = sem("u_product")
        s_ub = sem("u_copied")
        s_hp = sem("hsum_product")
        s_mt = sem("extremes_ready")
        s_mb = sem("extremes_products")
        s_md = sem("extremes_taken")
        s_flag = sem("spread_known")
        s_wa = sem("wide_adj_in")
        s_wpm = sem("wide_partition_max")
        s_wt = sem("wide_max_turned")
        s_wd = sem("wide_max_diagonal")
        s_wm = sem("wide_max_spread")
        s_wx = sem("wide_exponents")
        s_we = sem("wide_exp_done")
        s_wp = sem("wide_weights")
        s_wo = sem("wide_sums")
        s_wr = sem("wide_rows_taken")
        s_wv = sem("wide_dve_steps")
        s_wu = sem("wide_identity")
        s_wuo = sem("wide_identity_out")
        s_ww = [sem(f"wide_window_in{k}") for k in range(GB)]
        s_gf = sem("g_rest")
        s_gc = sem("g_cast")
        s_mask = sem("mask_ready")
        s_at = sem("attention_done")
        s_pf = sem("attention_taken")
        s_tk = sem("take_dve_steps")
        s_e1 = sem("elu_operand")
        s_e2 = sem("elu_exp")
        s_y1 = sem("emb_ready")
        s_y2 = sem("emb_squared")
        s_al2 = sem("log_scale_ready")
        s_ex = sem("sigmoid_exp")
        s_sg = sem("sigmoid_ready")
        s_sg2 = sem("sigmoid_squared")
        s_r = sem("batch_vectors_for_act")
        s_ra = sem("batch_vectors_from_act")
        s_var = sem("variance")
        s_varr = sem("deviation")
        s_x1 = sem("x1_ready")
        s_x2 = sem("x1_squared")
        s_ns = sem("norm_scale_ready")
        s_xl = sem("xl_ready")
        s_bas = sem("batch_act_steps")
        s_tt = sem("xl_turned")
        s_ttc = sem("xl_turned_copied")
        s_lg = sem("logits")
        s_dl = sem("gate_difference")
        s_de = sem("gate_exp")
        s_m = sem("choice_ready")
        s_pr = sem("prefix_ready")
        s_sl = sem("rows_addressed")
        s_sp = sem("dispatch_begun")
        s_yp = sem("return_begun")
        s_spare = sem("spare_rows_out")
        s_sc = [sem(f"rows_dispatched{i}") for i in range(2)]
        s_pd = sem("padding_rows_out")
        s_ep = sem("epilogue_dve_steps")
        s_ch = sem("choice_dve_steps")
        s_plc = sem("place_dve_steps")
        s_tab = sem("tables_ready")
        s_pad = sem("padding_addressed")
        s_xsw = [sem(f"slot_rows_in{i}") for i in range(8)]
        s_T = sem("slot_turned")
        s_Tc = sem("slot_turned_copied")
        s_L1 = sem("layer1")
        s_bi = sem("biased")
        s_ge = sem("gelu_done")
        s_hT = sem("hidden_turned")
        s_hTc = sem("hidden_turned_copied")
        s_L2 = sem("layer2")
        s_ya = sem("layer2_biased")
        s_ys = sem("result_weighted")
        s_yi = sem("result_place")
        s_yo = [sem(f"result_out{i}") for i in range(4)]
        s_pl = [sem(f"planes_in{c}") for c in range(4)]
        s_fs = sem("final_steps")
        s_fin = sem("final_sum")
        s_out = sem("out_stored")

        block = ctx.enter_context(nc.Block())

        @block.sync
        def _(sp):
            sp.dma_start(wgT[0:DC, :], wgT_in).then_inc(s_small, 16)
            sp.dma_start(waq[0:DC, 0:D], wa_in).then_inc(s_small, 16)
            sp.dma_start(waT[:, 0:DC], waT_in).then_inc(s_small, 16)
            sp.dma_start(a2, a2_in).then_inc(s_small, 16)
            sp.dma_start(vraw[:, 0:DC], wg_in).then_inc(s_small, 16)
            for c in range(4):
                sp.dma_start(x[:, CH * c:CH * c + CH, :], x_rows[:, CH * c:CH * c + CH, :]).then_inc(s_x[c], 16)
                sp.dma_start(xT[:, 1024 * c:1024 * (c + 1)], xT_in[:, 1024 * c:1024 * (c + 1)]).then_inc(s_xT[c], 16)
            for t in range(3):
                sp.dma_start(raw[:, t, :], adjT[t]).then_inc(s_adj[t], 16)
            sp.dma_start(gatew[:], gate_in).then_inc(s_w, 16)
            sp.dma_start(bgb[:], bg_in.partition_broadcast(P)).then_inc(s_w, 16)
            sp.wait_ge(s_spare, 16)
            sp.dma_start(w1[:], w1_in).then_inc(s_w, 16)
            sp.dma_start(w2[:], w2_in).then_inc(s_w, 16)
            sp.dma_start(b2b[:], b2_in.partition_broadcast(P)).then_inc(s_w, 16)
            sp.wait_ge(s_sqd, 4)
            sp.wait_ge(s_pwc, 3)
            sp.dma_start(raw[:, 3, :], adjT[3]).then_inc(s_adj[3], 16)
            def stream(tile):
                with sp.Fori(1, NB) as q:
                    for k in range(GB):
                        src = tile(GB * q + k)
                        sp.wait_ge(s_mask, GB * q - GB + k + 1)
                        sp.dma_start(raw[:, k, :], src).then_inc(s_adj[k], 16)

            def window(t):
                return unit[:, bass.ds(t * P, N)]

            sp.wait_ge(s_flag, 1)
            wide = sp.value_load(flagi[0:1, 0:1], min_val=0, max_val=1)
            with sp.If(wide > 0):
                for k in range(GB):
                    sp.wait_ge(s_adj[k], 16)
                sp.dma_start(raw[:, 0, :], adjT[0]).then_inc(s_wa, 16)
                with sp.Fori(1, NT) as t:
                    sp.wait_ge(s_wr, t)
                    sp.dma_start(raw[:, 0, :], adjT[bass.ds(t, 1)].rearrange("a p n -> (a p) n")).then_inc(s_wa, 16)
                sp.wait_ge(s_wu, 1)
                sp.dma_start(unit[:, 0:(NT - 1) * P], raw[:, 1, 0:(NT - 1) * P]).then_inc(s_wuo, 16)
                sp.dma_start(unit[:, NT * P:], raw[:, 1, 0:(NT - 1) * P]).then_inc(s_wuo, 16)
                sp.dma_start(unit[:, (NT - 1) * P:NT * P], raw[:, 2, 0:P]).then_inc(s_wuo, 16)
                sp.wait_ge(s_wuo, 48)
                for k in range(GB):
                    sp.dma_start(raw[:, k, :], unit[:, k * P:k * P + N]).then_inc(s_ww[k], 16)
                stream(window)
            with sp.Else():
                stream(lambda t: adjT[bass.ds(t, 1)].rearrange("a p n -> (a p) n"))
            sp.wait_ge(s_gc, 12)
            sp.dma_start(b1b, b1_in.partition_broadcast(P)).then_inc(s_b1, 16)
            sp.wait_ge(s_tab, 1)
            for i in range(2):
                sp.wait_ge(s_sc[i], 16 * TOP * GB * NB // 2)
            sp.wait_ge(s_pd, 16 * E)

            def load(s, j):
                rb = sp.value_load(tabi[0:1, 0, bass.ds(s, 1)], min_val=0, max_val=E * REGION + (SPARE - 1) * P)
                sp.dma_start(xs[:, j, :], disp[bass.ds(rb, P), :]).then_inc(s_xsw[j], 16)

            for s in range(8):
                load(s, s)
            with sp.Fori(1, SLOTS // 8) as o:
                for j in range(8):
                    s = 8 * o + j
                    sp.wait_ge(s_T, s - 7)
                    sp.wait_ge(s_ys, s - 7)
                    sp.wait_ge(s_yi, s - 7)
                    load(s, j)
            for j in range(4):
                sp.wait_ge(s_yo[j], 16 * (SLOTS // 4))
            for c in range(4):
                for k in range(TOP):
                    src = planes[k * N + c * 1024:k * N + (c + 1) * 1024, :].rearrange("(t p) d -> p t d", p=P)
                    sp.dma_start(yplane[k][:, CH * c:CH * c + CH, :], src).then_inc(s_pl[c], 16)
            for c in range(4):
                sp.wait_ge(s_fin, c + 1)
                dst = out[c * 1024:(c + 1) * 1024, :].rearrange("(t p) d -> p t d", p=P)
                sp.dma_start(dst, x[:, CH * c:CH * c + CH, :]).then_inc(s_out, 16)
            sp.wait_ge(s_out, 64)

        @block.gpsimd
        def _(pool):
            st = Steps(pool, s_pc)
            st.did(pool.memset(ident[:], 0.0))
            st.did(pool.memset(ones[:], 1.0))
            st.did(pool.memset(onesb[:], 1.0))
            st.did(pool.memset(nhalf[:], -HALF_LN_SCALE))
            st.did(pool.memset(hsum[:, D:G], float(N)))
            st.did(pool.memset(spare, 0.0))
            st.did(pool.iota(ia[:, 0:NT], pattern=[[P, NT]], base=0, channel_multiplier=1))
            st.settle()
            pool.affine_select(out=ident[:], in_=ident[:], compare_op=ALU.not_equal, fill=1.0,
                               base=0, pattern=[[-1, P]], channel_multiplier=1).then_inc(s_const, 1)
            st.did(pool.affine_select(out=ltri[:], in_=onesb[:], compare_op=ALU.is_gt, fill=0.0,
                                      base=0, pattern=[[1, P]], channel_multiplier=-1))
            st.did(pool.tensor_copy(tokid[:], ia[:, 0:NT]))
            st.settle()
            st.step(pool.iota(ia[:, 0:SLOTS], pattern=[[1, SLOTS]], base=0, channel_multiplier=0))
            st.did(pool.tensor_copy(slotno[:], ia[:, 0:SLOTS]))
            st.did(pool.tensor_copy(iota8[:], ia[:, 0:E]))
            st.settle()
            st.step(pool.iota(ia[:, 0:E], pattern=[[REGION, E]], base=0, channel_multiplier=0))
            st.did(pool.tensor_copy(region0[:], ia[:, 0:E]))
            st.did(pool.tensor_copy(run[:, GB, :], ia[:, 0:E]))
            st.settle()
            st.step(pool.iota(ia[:, 0:SPARE], pattern=[[P, SPARE]], base=TOP * N + E * P, channel_multiplier=1))
            pool.tensor_copy(spare[:, :, D + 1], ia[:, 0:SPARE]).then_inc(s_const, 1)
            pool.wait_ge(s_const, 2)
            pool.dma_start(disp[E * REGION:, :].rearrange("(e p) r -> p e r", p=P), spare).then_inc(s_spare, 16)

            def pass_wait(i, done):
                pool.tensor_tensor(out=still[:, i:i + 1], in0=nhalf[:], in1=nhalf[:], op=ALU.add).then_inc(done, 1)

            with pool.Fori(0, NB // 2) as o:
                for par in range(2):
                    pool.wait_ge(s_sl, 2 * o + par + 1)
                    pass_wait(par, s_sp)
                    for c in range(TOP):
                        for k in range(GB):
                            i = c * GB + k
                            pool.indirect_dma_start(disp, bass.IndirectOffsetOnAxis(slot[:, i:i + 1], axis=0),
                                                    xrow[:, par, k, c, :], None).then_inc(s_sc[par], 16)
            pool.wait_ge(s_mask, NT)
            st.did(pool.memset(pad, 0.0))
            st.step(pool.iota(ia[:, 0:E], pattern=[[P, E]], base=TOP * N, channel_multiplier=1))
            st.step(pool.tensor_copy(pad[:, :, D + 1], ia[:, 0:E]))
            pool.wait_ge(s_pad, 1)
            for e in range(E):
                pool.indirect_dma_start(disp, bass.IndirectOffsetOnAxis(padid[:, e:e + 1], axis=0),
                                        pad[:, e, :], None).then_inc(s_pd, 16)
            with pool.Fori(0, SLOTS // 4) as o:
                for j in range(4):
                    s = 4 * o + j
                    pool.wait_ge(s_ys, s + 1)
                    pool.wait_ge(s_yi, s + 1)
                    pass_wait(2 + j, s_yp)
                    pool.indirect_dma_start(planes, bass.IndirectOffsetOnAxis(yid[:, j:j + 1], axis=0),
                                            ys[:, j, :], None).then_inc(s_yo[j], 16)

        @block.tensor
        def _(pe):
            mmul = pe.matmul
            pe.wait_ge(s_small, 80)
            mmul(ps[0][0:DC, 0:1], waT[:, 0:DC], a2, start=True, stop=True).then_inc(s_pw, 1)
            pe.wait_ge(s_pwc, 1)
            mmul(ps[0][:, 0:G], wgT[0:DC, :], waq[0:DC, :], start=True, stop=True).then_inc(s_pw, 1)
            pe.wait_ge(s_pwc, 2)
            pe.wait_ge(s_cdve, 1)
            mmul(ps[0][:, 0:256], center[:], vraw, start=True, stop=True).then_inc(s_pw, 1)
            pe.wait_ge(s_pwc, 3)
            for t in range(NT):
                if t % CH == 0:
                    pe.wait_ge(s_xT[t // CH], 16)
                if t >= 16:
                    pe.wait_ge(s_fcd, t // 2 - 7)
                    pe.wait_ge(s_fca, t // 2 * 2 - 14)
                mmul(ps[t // 2 % 8][:, t % 2 * 256:t % 2 * 256 + 256], xT[:, t * P:(t + 1) * P], vc[:],
                     start=True, stop=True).then_inc(s_ft, 1)
            pe.wait_ge(s_fcd, NT // 2)
            pe.wait_ge(s_fca, NT)
            pe.wait_ge(s_mt, 1)
            pe.transpose(ps[4][0:2, 0:P], mm[:, 0:2], ident[:]).then_inc(s_mb, 1)
            pe.wait_ge(s_md, 1)
            mmul(ps[4][:, 128:130], ones[:], mm[0:2, 4:6], start=True, stop=True).then_inc(s_mb, 1)
            pe.wait_ge(s_flag, 1)
            wide = pe.value_load(flagi[0:1, 0:1], min_val=0, max_val=1)
            with pe.If(wide > 0):
                pe.wait_ge(s_wp, 1)
                for t in range(NT):
                    m = mmul(ps[3][:, 0:G], onesf, h3[:, t, :], start=(t == 0), stop=(t == NT - 1))
                m.then_inc(s_wo, 1)
                with pe.Fori(0, NT) as t:
                    pe.wait_ge(s_wpm, t + 1)
                    pe.transpose(ps[0][:, 0:P], part_max, ident[:]).then_inc(s_wt, 1)
                    pe.wait_ge(s_wd, t + 1)
                    mmul(ps[1][:, 0:P], onesf, diag, start=True, stop=True).then_inc(s_wm, 1)
                    pe.wait_ge(s_wp, t + 2)
                    for j in range(NT):
                        m = mmul(ps[2][:, 0:G], ex_row[:, j * P:(j + 1) * P], h3[:, j, :], start=(j == 0), stop=(j == NT - 1))
                    m.then_inc(s_wo, 1)
            for t in range(NT):
                m = mmul(ps[5][:, 0:1], x[:, t, :], vec[:, 15, t:t + 1], start=(t == 0), stop=(t == NT - 1))
            m.then_inc(s_u, 1)
            pe.wait_ge(s_ub, 1)
            mmul(ps[5][:, 128:256], ty[:, 0, :], vc[:, DC:DC + D], start=True, stop=True).then_inc(s_hp, 1)
            pe.wait_ge(s_ub, 2)

            def attend(b, k, first=False):
                n = GB * b + k
                pe.wait_ge(s_mask, n + 1)
                if not first:
                    pe.wait_ge(s_pf, n - GB + 1)
                for j in range(NT):
                    if first and k == 0 and j % CH == 0:
                        pe.wait_ge(s_gc, PARTS.index((2, j // CH)) + 1)
                    m = mmul(ps[k][:, 0:3 * G], mask[:, k % 2, j * P:(j + 1) * P],
                             g[:, j, :, :].rearrange("p a b -> p (a b)"), start=(j == 0), stop=(j == NT - 1))
                m.then_inc(s_at, 1)

            def turn(b, par):
                pe.wait_ge(s_xl, b + 1)
                for k in range(GB):
                    m = pe.transpose(ps[4][:, k * P:(k + 1) * P], xrow[:, par, k, 0, 0:D], ident[:])
                m.then_inc(s_tt, 1)

            def gate(b):
                pe.wait_ge(s_ttc, b + 1)
                for k in range(GB):
                    m = mmul(ps[5][:, k * E:(k + 1) * E], xlT[:, k * P:(k + 1) * P], gatew[:], start=True, stop=True)
                m.then_inc(s_lg, 1)

            def places(b):
                pe.wait_ge(s_m, b + 1)
                mmul(ps[6][:, 0:GB * E], ltri[:], both[:], start=True, stop=True)
                mmul(ps[6][:, 64:64 + GB * E], onesb[:], both[:], start=True, stop=True).then_inc(s_pr, 1)

            def batch(b, par, first=False, route=True):
                if route:
                    turn(b - 2, par)
                attend(b, 0, first)
                if route:
                    gate(b - 2)
                attend(b, 1, first)
                attend(b, 2, first)
                if route:
                    places(b - 2)
                attend(b, 3, first)

            pe.wait_ge(s_w, 80)
            batch(0, 0, True, False)
            batch(1, 1, False, False)
            with pe.Fori(1, NB // 2) as o:
                for par in range(2):
                    batch(2 * o + par, par)
            for b in (NB - 2, NB - 1):
                turn(b, b % 2)
                gate(b)
                places(b)

            def turn_rows(s, j):
                pe.wait_ge(s_xsw[j], 2 * (s - j) + 16)
                if not (isinstance(s, int) and s < 2):
                    pe.wait_ge(s_Tc, s - 1)
                pe.transpose(ps[(4, 7)[j % 2]][:, 0:P], xs[:, j, 0:D], ident[:]).then_inc(s_T, 1)

            def layer1(s, j):
                e = pe.value_load(tabi[0:1, 1, bass.ds(s, 1)], min_val=0, max_val=E - 1)
                pe.wait_ge(s_Tc, s + 1)
                if not (isinstance(s, int) and s < 2):
                    pe.wait_ge(s_bi, s - 1)
                mmul(ps[j % 2][:], xsT[:, j % 4, :], w1[:, bass.ds(e * H, H)], start=True, stop=True).then_inc(s_L1, 1)

            def turn_hidden(s, j):
                pe.wait_ge(s_ge, s + 1)
                if not (isinstance(s, int) and s < 2):
                    pe.wait_ge(s_hTc, s - 1)
                for k in range(HK):
                    m = pe.transpose(ps[2 + j % 2][:, k * P:(k + 1) * P], hg[:, j % 2, k * P:(k + 1) * P], ident[:])
                m.then_inc(s_hT, 1)

            def layer2(s, j):
                e = pe.value_load(tabi[0:1, 1, bass.ds(s, 1)], min_val=0, max_val=E - 1)
                pe.wait_ge(s_hTc, s + 1)
                if not (isinstance(s, int) and s < 2):
                    pe.wait_ge(s_ya, s - 1)
                for k in range(HK):
                    m = mmul(ps[5 + j % 2][:, 0:D], hT[:, j % 2, k * P:(k + 1) * P],
                             w2[:, bass.ds(e * H + k * P, P)], start=(k == 0), stop=(k == HK - 1))
                m.then_inc(s_L2, 1)

            pe.wait_ge(s_tab, 1)
            for s in range(3):
                turn_rows(s, s)
            layer1(0, 0)
            layer1(1, 1)

            def slot_step(s, j):
                if not isinstance(s, int) or s + 3 < SLOTS:
                    turn_rows(s + 3, (j + 3) % 8)
                turn_hidden(s, j)
                if not isinstance(s, int) or s + 2 < SLOTS:
                    layer1(s + 2, (j + 2) % 8)
                layer2(s, j)

            for s in range(8):
                slot_step(s, s)
            with pe.Fori(1, SLOTS // 8 - 1) as o:
                for j in range(8):
                    slot_step(8 * o + j, j)
            for j in range(8):
                slot_step(SLOTS - 8 + j, j)

        @block.scalar
        def _(act):
            act.preload_act_table_set("natural_log_exp_and_others")
            st = Steps(act, s_as)
            for c in range(4):
                act.wait_ge(s_xc, c + 1)
                act.activation(xc[:, c % 2], xc[:, c % 2], ACT.Square).then_inc(s_sq, 1)
                for t in range(CH * c, CH * c + CH):
                    act.wait_ge(s_fcd, t // 2 + 1)
                    if t >= 4:
                        act.wait_ge(s_fca, t - 3)
                    act.activation(sqj[:, t % 4, 0:DC], ps[t // 2 % 8][:, t % 2 * 256:t % 2 * 256 + DC], ACT.Square,
                                   accum_out=vec[:, 19, t:t + 1]).then_inc(s_fca, 1)

            def root(o, v):
                return ((o, v, ACT.Ln, dict(scale=LN_SCALE)), (o, o, ACT.Exp, dict(scale=0.5, bias=nhalf[:])))

            def functions(st, ready, n, done, *ops):
                act.wait_ge(ready, n)
                for i, (o, a, f, kw) in enumerate(ops):
                    ins = act.activation(o, a, f, **kw)
                    if i < len(ops) - 1:
                        st.step(ins)
                    else:
                        ins.then_inc(done, 1)

            functions(st, s_va, 1, s_av, *root(vec[:, 3:6, :], vec[:, 0:3, :]))
            functions(st, s_va, 2, s_av, *root(vec[:, 7, :], vec[:, 6, :]))
            functions(st, s_va, 3, s_av, (vec[:, 8, :], vec[:, 8, :], ACT.Ln, {}))
            functions(st, s_va, 4, s_av, (vec[:, 20, :], vec[:, 9, :], ACT.Exp, {}))
            functions(st, s_va, 5, s_av, (vec[:, 14, :], vec[:, 14, :], ACT.Ln, {}))
            functions(st, s_va, 6, s_av, (vec[:, 23, :], vec[:, 22, :], ACT.Exp, dict(bias=mm[:, 6:7])))
            act.wait_ge(s_flag, 1)
            wide = act.value_load(flagi[0:1, 0:1], min_val=0, max_val=1)
            with act.If(wide > 0):
                with act.Fori(0, NT) as t:
                    act.wait_ge(s_wx, t + 1)
                    act.activation(ex_row, sc_row, ACT.Exp).then_inc(s_we, 1)
            for n, (p, c) in enumerate(PARTS):
                act.wait_ge(s_gf, n + 1)
                act.activation(g[:, CH * c:CH * c + CH, p, :], h3[:, CH * c:CH * c + CH, :], ACT.Copy).then_inc(s_gc, 1)

            def epilogue(b, par):
                st = Steps(act, s_bas, 3 * b)
                act.wait_ge(s_e1, b + 1)
                act.activation(te[:], ty[:], ACT.Exp).then_inc(s_e2, 1)
                act.wait_ge(s_y1, b + 1)
                for k in range(GB):
                    m = act.activation(sqj[:, k, 0:DC], ty[:, k, 1:D], ACT.Square, accum_out=bv[:, 0, k:k + 1])
                m.then_inc(s_y2, 1)
                functions(st, s_r, 4 * b + 1, s_ra, *root(bv[:, 4:7, :], bv[:, 1:4, :]))
                functions(st, s_r, 4 * b + 2, s_ra, (bv[:, 7, :], bv[:, 7, :], ACT.Ln, {}))
                act.wait_ge(s_al2, b + 1)
                for k in range(GB):
                    m = act.activation(te[:, k, :], ty[:, k, :], ACT.Exp, scale=bv[:, 8, k:k + 1])
                m.then_inc(s_ex, 1)
                act.wait_ge(s_sg, b + 1)
                for k in range(GB):
                    m = act.activation(sqj[:, k, 0:DC], te[:, k, 1:D], ACT.Square, accum_out=bv[:, 9, k:k + 1])
                m.then_inc(s_sg2, 1)
                act.wait_ge(s_r, 4 * b + 3)
                st.step(act.activation(bv[:, 11, :], bv[:, 10, :], ACT.Ln, scale=LN_SCALE))
                act.activation(bv[:, 11, :], bv[:, 11, :], ACT.Exp, scale=0.5, bias=nhalf[:]).then_inc(s_ra, 1)
                functions(st, s_r, 4 * b + 4, s_ra, (bv[:, 12, :], bv[:, 11, :], ACT.Exp, {}))
                act.wait_ge(s_x1, b + 1)
                for k in range(GB):
                    m = act.activation(sqj[:, k, :], ta[:, k, 0:D], ACT.Square, bias=bv[:, 17, k:k + 1],
                                       accum_out=bv[:, 18, k:k + 1])
                m.then_inc(s_x2, 1)
                act.activation(x[:, bass.ds(GB * b, GB), :], ta[:, :, 0:D], ACT.Copy)
                act.wait_ge(s_var, b + 1)
                st.step(act.activation(bv[:, 20, :], bv[:, 19, :], ACT.Ln, scale=LN_SCALE))
                act.activation(bv[:, 20, :], bv[:, 20, :], ACT.Exp, scale=0.5, bias=nhalf[:]).then_inc(s_varr, 1)
                act.wait_ge(s_ns, b + 1)
                for c in range(TOP):
                    for k in range(GB):
                        m = act.activation(xrow[:, par, k, c, 0:D], ta[:, k, 0:D], ACT.Identity,
                                           scale=bv[:, 21, k:k + 1], bias=bv[:, 22, k:k + 1])
                m.then_inc(s_xl, 1)
                assert st.n == 3

            def gate_exp(b):
                act.wait_ge(s_dl, b + 1)
                act.activation(bv[:, 24, :], bv[:, 23, :], ACT.Exp).then_inc(s_de, 1)

            epilogue(0, 0)
            with act.Fori(1, NB // 2) as o:
                for par in range(2):
                    gate_exp(2 * o + par - 2)
                    epilogue(2 * o + par - 1, (par + 1) % 2)
            gate_exp(NB - 2)
            epilogue(NB - 1, 1)
            gate_exp(NB - 1)

            act.preload_act_table(ACT.Gelu)

            def copy_rows(s, j):
                act.wait_ge(s_T, s + 1)
                if not (isinstance(s, int) and s < 4):
                    act.wait_ge(s_L1, s - 3)
                act.activation(xsT[:, j % 4, :], ps[(4, 7)[j % 2]][:, 0:P], ACT.Copy).then_inc(s_Tc, 1)

            def gelu(s, j):
                act.wait_ge(s_bi, s + 1)
                if not (isinstance(s, int) and s < 2):
                    act.wait_ge(s_hT, s - 1)
                act.activation(hg[:, j % 2, :], hs[:, j % 2, :], ACT.Gelu).then_inc(s_ge, 1)

            def weigh(s, j):
                act.wait_ge(s_ya, s + 1)
                if not (isinstance(s, int) and s < 4):
                    act.wait_ge(s_yp, s - 3)
                    act.wait_ge(s_yo[j % 4], 4 * (s - j % 4))
                act.activation(ys[:, j % 4, :], ya[:, j % 2, :], ACT.Copy, scale=xs[:, j, D:D + 1]).then_inc(s_ys, 1)

            for s in range(3):
                copy_rows(s, s)
            gelu(0, 0)
            gelu(1, 1)

            def slot_step(s, j):
                if not isinstance(s, int) or s + 3 < SLOTS:
                    copy_rows(s + 3, (j + 3) % 8)
                if not isinstance(s, int) or s + 2 < SLOTS:
                    gelu(s + 2, (j + 2) % 8)
                weigh(s, j)

            for j in range(8):
                slot_step(j, j)
            with act.Fori(1, SLOTS // 8 - 1) as o:
                for j in range(8):
                    slot_step(8 * o + j, j)
            for j in range(8):
                slot_step(SLOTS - 8 + j, j)

        @block.vector
        def _(v):
            st = Steps(v, s_vs)
            TT, TS, STT = v.tensor_tensor, v.tensor_scalar, v.scalar_tensor_tensor

            def newton(st, u, val, tmp):
                st.step(v.reciprocal(tmp, u))
                st.step(STT(out=tmp, in0=val, scalar=0.5, in1=tmp, op0=ALU.mult, op1=ALU.mult))
                st.step(STT(out=u, in0=u, scalar=0.5, in1=tmp, op0=ALU.mult, op1=ALU.add))

            v.wait_ge(s_const, 1)
            TS(center[:], ident[:], -1.0 / D, None, ALU.add).then_inc(s_cdve, 1)
            v.wait_ge(s_pw, 1)
            v.tensor_copy(waq[0:DC, D:G], ps[0][0:DC, 0:1]).then_inc(s_pwc, 1)
            v.wait_ge(s_pw, 2)
            v.tensor_copy(vraw[:, DC:256], ps[0][:, 0:G]).then_inc(s_pwc, 1)
            v.wait_ge(s_pw, 3)
            v.tensor_copy(vc[:], ps[0][:, 0:256]).then_inc(s_pwc, 1)

            def take_features(i):
                v.wait_ge(s_ft, 2 * i + 2)
                v.tensor_copy(h3[:, 2 * i:2 * i + 2, :],
                              ps[i % 8][:].rearrange("p (a c) -> p a c", a=2)[:, :, DC:256]).then_inc(s_fcd, 1)

            def sum_squares(c):
                cs = slice(CH * c, CH * c + CH)
                v.wait_ge(s_sq, c + 1)
                v.reduce_sum(vec[:, 18, cs], xc[:, c % 2, :, 1:D], AX_X).then_inc(s_sqd, 1)

            for c in range(4):
                cs = slice(CH * c, CH * c + CH)
                v.wait_ge(s_x[c], 16)
                st.step(v.reduce_sum(vec[:, 16, cs], x[:, cs, :], AX_X))
                st.step(TS(vec[:, 16, cs], vec[:, 16, cs], -1.0 / D, None, ALU.mult))
                if c >= 2:
                    sum_squares(c - 2)
                    v.wait_ge(s_sqd, c - 1)
                st.step(TT(xc[:, c % 2], x[:, cs, :], vec[:, 16, cs].unsqueeze(2).to_broadcast([P, CH, D]), ALU.add))
                v.tensor_copy(vec[:, 17, cs], xc[:, c % 2, :, 0]).then_inc(s_xc, 1)
                for i in range(4 * c, 4 * c + 4):
                    take_features(i)
            sum_squares(2)
            sum_squares(3)
            v.wait_ge(s_sqd, 4)
            v.wait_ge(s_fca, NT)
            st.step(TT(vec[:, 20, :], vec[:, 17, :], vec[:, 17, :], ALU.mult))
            st.step(TT(vec[:, 20, :], vec[:, 20, :], vec[:, 18, :], ALU.add))
            st.did(TS(vec[:, 0, :], vec[:, 20, :], 1.0 / D, LN_EPS, ALU.mult, ALU.add))
            st.did(TS(vec[:, 1, :], vec[:, 18, :], NORM2_MIN, None, ALU.max))
            st.settle()
            TS(vec[:, 2, :], vec[:, 19, :], NORM2_MIN, None, ALU.max).then_inc(s_va, 1)
            v.wait_ge(s_va, 1)
            v.wait_ge(s_av, 1)
            newton(st, vec[:, 3:6, :], vec[:, 0:3, :], vt[:])
            st.step(v.reciprocal(vec[:, 26, :], vec[:, 3:5, :][:, 0, :]))
            st.step(TT(vec[:, 24, :], vec[:, 17, :], vec[:, 26, :], ALU.mult))
            st.step(TS(vec[:, 24, :], vec[:, 24, :], THETA_MIN, None, ALU.max))
            st.step(TS(vec[:, 6, :], vec[:, 24, :], 1.0, None, ALU.add))
            STT(out=vec[:, 6, :], in0=vec[:, 24, :], scalar=-1.0, in1=vec[:, 6, :],
                op0=ALU.add, op1=ALU.mult).then_inc(s_va, 1)
            v.wait_ge(s_va, 2)
            v.wait_ge(s_av, 2)
            newton(st, vec[:, 7, :], vec[:, 6, :], vt[:, 0, :])
            TT(vec[:, 8, :], vec[:, 24, :], vec[:, 7, :], ALU.add).then_inc(s_va, 1)
            st.step(v.reciprocal(vec[:, 26, :], vec[:, 4, :]))
            v.wait_ge(s_av, 3)
            st.step(TT(vec[:, 15, :], vec[:, 8, :], vec[:, 26, :], ALU.mult))
            TT(vec[:, 9, :], vec[:, 15, :], vec[:, 5, :], ALU.mult).then_inc(s_va, 1)
            v.wait_ge(s_va, 4)
            v.wait_ge(s_av, 4)
            st.step(v.reciprocal(vec[:, 21, :], vec[:, 20, :]))
            st.did(TT(vec[:, 12, :], vec[:, 20, :], vec[:, 21, :], ALU.subtract))
            st.step(TT(vec[:, 13, :], vec[:, 20, :], vec[:, 21, :], ALU.add))
            st.did(TS(vec[:, 12, :], vec[:, 12, :], 0.5, ROOT_CL, ALU.mult, ALU.max))
            st.step(TS(vec[:, 13, :], vec[:, 13, :], 0.5, THETA_MIN, ALU.mult, ALU.max))
            TT(vec[:, 14, :], vec[:, 12, :], vec[:, 13, :], ALU.add).then_inc(s_va, 1)
            st.step(TS(vec[:, 25, :], vec[:, 9, :], 1e-15, None, ALU.max))
            st.step(v.reciprocal(vec[:, 25, :], vec[:, 25, :]))
            v.wait_ge(s_av, 5)
            st.step(TT(vec[:, 25, :], vec[:, 14, :], vec[:, 25, :], ALU.mult))
            TT(vec[:, 15, :], vec[:, 15, :], vec[:, 25, :], ALU.mult).then_inc(s_al, 1)
            v.wait_ge(s_al, 1)
            st.step(TT(vec[:, 22, :], h3[:, :, D], vec[:, 15, :], ALU.mult))
            st.did(v.reduce_max(mm[:, 0:1], vec[:, 22, :], AX_X))
            st.step(TS(vec[:, 21, :], vec[:, 22, :], -1.0, None, ALU.mult))
            v.reduce_max(mm[:, 1:2], vec[:, 21, :], AX_X).then_inc(s_mt, 1)
            v.wait_ge(s_mb, 1)
            st.step(v.reduce_max(mm[0:2, 2:3], ps[4][0:2, 0:P], AX_X))
            TS(mm[0:2, 4:6], ident[0:2, 0:2], mm[0:2, 2:3], None, ALU.mult).then_inc(s_md, 1)
            v.wait_ge(s_mb, 2)
            TS(mm[:, 6:7], ps[4][:, 128:129], -1.0, None, ALU.mult).then_inc(s_va, 1)
            st.step(v.tensor_copy(mm[:, 7:8], ps[4][:, 129:130]))
            st.step(TT(mm[:, 7:8], mm[:, 7:8], mm[:, 6:7], ALU.subtract))
            TS(flagi[:], mm[:, 7:8], SPREAD_MAX, None, ALU.is_gt).then_inc(s_flag, 1)

            def make_mask(b, k, first=False):
                v.wait_ge(s_adj[k], 16 * b + 16)
                if not (first and k < 2):
                    v.wait_ge(s_at, GB * b + k - 1)
                TS(mask[:, k % 2, :], raw[:, k, :], 0, None, ALU.is_gt).then_inc(s_mask, 1)

            v.wait_ge(s_av, 6)
            st.step(TT(vec[:, 24, :], vec[:, 15, :], vec[:, 23, :], ALU.mult))

            def wide_softmax():
                st = Steps(v, s_wv)
                alpha = vec[:, 15, :].unsqueeze(2).to_broadcast([P, NT, D])
                st.did(TT(h3[:, :, 0:D], h3[:, :, 0:D], alpha, ALU.mult))
                st.step(v.tensor_scalar(vec[:, 22, :], vec[:, 22, :], ps[4][:, 129:130], 1.0, ALU.add, ALU.add))
                st.did(TS(h3[:, :, D], vec[:, 15, :], 0.0, 1.0, ALU.mult, ALU.add))
                for k in range(GB):
                    v.wait_ge(s_adj[k], 16)
                st.step(TS(onesf, ident[:], 0.0, 1.0, ALU.mult, ALU.add))
                v.tensor_copy(mm[:, 7:8], mm[:, 6:7]).then_inc(s_wp, 1)
                v.wait_ge(s_wo, 1)
                st.step(v.tensor_copy(tk[:, 0, :], ps[3][:, 0:G]))
                loop = Steps(v, s_wv, st.n)
                logits = vec[:, 22, :].unsqueeze(2).to_broadcast([P, NT, P])
                scores = sc_row.rearrange("p (j i) -> p j i", i=P)
                with v.Fori(0, NT) as t:
                    loop = Steps(v, s_wv, st.n + WIDE * t)
                    v.wait_ge(s_wa, 16 * t + 16)
                    loop.step(TS(sc_row, raw[:, 0, :], 0, None, ALU.is_gt))
                    loop.step(TT(scores, scores, logits, ALU.mult))
                    v.reduce_max(part_max, sc_row.rearrange("p (j i) -> p i j", i=P), AX_X).then_inc(s_wpm, 1)
                    v.wait_ge(s_wt, t + 1)
                    loop.step(v.reduce_max(ta[:, 0, 0:1], ps[0][:, 0:P], AX_X))
                    TS(diag, ident[:], ta[:, 0, 0:1], None, ALU.mult).then_inc(s_wd, 1)
                    v.wait_ge(s_wm, t + 1)
                    loop.step(v.tensor_copy(row_max, ps[1][:, 0:P]))
                    loop.step(TT(scores, scores, row_max.unsqueeze(1).to_broadcast([P, NT, P]), ALU.subtract))
                    TS(sc_row, sc_row, 0.0, None, ALU.min).then_inc(s_wx, 1)
                    v.wait_ge(s_we, t + 1)
                    loop.step(TS(sc_row, raw[:, 0, :], 0, None, ALU.is_gt))
                    TT(ex_row, ex_row, sc_row, ALU.mult).then_inc(s_wp, 1)
                    v.wait_ge(s_wo, t + 2)
                    loop.step(v.tensor_copy(ta[:, 1, :], ps[2][:, 0:G]))
                    loop.step(TS(ta[:, 0, 1:2], ta[:, 1, D:G], 0.0, None, ALU.is_equal))
                    loop.step(STT(out=ta[:, 1, :], in0=tk[:, 0, :], scalar=ta[:, 0, 1:2], in1=ta[:, 1, :],
                                  op0=ALU.mult, op1=ALU.add))
                    loop.step(v.reciprocal(ta[:, 0, 2:3], ta[:, 1, D:G]))
                    TS(gres[:, bass.ds(t, 1), :], ta[:, 1:2, 0:D], ta[:, 0, 2:3], None, ALU.mult).then_inc(s_wr, 1)
                    assert loop.n <= WIDE
                v.wait_ge(s_wr, NT)
                end = Steps(v, s_wv, st.n + WIDE * NT)
                with v.Fori(0, NT) as t:
                    TS(h3[:, bass.ds(NT - 1 - t, 1), 0:D], gres[:, bass.ds(t, 1), :], 1.0, None, ALU.mult).then_inc(s_wv, 1)
                end.n += NT
                for i in (23, 24):
                    end.did(TS(vec[:, i, :], vec[:, i, :], 0.0, 1.0, ALU.mult, ALU.add))
                end.did(TS(raw[:, 1, :], raw[:, 0, :], 0, None, ALU.mult))
                v.tensor_copy(raw[:, 2, 0:P], ident[:]).then_inc(s_wu, 1)
                end.settle()
                for k in range(GB):
                    v.wait_ge(s_ww[k], 16)

            WIDE = 10
            wide = v.value_load(flagi[0:1, 0:1], min_val=0, max_val=1)
            with v.If(wide > 0):
                wide_softmax()
            make_mask(0, 0, True)
            for n, (p, c) in enumerate(PARTS):
                cs = slice(CH * c, CH * c + CH)
                if p == 0:
                    st.step(TT(h3[:, cs, 0:D], h3[:, cs, 0:D], vec[:, 24, cs].unsqueeze(2).to_broadcast([P, CH, D]), ALU.mult))
                    v.tensor_copy(h3[:, cs, D], vec[:, 23, cs]).then_inc(s_gf, 1)
                else:
                    v.wait_ge(s_gc, PARTS.index((p - 1, c)) + 1)
                    TT(h3[:, cs, :], h3[:, cs, :], g[:, cs, p - 1, :], ALU.subtract).then_inc(s_gf, 1)
            v.wait_ge(s_u, 1)
            v.tensor_copy(ty[:, 0, :], ps[5][:, 0:1].to_broadcast([P, P])).then_inc(s_ub, 1)
            v.wait_ge(s_hp, 1)
            v.tensor_copy(hsum[:, 0:D], ps[5][:, 128:256]).then_inc(s_ub, 1)

            def take(b, k):
                st = Steps(v, s_tk, 2 * (GB * b + k))
                v.wait_ge(s_at, GB * b + k + 1)
                st.step(v.tensor_copy(tk[:, k, :], ps[k][:, 2 * G:3 * G]))
                st.step(TT(tk[:, k, :], tk[:, k, :], ps[k][:, G:2 * G], ALU.add))
                TT(tk[:, k, :], tk[:, k, :], ps[k][:, 0:G], ALU.add).then_inc(s_pf, 1)

            def epilogue_a(b, st):
                v.wait_ge(s_pf, GB * b + GB)
                if not (isinstance(b, int) and b == 0):
                    v.wait_ge(s_xl, b)
                st.step(TS(bv[:, 27, :], tk[:, :, D], 0.0, None, ALU.is_equal))
                for k in range(GB):
                    st.did(STT(out=ta[:, k, :], in0=hsum[:], scalar=bv[:, 27, k:k + 1], in1=tk[:, k, :],
                               op0=ALU.mult, op1=ALU.add))
                st.settle()
                st.step(v.reciprocal(bv[:, 28, :], ta[:, :, D]))
                st.step(TT(ta[:, :, 0:D], ta[:, :, 0:D], bv[:, 28, :].unsqueeze(2).to_broadcast([P, GB, D]), ALU.mult))
                TS(ty[:], ta[:, :, 0:D], 0.0, None, ALU.min).then_inc(s_e1, 1)
                st.step(TS(ta[:, :, 0:D], ta[:, :, 0:D], 0.0, -1.0, ALU.max, ALU.add))

            def epilogue_b(b, st):
                v.wait_ge(s_e2, b + 1)
                TT(ty[:], ta[:, :, 0:D], te[:], ALU.add).then_inc(s_y1, 1)
                v.wait_ge(s_y2, b + 1)
                st.did(TS(bv[:, 1, :], bv[:, 0, :], NORM2_MIN, None, ALU.max))
                st.step(TS(bv[:, 2, :], bv[:, 0, :], CL, None, ALU.max))
                TS(bv[:, 3, :], bv[:, 2, :], 1.0, None, ALU.add).then_inc(s_r, 1)
                v.wait_ge(s_r, 4 * b + 1)
                v.wait_ge(s_ra, 4 * b + 1)
                newton(st, bv[:, 4:7, :], bv[:, 1:4, :], bt[:])
                TT(bv[:, 7, :], bv[:, 5, :], bv[:, 6, :], ALU.add).then_inc(s_r, 1)
                st.step(v.reciprocal(bv[:, 26, :], bv[:, 4, :]))
                v.wait_ge(s_ra, 4 * b + 2)
                STT(out=bv[:, 8, :], in0=bv[:, 7, :], scalar=-1.0, in1=bv[:, 26, :],
                    op0=ALU.mult, op1=ALU.mult).then_inc(s_al2, 1)
                v.wait_ge(s_ex, b + 1)
                st.step(TS(te[:], te[:], 1.0, None, ALU.add))
                v.reciprocal(te[:], te[:]).then_inc(s_sg, 1)

            def epilogue_c(b, par, st):
                v.wait_ge(s_sg2, b + 1)
                TS(bv[:, 10, :], bv[:, 9, :], NORM2_MIN, None, ALU.max).then_inc(s_r, 1)
                v.wait_ge(s_r, 4 * b + 3)
                v.wait_ge(s_ra, 4 * b + 3)
                st.step(v.reciprocal(bt[:, 0, :], bv[:, 11, :]))
                st.step(STT(out=bt[:, 0, :], in0=bv[:, 10, :], scalar=0.5, in1=bt[:, 0, :], op0=ALU.mult, op1=ALU.mult))
                STT(out=bv[:, 11, :], in0=bv[:, 11, :], scalar=0.5, in1=bt[:, 0, :], op0=ALU.mult, op1=ALU.add).then_inc(s_r, 1)
                v.wait_ge(s_r, 4 * b + 4)
                st.step(v.reciprocal(bv[:, 26, :], bv[:, 11, :]))
                v.wait_ge(s_ra, 4 * b + 4)
                st.step(v.reciprocal(bv[:, 13, :], bv[:, 12, :]))
                st.step(TT(bv[:, 16, :], bv[:, 12, :], bv[:, 13, :], ALU.subtract))
                st.did(TT(bv[:, 14, :], bv[:, 12, :], bv[:, 13, :], ALU.add))
                st.step(STT(out=bv[:, 26, :], in0=bv[:, 16, :], scalar=0.5, in1=bv[:, 26, :], op0=ALU.mult, op1=ALU.mult))
                for k in range(GB):
                    st.did(STT(out=ta[:, k:k + 1, 1:D], in0=te[:, k:k + 1, 1:D], scalar=bv[:, 26, k:k + 1],
                               in1=x[:, bass.ds(GB * b + k, 1), 1:D], op0=ALU.mult, op1=ALU.add))
                first = x[:, bass.ds(GB * b, GB), 0:1].rearrange("p t a -> p (t a)")
                st.step(STT(out=ta[:, :, 0], in0=bv[:, 14, :], scalar=0.5, in1=first, op0=ALU.mult, op1=ALU.add))
                st.step(v.reduce_sum(bv[:, 16, :], ta[:, :, 0:D], AX_X))
                TS(bv[:, 17, :], bv[:, 16, :], -1.0 / D, None, ALU.mult).then_inc(s_x1, 1)
                v.wait_ge(s_x2, b + 1)
                TS(bv[:, 19, :], bv[:, 18, :], 1.0 / D, LN_EPS, ALU.mult, ALU.add).then_inc(s_var, 1)
                v.wait_ge(s_var, b + 1)
                v.wait_ge(s_varr, b + 1)
                newton(st, bv[:, 20, :], bv[:, 19, :], bt[:, 0, :])
                st.step(v.reciprocal(bv[:, 21, :], bv[:, 20, :]))
                if not (isinstance(b, int) and b < 2):
                    v.wait_ge(s_sc[par], 8 * TOP * GB * (b - par))
                TT(bv[:, 22, :], bv[:, 17, :], bv[:, 21, :], ALU.mult).then_inc(s_ns, 1)

            EP = 32

            def copy_turned(b):
                v.wait_ge(s_tt, b + 1)
                v.tensor_copy(xlT[:], ps[4][:]).then_inc(s_ttc, 1)

            CHO = 18

            def choice(b, par):
                st = Steps(v, s_ch, CHO * b)
                v.wait_ge(s_lg, b + 1)
                st.did(TT(lg[:], ps[5][:, 0:GB * E].rearrange("p (k e) -> p k e", e=E),
                           bgb[:].unsqueeze(1).to_broadcast([P, GB, E]), ALU.add))
                st.settle()
                st.did(TS(xrow[:, par, :, 0, D + 1], tokid[:, bass.ds(GB * b, GB)], 0.0, None, ALU.add))
                for k in range(GB):
                    st.did(v.max(top[:, k, :], lg[:, k, :]))
                st.settle()
                st.did(TS(xrow[:, par, :, 1, D + 1], tokid[:, bass.ds(GB * b, GB)], float(N), None, ALU.add))
                for k in range(GB):
                    st.did(v.max_index(idx[:, k, :], top[:, k, :], lg[:, k, :]))
                TT(bv[:, 23, :], top[:, :, 1], top[:, :, 0], ALU.subtract).then_inc(s_dl, 1)
                st.settle()
                st.step(v.tensor_copy(idxf[:], idx[:, :, 0:TOP].rearrange("p k c -> p c k")))
                for c in range(TOP):
                    st.did(TT(onehot[:, c], iota8[:].unsqueeze(1).to_broadcast([P, GB, E]),
                              idxf[:, c].unsqueeze(2).to_broadcast([P, GB, E]), ALU.is_equal))
                st.settle()
                TT(both[:].rearrange("p (k e) -> p k e", e=E), onehot[:, 0], onehot[:, 1], ALU.add).then_inc(s_m, 1)
                v.wait_ge(s_de, b + 1)
                st.step(TS(bv[:, 23, :], bv[:, 24, :], 1.0, None, ALU.add))
                st.step(v.reciprocal(bv[:, 25, :], bv[:, 23, :]))
                st.did(v.tensor_copy(xrow[:, par, :, 0, D], bv[:, 25, :]))
                st.did(TT(xrow[:, par, :, 1, D], bv[:, 24, :], bv[:, 25, :], ALU.mult))
                st.settle()
                return st.n

            PL = GB + 5

            def place(b, par):
                st = Steps(v, s_plc, PL * b)
                v.wait_ge(s_pr, b + 1)
                st.step(v.tensor_copy(run[:, 0, :], run[:, GB, :]))
                for k in range(GB):
                    st.step(TT(run[:, k + 1, :], run[:, k, :], ps[6][:, 64 + k * E:64 + (k + 1) * E], ALU.add))
                st.step(TT(rowid[:], ps[6][:, 0:GB * E].rearrange("p (k e) -> p k e", e=E), run[:, 0:GB, :], ALU.add))
                for c in range(TOP):
                    m = TT(pick[:, c * GB:(c + 1) * GB, :], onehot[:, c], rowid[:], ALU.mult)
                    if c == 0:
                        st.did(m)
                    else:
                        st.step(m)
                st.step(v.reduce_sum(slotf[:], pick[:], AX_X))
                if not (isinstance(b, int) and b == 0):
                    v.wait_ge(s_sp, b)
                    v.wait_ge(s_sc[1 - par], 8 * TOP * GB * (b - par) + (16 * TOP * GB if par else 0))
                v.tensor_copy(slot[:], slotf[:]).then_inc(s_sl, 1)
                return st.n

            counts = {}

            def batch(b, par, masks=True, first=False, ep=True, route=True):
                st = Steps(v, s_ep, EP * (b - 1))
                if masks and not first:
                    make_mask(b, 0)
                if ep:
                    take(b - 1, 2)
                if route:
                    copy_turned(b - 2)
                if masks:
                    make_mask(b, 1, first)
                if ep:
                    take(b - 1, 3)
                    epilogue_a(b - 1, st)
                if route:
                    counts['ch'] = choice(b - 2, par)
                if masks:
                    make_mask(b, 2)
                    take(b, 0)
                if ep:
                    epilogue_b(b - 1, st)
                if masks:
                    make_mask(b, 3)
                    take(b, 1)
                if route:
                    counts['pl'] = place(b - 2, par)
                if ep:
                    epilogue_c(b - 1, 1 - par, st)
                    counts['ep'] = st.n

            batch(0, 0, first=True, ep=False, route=False)
            batch(1, 1, route=False)
            with v.Fori(1, NB // 2) as o:
                for par in range(2):
                    batch(2 * o + par, par)
            batch(NB, 0, masks=False)
            copy_turned(NB - 1)
            choice(NB - 1, 1)
            place(NB - 1, 1)
            assert counts == dict(ch=CHO, pl=PL, ep=EP), counts

            v.wait_ge(s_sl, NB)
            TS(padid[:], run[:, GB, :], tokid[:, 0:1], None, ALU.add).then_inc(s_pad, 1)
            st.step(TT(cnt[:, 0, :], run[:, GB, :], region0[:], ALU.subtract))
            st.step(TS(cnt[:, 0, :], cnt[:, 0, :], float(P - 1), None, ALU.add))
            st.step(v.tensor_copy(cnti[:, 0, :], cnt[:, 0, :]))
            st.step(TS(cnti[:, 1, :], cnti[:, 0, :], 7, None, ALU.arith_shift_right))
            st.step(v.tensor_copy(cnt[:, 1, :], cnti[:, 1, :]))
            st.step(v.tensor_copy(cnt[:, 2, :], cnt[:, 1, :]))
            for sh in (1, 2, 4):
                a, z = (2, 3) if sh != 2 else (3, 2)
                st.did(v.tensor_copy(cnt[:, z, 0:sh], cnt[:, a, 0:sh]))
                st.step(TT(cnt[:, z, sh:E], cnt[:, a, sh:E], cnt[:, a, 0:E - sh], ALU.add))
            slots = slotno[:].unsqueeze(2).to_broadcast([P, SLOTS, E])
            st.step(TT(cmpb, cnt[:, 3, :].unsqueeze(1).to_broadcast([P, SLOTS, E]), slots, ALU.is_le))
            st.step(v.reduce_sum(tabs[:, 0, :], cmpb, AX_X))
            st.step(TT(cmpb, cmpb, cnt[:, 1, :].unsqueeze(1).to_broadcast([P, SLOTS, E]), ALU.mult))
            st.step(v.reduce_sum(tabs[:, 1, :], cmpb, AX_X))
            st.step(TT(tabs[:, 1, :], slotno[:], tabs[:, 1, :], ALU.subtract))
            st.step(TS(tabs[:, 1, :], tabs[:, 1, :], float(P), None, ALU.mult))
            st.step(STT(out=tabs[:, 1, :], in0=tabs[:, 0, :], scalar=float(REGION), in1=tabs[:, 1, :],
                        op0=ALU.mult, op1=ALU.add))
            st.step(TS(tabs[:, 0, :], tabs[:, 0, :], float(E - 1), None, ALU.min))
            st.step(v.tensor_copy(tabi[:, 0, :], tabs[:, 1, :]))
            v.tensor_copy(tabi[:, 1, :], tabs[:, 0, :]).then_inc(s_tab, 1)
            v.wait_ge(s_tab, 1)

            def bias(s, j):
                e = v.value_load(tabi[0:1, 1, bass.ds(s, 1)], min_val=0, max_val=E - 1)
                v.wait_ge(s_L1, s + 1)
                if not (isinstance(s, int) and s < 2):
                    v.wait_ge(s_ge, s - 1)
                TT(hs[:, j % 2, :], ps[j % 2][:], b1b[:, bass.ds(e * H, H)], ALU.add).then_inc(s_bi, 1)

            def copy_hidden(s, j):
                v.wait_ge(s_hT, s + 1)
                if not (isinstance(s, int) and s < 2):
                    v.wait_ge(s_L2, s - 1)
                v.tensor_copy(hT[:, j % 2, :], ps[2 + j % 2][:]).then_inc(s_hTc, 1)

            def result(s, j):
                e = v.value_load(tabi[0:1, 1, bass.ds(s, 1)], min_val=0, max_val=E - 1)
                v.wait_ge(s_L2, s + 1)
                if not (isinstance(s, int) and s < 2):
                    v.wait_ge(s_ys, s - 1)
                TT(ya[:, j % 2, :], ps[5 + j % 2][:, 0:D], b2b[:, bass.ds(e * D, D)], ALU.add).then_inc(s_ya, 1)
                if not (isinstance(s, int) and s < 4):
                    v.wait_ge(s_yo[j % 4], 4 * (s - j % 4))
                v.tensor_copy(yid[:, j % 4:j % 4 + 1], xs[:, j, D + 1:D + 2]).then_inc(s_yi, 1)

            v.wait_ge(s_b1, 16)
            bias(0, 0)
            bias(1, 1)

            def slot_step(s, j):
                copy_hidden(s, j)
                if not isinstance(s, int) or s + 2 < SLOTS:
                    bias(s + 2, (j + 2) % 8)
                result(s, j)

            for j in range(8):
                slot_step(j, j)
            with v.Fori(1, SLOTS // 8 - 1) as o:
                for j in range(8):
                    slot_step(8 * o + j, j)
            for j in range(8):
                slot_step(SLOTS - 8 + j, j)

            for c in range(4):
                cs = slice(CH * c, CH * c + CH)
                v.wait_ge(s_pl[c], 32)
                TT(x[:, cs, :], x[:, cs, :], yplane[0][:, cs, :], ALU.add).then_inc(s_fs, 1)
                v.wait_ge(s_fs, c + 1)
                TT(x[:, cs, :], x[:, cs, :], yplane[1][:, cs, :], ALU.add).then_inc(s_fin, 1)


def kernel(**inputs):
    import concourse.bacc as bacc
    from concourse.bass_utils import run_bass_kernel_spmd

    a = {k: np.asarray(v) for k, v in inputs.items()}
    x = a["x"]
    wg = np.zeros((D, DC), x.dtype)
    wg[1:, :] = a["L0_gnn_W_gcn"]
    wa = a["L0_gnn_W_att"][1:, :]
    arrays = {
        "x_rows": x.reshape(NT, P, D).transpose(1, 0, 2),
        "xT": x.T,
        "adjT": a["adj"].reshape(NT, P, NT, P).transpose(0, 3, 2, 1).reshape(NT, P, N),
        "w_gcn": wg,
        "w_gcnT": wg.T,
        "w_att": wa,
        "w_attT": wa.T,
        "a2": a["L0_gnn_a_att"][D:, :],
        "gate_w": a["L0_ffn_Wg"],
        "gate_b": a["L0_ffn_bg"],
        "w1": a["L0_ffn_W1"].transpose(1, 0, 2).reshape(D, E * H),
        "b1": a["L0_ffn_b1"].reshape(E * H),
        "w2": a["L0_ffn_W2"].reshape(E, HK, P, D).transpose(2, 0, 1, 3).reshape(P, E * HK * D),
        "b2": a["L0_ffn_b2"].reshape(E * D),
    }
    arrays = {k: np.ascontiguousarray(v) for k, v in arrays.items()}
    nc = bacc.Bacc("TRN2", target_bir_lowering=False, num_devices=1)
    args = [nc.dram_tensor(f"in_{k}", v.shape, mybir.dt.from_np(v.dtype), kind="ExternalInput").ap() for k, v in arrays.items()]
    out = nc.dram_tensor("out", (N, D), F32, kind="ExternalOutput").ap()
    gnn_moe_kernel(nc, *args, out)
    result = run_bass_kernel_spmd(nc, [{f"in_{k}": v for k, v in arrays.items()}], core_ids=[0])
    return result.results[0]["out"]
```

```python
from contextlib import ExitStack

import numpy as np

import concourse.bass as bass
from concourse import mybir

F32 = mybir.dt.float32
BF16 = mybir.dt.bfloat16
I32 = mybir.dt.int32
U32 = mybir.dt.uint32
ALU = mybir.AluOpType
ACT = mybir.ActivationFunctionType
AX_X = mybir.AxisListType.X

P = 128
N = 4096
D = 128
NT = N // P
GB = 4
NB = NT // GB
DC = D - 1
G = D + 1
E = 8
H = 512
HK = H // P
TOP = 2
REGION = N + P
SLOTS = 72
SPARE = SLOTS - TOP * N // P
ROW = D + 2
LN_EPS = 1e-5
THETA_MIN = float(np.float32(1.0 + 1e-7))
CL = THETA_MIN ** 2 - 1.0
ROOT_CL = CL ** 0.5
NORM2_MIN = 1e-30
SPREAD_MAX = 50.0
LN_SCALE = 2.0 ** 36
HALF_LN_SCALE = 18.0 * float(np.log(2.0))
CH = NT // 4
PARTS = sorted(((p, c) for p in range(3) for c in range(4)), key=lambda pc: (pc[0] + pc[1], pc[0]))


class Steps:

    def __init__(self, eng, sem, start=0):
        self.eng, self.sem, self.base, self.n = eng, sem, start, 0

    def value(self):
        return self.base + self.n

    def did(self, ins):
        ins.then_inc(self.sem, 1)
        self.n += 1

    def settle(self):
        self.eng.wait_ge(self.sem, self.base + self.n)

    def step(self, ins):
        self.did(ins)
        self.settle()



def gnn_moe_kernel(nc, x_rows, xT_in, adjT, wg_in, wgT_in, wa_in, waT_in, a2_in,
                   gate_in, bg_in, w1_in, b1_in, w2_in, b2_in, out):
    disp = nc.dram_tensor("disp", [E * REGION + SPARE * P, ROW], F32).ap()
    unit = nc.dram_tensor("unit", [P, (2 * NT - 1) * P], I32).ap()
    planes = nc.dram_tensor("planes", [TOP * N + (E + SPARE) * P, D], F32).ap()
    with ExitStack() as ctx:
        def sb(name, shape, dt=F32):
            return ctx.enter_context(nc.sbuf_tensor(name, shape, dt))

        def sem(name):
            return ctx.enter_context(nc.semaphore(name))

        x = sb("x", [P, NT, D])
        hb = sb("hb", [P, NT * G])
        h3 = hb[:].rearrange("p (t g) -> p t g", g=G)
        w2c = hb[:, 0:4 * H].rearrange("p (s r) -> p s r", r=H)
        b2c = hb[:, 4 * H:4 * H + 8 * D].rearrange("p (s r) -> p s r", r=D)
        gb = sb("gb", [P, NT * 3 * G], BF16)
        g = gb[:].rearrange("p (t a b) -> p t a b", a=3, b=G)
        b1t = sb("b1t", [P, E * HK])
        b2b = sb("b2b", [P, E * D])
        raw = sb("raw", [P, 4, N], I32)
        mask = sb("mask", [P, GB, N], BF16)
        maskf = mask[:].rearrange("p a n -> p (a n)").bitcast(F32)
        xT = maskf[:, 0:N]
        rawf = raw[:].bitcast(F32).rearrange("p a n -> p (a n)")
        ident = sb("ident", [P, P])
        ones = sb("ones", [2, P])
        center = sb("center", [P, P])
        ltri = sb("ltri", [P, P], BF16)
        onesb = sb("onesb", [P, P], BF16)
        gatew = sb("gatew", [P, E])
        bgb = sb("bgb", [P, E])
        iota8 = sb("iota8", [P, E])
        region0 = sb("region0", [P, E])
        tokid = sb("tokid", [P, NT])
        ia = sb("ia", [P, SLOTS], I32)
        slotno = sb("slotno", [P, SLOTS])
        nhalf = sb("nhalf", [P, 1])
        sqj = sb("sqj", [P, 4, D], BF16)
        tk = sb("tk", [P, GB, G])
        alone = sb("alone", [P, GB, 1], U32)
        ta = sb("ta", [P, GB, D])
        ty = sb("ty", [P, GB, D])
        te = sb("te", [P, 2, GB, D])
        x1 = sb("x1", [P, GB, D])
        xlT = sb("xlT", [P, GB * P])
        xrow = sb("xrow", [P, 2, GB, TOP, ROW])
        hsum = sb("hsum", [P, G])
        vc = sb("vc", [P, 256])
        vec = sb("vec", [P, 28, NT])
        junk = vec[:].rearrange("p a t -> p (a t)").bitcast(BF16)[:, 0:2 * GB * D].rearrange("p (a k d) -> p a k d", a=2, d=D)
        bn = sb("bn", [P, NT, 6])
        vt = sb("vt", [P, 3, NT])
        bv = sb("bv", [P, 29, GB])
        bt = sb("bt", [P, 4, GB])
        lg = sb("lg", [P, GB, E])
        top = sb("top", [P, GB, 8])
        idx = sb("idx", [P, GB, 8], U32)
        idxf = sb("idxf", [P, TOP, GB])
        onehot = sb("onehot", [P, TOP, GB, E])
        both = sb("both", [P, GB * E], BF16)
        run = sb("run", [P, E])
        rowid = sb("rowid", [P, GB, E])
        pick = sb("pick", [P, TOP * GB, E])
        slotf = sb("slotf", [P, TOP * GB])
        slot = sb("slot", [P, TOP * GB], U32)
        mm = sb("mm", [P, 8])
        flagi = sb("flagi", [P, 1], I32)
        padrow = sb("padrow", [P, E], I32)
        tabs = sb("tabs", [P, 3, SLOTS])
        tabi = sb("tabi", [P, 2, SLOTS], I32)
        cnt = sb("cnt", [P, 5, E])
        cnti = sb("cnti", [P, 2, E], I32)
        yid = sb("yid", [P, 4], U32)
        carry = sb("carry", [P, 1])
        still = sb("still", [P, 6])
        pre = rawf[:, 3 * N:4 * N]
        wgT, waq, waT, a2, vraw = pre[:, 0:128], pre[:, 128:257], pre[:, 257:384], pre[:, 384:385], pre[:, 385:641]
        cmpb = sb("cmpb", [P, SLOTS, E])[:]
        pad = sb("pad", [P, E, ROW])[:]
        w1, w2 = rawf[:, 2 * N:3 * N], rawf[:, 3 * N:4 * N]
        sc_row, ex_row = (rawf[:, k * N:(k + 1) * N] for k in (1, 2))
        grp = rawf[:, 3 * N:3 * N + 5 * P].rearrange("p (a i) -> p a i", i=P)
        onesf, part_max, diag, row_max, h_sum = (grp[:, i, :] for i in range(5))
        gres = gb[:].bitcast(F32)[:, 0:N].rearrange("p (t d) -> p t d", d=D)
        xs = rawf[:, 0:8 * ROW].rearrange("p (s r) -> p s r", r=ROW)
        xsT = rawf[:, 2048:2048 + 4 * P].rearrange("p (s r) -> p s r", r=P)
        w1c = rawf[:, 2560:2560 + 4 * H].rearrange("p (s r) -> p s r", r=H)
        hT = rawf[:, 4608:4608 + 4 * H].rearrange("p (s r) -> p s r", r=H)
        b1c = rawf[:, 6656:6656 + 4 * HK].rearrange("p (s r) -> p s r", r=HK)
        ya = rawf[:, 7168:7168 + 2 * D].rearrange("p (s r) -> p s r", r=D)
        ys = rawf[:, 7424:7424 + 4 * D].rearrange("p (s r) -> p s r", r=D)
        yplane = [rawf[:, k * N:(k + 1) * N].rearrange("p (t d) -> p t d", d=D) for k in range(TOP)]
        spare = maskf[:, N:N + SPARE * ROW].rearrange("p (e r) -> p e r", r=ROW)

        ps = [ctx.enter_context(nc.psum_tensor(f"ps{i}", [P, 512], F32)) for i in range(8)]

        s_small = sem("small_weights_in")
        s_x = [sem(f"x_in{c}") for c in range(4)]
        s_xT = [sem(f"xT_in{c}") for c in range(4)]
        s_adj = [sem(f"adj_in{i}") for i in range(4)]
        s_gw = sem("gate_weights_in")
        s_w = sem("expert_weights_in")
        s_const = sem("constants")
        s_cdve = sem("centre_matrix")
        s_pc = sem("pool_steps")
        s_vs = sem("dve_steps")
        s_as = sem("act_steps")
        s_pw = sem("weight_products")
        s_pwc = sem("weight_products_copied")
        s_ft = sem("feature_products")
        s_fcd = sem("feature_rows_copied")
        s_fca = sem("feature_squares")
        s_va = sem("vectors_for_act")
        s_av = sem("vectors_from_act")
        s_al = sem("alpha_ready")
        s_u = sem("u_product")
        s_ub = sem("u_copied")
        s_hp = sem("hsum_product")
        s_mt = sem("extremes_ready")
        s_mb = sem("extremes_products")
        s_md = sem("extremes_taken")
        s_flag = sem("spread_known")
        s_wa = sem("wide_adj_in")
        s_wpm = sem("wide_partition_max")
        s_wt = sem("wide_max_turned")
        s_wd = sem("wide_max_diagonal")
        s_wm = sem("wide_max_spread")
        s_wx = sem("wide_exponents")
        s_we = sem("wide_exp_done")
        s_wp = sem("wide_weights")
        s_wo = sem("wide_sums")
        s_wr = sem("wide_rows_taken")
        s_wv = sem("wide_dve_steps")
        s_wu = sem("wide_identity")
        s_wuo = sem("wide_identity_out")
        s_ww = [sem(f"wide_window_in{k}") for k in range(GB)]
        s_gf = sem("g_rest")
        s_gc = sem("g_cast")
        s_mask = sem("mask_ready")
        s_at = sem("attention_done")
        s_pf = sem("attention_taken")
        s_tk = sem("take_dve_steps")
        s_e1 = sem("elu_operand")
        s_e2 = sem("elu_exp")
        s_y1 = sem("emb_ready")
        s_y2 = sem("emb_squared")
        s_al2 = sem("log_scale_ready")
        s_sg2 = sem("sigmoid_squared")
        s_r = sem("log_vectors_for_act")
        s_ra = sem("log_vectors_from_act")
        s_rc = sem("exp_vectors_for_act")
        s_rca = sem("exp_vectors_from_act")
        s_var = sem("variance")
        s_varr = sem("deviation")
        s_x1 = sem("x1_ready")
        s_x2 = sem("x1_squared")
        s_ns = sem("norm_scale_ready")
        s_xl = sem("xl_ready")
        s_bas = sem("log_act_steps")
        s_bcs = sem("exp_act_steps")
        s_tt = sem("xl_turned")
        s_ttc = sem("xl_turned_copied")
        s_lg = sem("logits")
        s_dl = sem("gate_difference")
        s_de = sem("gate_exp")
        s_m = sem("choice_ready")
        s_pr = sem("prefix_ready")
        s_sl = sem("rows_addressed")
        s_sp = sem("dispatch_begun")
        s_yp = sem("return_begun")
        s_spare = sem("spare_rows_out")
        s_sc = [sem(f"rows_dispatched{i}") for i in range(2)]
        s_pd = sem("padding_rows_out")
        s_ea = sem("elu_dve_steps")
        s_eb = sem("log_dve_steps")
        s_ec = sem("exp_dve_steps")
        s_ch = sem("choice_dve_steps")
        s_plc = sem("place_dve_steps")
        s_tab = sem("tables_ready")
        s_pad = sem("padding_addressed")
        s_xsw = [sem(f"slot_rows_in{i}") for i in range(8)]
        s_T = sem("slot_turned")
        s_Tc = sem("slot_turned_copied")
        s_L1 = sem("layer1")
        s_wc = sem("tile_weights_fetched")
        s_ge = sem("gelu_done")
        s_L2 = sem("layer2")
        s_ya = sem("layer2_biased")
        s_ys = sem("result_weighted")
        s_yi = sem("result_place")
        s_yo = [sem(f"result_out{i}") for i in range(4)]
        s_pl = [sem(f"planes_in{c}") for c in range(4)]
        s_fs = sem("final_steps")
        s_fin = sem("final_sum")
        s_out = sem("out_stored")

        block = ctx.enter_context(nc.Block())

        @block.sync
        def _(sp):
            sp.dma_start(wgT[0:DC, :], wgT_in).then_inc(s_small, 16)
            sp.dma_start(waq[0:DC, 0:D], wa_in).then_inc(s_small, 16)
            sp.dma_start(waT[:, 0:DC], waT_in).then_inc(s_small, 16)
            sp.dma_start(a2, a2_in).then_inc(s_small, 16)
            sp.dma_start(vraw[:, 0:DC], wg_in).then_inc(s_small, 16)
            for c in range(4):
                sp.dma_start(x[:, CH * c:CH * c + CH, :], x_rows[:, CH * c:CH * c + CH, :]).then_inc(s_x[c], 16)
                sp.dma_start(xT[:, 1024 * c:1024 * (c + 1)], xT_in[:, 1024 * c:1024 * (c + 1)]).then_inc(s_xT[c], 16)
            for t in range(3):
                sp.dma_start(raw[:, t, :], adjT[t]).then_inc(s_adj[t], 16)
            sp.dma_start(gatew[:], gate_in).then_inc(s_gw, 16)
            sp.dma_start(bgb[:], bg_in.partition_broadcast(P)).then_inc(s_gw, 16)
            sp.dma_start(b1t[:], b1_in).then_inc(s_w, 16)
            sp.dma_start(b2b[:], b2_in.partition_broadcast(P)).then_inc(s_w, 16)
            sp.wait_ge(s_pwc, 3)
            sp.dma_start(raw[:, 3, :], adjT[3]).then_inc(s_adj[3], 16)
            def stream(tile):
                with sp.Fori(1, NB) as q:
                    for k in range(GB):
                        src = tile(GB * q + k)
                        sp.wait_ge(s_mask, GB * q - GB + k + 1)
                        sp.dma_start(raw[:, k, :], src).then_inc(s_adj[k], 16)

            def window(t):
                return unit[:, bass.ds(t * P, N)]

            sp.wait_ge(s_flag, 1)
            wide = sp.value_load(flagi[0:1, 0:1], min_val=0, max_val=1)
            with sp.If(wide > 0):
                for k in range(GB):
                    sp.wait_ge(s_adj[k], 16)
                sp.dma_start(raw[:, 0, :], adjT[0]).then_inc(s_wa, 16)
                with sp.Fori(1, NT) as t:
                    sp.wait_ge(s_wr, t)
                    sp.dma_start(raw[:, 0, :], adjT[bass.ds(t, 1)].rearrange("a p n -> (a p) n")).then_inc(s_wa, 16)
                sp.wait_ge(s_wu, 1)
                sp.dma_start(unit[:, 0:(NT - 1) * P], raw[:, 1, 0:(NT - 1) * P]).then_inc(s_wuo, 16)
                sp.dma_start(unit[:, NT * P:], raw[:, 1, 0:(NT - 1) * P]).then_inc(s_wuo, 16)
                sp.dma_start(unit[:, (NT - 1) * P:NT * P], raw[:, 2, 0:P]).then_inc(s_wuo, 16)
                sp.wait_ge(s_wuo, 48)
                for k in range(GB):
                    sp.dma_start(raw[:, k, :], unit[:, k * P:k * P + N]).then_inc(s_ww[k], 16)
                stream(window)
            with sp.Else():
                stream(lambda t: adjT[bass.ds(t, 1)].rearrange("a p n -> (a p) n"))
            sp.wait_ge(s_mask, NT - 1)
            sp.dma_start(w1, w1_in).then_inc(s_w, 16)
            sp.wait_ge(s_mask, NT)
            sp.dma_start(w2, w2_in).then_inc(s_w, 16)
            sp.wait_ge(s_pad, 1)
            for e in range(E):
                last = sp.value_load(padrow[0:1, e:e + 1], min_val=0, max_val=E * REGION - P)
                sp.dma_start(disp[bass.ds(last, P), :], pad[:, e, :]).then_inc(s_pd, 16)
            sp.wait_ge(s_spare, 16)
            sp.wait_ge(s_tab, 1)
            for i in range(2):
                sp.wait_ge(s_sc[i], 16 * TOP * GB * NB // 2)
            sp.wait_ge(s_pd, 16 * E)

            def load(s, j):
                rb = sp.value_load(tabi[0:1, 0, bass.ds(s, 1)], min_val=0, max_val=E * REGION + (SPARE - 1) * P)
                sp.dma_start(xs[:, j, :], disp[bass.ds(rb, P), :]).then_inc(s_xsw[j], 16)

            for s in range(8):
                load(s, s)
            with sp.Fori(1, SLOTS // 8) as o:
                for j in range(8):
                    s = 8 * o + j
                    sp.wait_ge(s_T, s - 7)
                    sp.wait_ge(s_ys, s - 7)
                    sp.wait_ge(s_yi, s - 7)
                    load(s, j)
            for j in range(4):
                sp.wait_ge(s_yo[j], 16 * (SLOTS // 4))
            for c in range(4):
                for k in range(TOP):
                    src = planes[k * N + c * 1024:k * N + (c + 1) * 1024, :].rearrange("(t p) d -> p t d", p=P)
                    sp.dma_start(yplane[k][:, CH * c:CH * c + CH, :], src).then_inc(s_pl[c], 16)
            for c in range(4):
                sp.wait_ge(s_fin, c + 1)
                dst = out[c * 1024:(c + 1) * 1024, :].rearrange("(t p) d -> p t d", p=P)
                sp.dma_start(dst, x[:, CH * c:CH * c + CH, :]).then_inc(s_out, 16)
            sp.wait_ge(s_out, 64)

        @block.gpsimd
        def _(pool):
            st = Steps(pool, s_pc)
            st.did(pool.memset(ident[:], 0.0))
            st.did(pool.memset(ones[:], 1.0))
            st.did(pool.memset(onesb[:], 1.0))
            st.did(pool.memset(nhalf[:], -HALF_LN_SCALE))
            st.did(pool.memset(hsum[:, D:G], float(N)))
            st.did(pool.memset(spare, 0.0))
            st.did(pool.memset(pad, 0.0))
            st.did(pool.iota(ia[:, 0:NT], pattern=[[P, NT]], base=0, channel_multiplier=1))
            st.settle()
            pool.affine_select(out=ident[:], in_=ident[:], compare_op=ALU.not_equal, fill=1.0,
                               base=0, pattern=[[-1, P]], channel_multiplier=1).then_inc(s_const, 1)
            st.did(pool.affine_select(out=ltri[:], in_=onesb[:], compare_op=ALU.is_gt, fill=0.0,
                                      base=0, pattern=[[1, P]], channel_multiplier=-1))
            st.did(pool.tensor_copy(tokid[:], ia[:, 0:NT]))
            st.settle()
            st.step(pool.iota(ia[:, 0:SLOTS], pattern=[[1, SLOTS]], base=0, channel_multiplier=0))
            st.did(pool.tensor_copy(slotno[:], ia[:, 0:SLOTS]))
            st.did(pool.tensor_copy(iota8[:], ia[:, 0:E]))
            st.settle()
            st.step(pool.iota(ia[:, 0:E], pattern=[[REGION, E]], base=0, channel_multiplier=0))
            st.did(pool.tensor_copy(region0[:], ia[:, 0:E]))
            st.did(pool.tensor_copy(run[:], ia[:, 0:E]))
            st.settle()
            st.step(pool.iota(ia[:, 0:SPARE], pattern=[[P, SPARE]], base=TOP * N + E * P, channel_multiplier=1))
            st.step(pool.tensor_copy(spare[:, :, D + 1], ia[:, 0:SPARE]))
            st.step(pool.iota(ia[:, 0:E], pattern=[[P, E]], base=TOP * N, channel_multiplier=1))
            pool.tensor_copy(pad[:, :, D + 1], ia[:, 0:E]).then_inc(s_const, 1)
            pool.wait_ge(s_const, 2)
            pool.dma_start(disp[E * REGION:, :].rearrange("(e p) r -> p e r", p=P), spare).then_inc(s_spare, 16)

            def pass_wait(i, done):
                pool.tensor_tensor(out=still[:, i:i + 1], in0=nhalf[:], in1=nhalf[:], op=ALU.add).then_inc(done, 1)

            with pool.Fori(0, NB // 2) as o:
                for par in range(2):
                    pool.wait_ge(s_sl, 2 * o + par + 1)
                    pass_wait(par, s_sp)
                    for c in range(TOP):
                        for k in range(GB):
                            i = c * GB + k
                            pool.indirect_dma_start(disp, bass.IndirectOffsetOnAxis(slot[:, i:i + 1], axis=0),
                                                    xrow[:, par, k, c, :], None).then_inc(s_sc[par], 16)
            with pool.Fori(0, SLOTS // 4) as o:
                for j in range(4):
                    s = 4 * o + j
                    pool.wait_ge(s_ys, s + 1)
                    pool.wait_ge(s_yi, s + 1)
                    pass_wait(2 + j, s_yp)
                    pool.indirect_dma_start(planes, bass.IndirectOffsetOnAxis(yid[:, j:j + 1], axis=0),
                                            ys[:, j, :], None).then_inc(s_yo[j], 16)

        @block.tensor
        def _(pe):
            mmul = pe.matmul
            pe.wait_ge(s_small, 80)
            mmul(ps[0][0:DC, 0:1], waT[:, 0:DC], a2, start=True, stop=True).then_inc(s_pw, 1)
            pe.wait_ge(s_pwc, 1)
            mmul(ps[0][:, 0:G], wgT[0:DC, :], waq[0:DC, :], start=True, stop=True).then_inc(s_pw, 1)
            pe.wait_ge(s_pwc, 2)
            pe.wait_ge(s_cdve, 1)
            mmul(ps[0][:, 0:256], center[:], vraw, start=True, stop=True).then_inc(s_pw, 1)
            pe.wait_ge(s_pwc, 3)
            for t in range(NT):
                if t % CH == 0:
                    pe.wait_ge(s_xT[t // CH], 16)
                if t >= 16:
                    pe.wait_ge(s_fcd, t // 2 - 7)
                    pe.wait_ge(s_fca, t // 2 * 2 - 14)
                mmul(ps[t // 2 % 8][:, t % 2 * 256:t % 2 * 256 + 256], xT[:, t * P:(t + 1) * P], vc[:],
                     start=True, stop=True).then_inc(s_ft, 1)
            pe.wait_ge(s_fcd, NT // 2)
            pe.wait_ge(s_fca, NT)
            pe.wait_ge(s_mt, 1)
            pe.transpose(ps[4][0:2, 0:P], mm[:, 0:2], ident[:]).then_inc(s_mb, 1)
            pe.wait_ge(s_md, 1)
            mmul(ps[4][:, 128:130], ones[:], mm[0:2, 4:6], start=True, stop=True).then_inc(s_mb, 1)
            pe.wait_ge(s_flag, 1)
            wide = pe.value_load(flagi[0:1, 0:1], min_val=0, max_val=1)
            with pe.If(wide > 0):
                pe.wait_ge(s_wp, 1)
                for t in range(NT):
                    m = mmul(ps[3][:, 0:G], onesf, h3[:, t, :], start=(t == 0), stop=(t == NT - 1))
                m.then_inc(s_wo, 1)
                with pe.Fori(0, NT) as t:
                    pe.wait_ge(s_wpm, t + 1)
                    pe.transpose(ps[0][:, 0:P], part_max, ident[:]).then_inc(s_wt, 1)
                    pe.wait_ge(s_wd, t + 1)
                    mmul(ps[1][:, 0:P], onesf, diag, start=True, stop=True).then_inc(s_wm, 1)
                    pe.wait_ge(s_wp, t + 2)
                    for j in range(NT):
                        m = mmul(ps[2][:, 0:G], ex_row[:, j * P:(j + 1) * P], h3[:, j, :], start=(j == 0), stop=(j == NT - 1))
                    m.then_inc(s_wo, 1)
            for t in range(NT):
                m = mmul(ps[5][:, 0:1], x[:, t, :], vec[:, 15, t:t + 1], start=(t == 0), stop=(t == NT - 1))
            m.then_inc(s_u, 1)
            pe.wait_ge(s_ub, 1)
            mmul(ps[5][:, 128:256], ty[:, 0, :], vc[:, DC:DC + D], start=True, stop=True).then_inc(s_hp, 1)
            pe.wait_ge(s_ub, 2)

            def attend(b, k, first=False):
                n = GB * b + k
                pe.wait_ge(s_mask, n + 1)
                if not first:
                    pe.wait_ge(s_pf, n - GB + 1)
                for j in range(NT):
                    if first and k == 0 and j % CH == 0:
                        pe.wait_ge(s_gc, PARTS.index((2, j // CH)) + 1)
                    m = mmul(ps[k][:, 0:3 * G], mask[:, k, j * P:(j + 1) * P],
                             g[:, j, :, :].rearrange("p a b -> p (a b)"), start=(j == 0), stop=(j == NT - 1))
                m.then_inc(s_at, 1)

            def turn(b, par):
                pe.wait_ge(s_xl, b + 1)
                for k in range(GB):
                    m = pe.transpose(ps[4][:, k * P:(k + 1) * P], xrow[:, par, k, 0, 0:D], ident[:])
                m.then_inc(s_tt, 1)

            def gate(b):
                pe.wait_ge(s_ttc, b + 1)
                for k in range(GB):
                    m = mmul(ps[5][:, k * E:(k + 1) * E], xlT[:, k * P:(k + 1) * P], gatew[:], start=True, stop=True)
                m.then_inc(s_lg, 1)

            def places(b):
                pe.wait_ge(s_m, b + 1)
                for k in range(GB):
                    for i in range(k + 1):
                        mmul(ps[6][:, k * E:(k + 1) * E], (ltri if i == k else onesb)[:], both[:, i * E:(i + 1) * E],
                             start=(i == 0), stop=(i == k))
                for i in range(GB):
                    m = mmul(ps[6][:, GB * E:GB * E + E], onesb[:], both[:, i * E:(i + 1) * E],
                             start=(i == 0), stop=(i == GB - 1))
                m.then_inc(s_pr, 1)

            def batch(b, par, first=False, route=True):
                if route:
                    turn(b - 3, 1 - par)
                attend(b, 0, first)
                if route:
                    gate(b - 3)
                attend(b, 1, first)
                if route:
                    places(b - 3)
                attend(b, 2, first)
                attend(b, 3, first)

            pe.wait_ge(s_gw, 32)
            batch(0, 0, True, False)
            batch(1, 1, False, False)
            batch(2, 0, False, False)
            batch(3, 1)
            with pe.Fori(2, NB // 2) as o:
                for par in range(2):
                    batch(2 * o + par, par)
            for b in (NB - 3, NB - 2, NB - 1):
                turn(b, b % 2)
                gate(b)
                places(b)

            def turn_rows(s, j):
                pe.wait_ge(s_xsw[j], 2 * (s - j) + 16)
                if not (isinstance(s, int) and s < 2):
                    pe.wait_ge(s_Tc, s - 1)
                pe.transpose(ps[(4, 7)[j % 2]][:, 0:P], xs[:, j, 0:D], ident[:]).then_inc(s_T, 1)

            def layer1(s, j):
                pe.wait_ge(s_Tc, s + 1)
                pe.wait_ge(s_wc, s + 1)
                if not (isinstance(s, int) and s < 4):
                    pe.wait_ge(s_ge, s - 3)
                for k in range(HK):
                    m = mmul(ps[j % 4][:, k * P:(k + 1) * P], w1c[:, j % 4, k * P:(k + 1) * P], xsT[:, j % 4, :],
                             start=True, stop=True)
                m.then_inc(s_L1, 1)

            def layer2(s, j):
                pe.wait_ge(s_ge, s + 1)
                if not (isinstance(s, int) and s < 2):
                    pe.wait_ge(s_ya, s - 1)
                for k in range(HK):
                    m = mmul(ps[5 + j % 2][:, 0:D], hT[:, j % 4, k * P:(k + 1) * P],
                             w2c[:, j % 4, k * P:(k + 1) * P], start=(k == 0), stop=(k == HK - 1))
                m.then_inc(s_L2, 1)

            pe.wait_ge(s_w, 64)
            pe.wait_ge(s_tab, 1)
            for s in range(4):
                turn_rows(s, s)
            layer1(0, 0)
            layer1(1, 1)

            def slot_step(s, j):
                if not isinstance(s, int) or s + 4 < SLOTS:
                    turn_rows(s + 4, (j + 4) % 8)
                if not isinstance(s, int) or s + 2 < SLOTS:
                    layer1(s + 2, (j + 2) % 8)
                layer2(s, j)

            for s in range(8):
                slot_step(s, s)
            with pe.Fori(1, SLOTS // 8 - 1) as o:
                for j in range(8):
                    slot_step(8 * o + j, j)
            for j in range(8):
                slot_step(SLOTS - 8 + j, j)

        @block.scalar
        def _(act):
            act.preload_act_table_set("natural_log_exp_and_others")
            st = Steps(act, s_as)
            if True:
                for t in range(NT):
                    act.wait_ge(s_fcd, t // 2 + 1)
                    if t >= 4:
                        act.wait_ge(s_fca, t - 3)
                    act.activation(sqj[:, t % 4, 0:DC], ps[t // 2 % 8][:, t % 2 * 256:t % 2 * 256 + DC], ACT.Square,
                                   accum_out=vec[:, 19, t:t + 1]).then_inc(s_fca, 1)

            def root(o, v):
                return ((o, v, ACT.Ln, dict(scale=LN_SCALE)), (o, o, ACT.Exp, dict(scale=0.5, bias=nhalf[:])))

            def functions(st, ready, n, done, *ops):
                act.wait_ge(ready, n)
                for i, (o, a, f, kw) in enumerate(ops):
                    ins = act.activation(o, a, f, **kw)
                    if i < len(ops) - 1:
                        st.step(ins)
                    else:
                        ins.then_inc(done, 1)

            functions(st, s_va, 1, s_av, *root(vec[:, 3:6, :], vec[:, 0:3, :]))
            functions(st, s_va, 2, s_av, *root(vec[:, 7, :], vec[:, 6, :]))
            functions(st, s_va, 3, s_av, (vec[:, 8, :], vec[:, 8, :], ACT.Ln, {}))
            functions(st, s_va, 4, s_av, (vec[:, 20, :], vec[:, 9, :], ACT.Exp, {}))
            functions(st, s_va, 5, s_av, (vec[:, 14, :], vec[:, 14, :], ACT.Ln, {}))
            functions(st, s_va, 6, s_av, (vec[:, 23, :], vec[:, 22, :], ACT.Exp, dict(bias=mm[:, 6:7])))
            act.wait_ge(s_flag, 1)
            wide = act.value_load(flagi[0:1, 0:1], min_val=0, max_val=1)
            with act.If(wide > 0):
                with act.Fori(0, NT) as t:
                    act.wait_ge(s_wx, t + 1)
                    act.activation(ex_row, sc_row, ACT.Exp).then_inc(s_we, 1)
            for n, (p, c) in enumerate(PARTS):
                act.wait_ge(s_gf, n + 1)
                act.activation(g[:, CH * c:CH * c + CH, p, :], h3[:, CH * c:CH * c + CH, :], ACT.Copy).then_inc(s_gc, 1)

            def copy_turned(b):
                act.wait_ge(s_tt, b + 1)
                act.activation(xlT[:], ps[4][:], ACT.Copy).then_inc(s_ttc, 1)

            def gate_exp(b):
                act.wait_ge(s_dl, b + 1)
                act.activation(bv[:, 24, :], bv[:, 23, :], ACT.Exp).then_inc(s_de, 1)

            def elu_exp(b, par, st):
                act.wait_ge(s_e1, b + 1)
                for k in range(GB):
                    st.did(act.activation(ta[:, k, :], tk[:, k, 0:D], ACT.Copy, scale=bv[:, 28, k:k + 1]))
                st.settle()
                st.step(act.activation(ty[:], ta[:], ACT.Relu, scale=-1.0))
                act.activation(te[:, par], ty[:], ACT.Exp, scale=-1.0)
                act.activation(ta[:], ta[:], ACT.Relu).then_inc(s_e2, 1)

            def square_y(b):
                act.wait_ge(s_y1, b + 1)
                for k in range(GB):
                    m = act.activation(sqj[:, k, 0:DC], ty[:, k, 1:D], ACT.Square, accum_out=bv[:, 0, k:k + 1])
                m.then_inc(s_y2, 1)

            def sigmoid(b, par, st):
                act.preload_act_table_set("sigmoid_and_others")
                act.wait_ge(s_al2, b + 1)
                for k in range(GB):
                    st.did(act.activation(te[:, par, k, :], ty[:, k, :], ACT.Sigmoid, scale=bv[:, 8, k:k + 1]))
                st.settle()
                for k in range(GB):
                    m = act.activation(junk[:, 1, k, 0:DC], te[:, par, k, 1:D], ACT.Square, accum_out=bv[:, 9, k:k + 1])
                m.then_inc(s_sg2, 1)
                act.preload_act_table_set("natural_log_exp_and_others")

            def square_x1(b, st):
                act.wait_ge(s_x1, b + 1)
                for k in range(GB):
                    st.did(act.activation(x[:, bass.ds(GB * b + k, 1), :], x1[:, k:k + 1, :], ACT.Copy,
                                          accum_out=bv[:, 18, k:k + 1]))
                st.settle()
                st.step(act.activation(bv[:, 17, :], bv[:, 18, :], ACT.Copy, scale=-1.0 / D))
                for k in range(GB):
                    m = act.activation(junk[:, 0, k, :], x1[:, k, :], ACT.Square, bias=bv[:, 17, k:k + 1],
                                       accum_out=bv[:, 18, k:k + 1])
                m.then_inc(s_x2, 1)

            def normalise(b, par):
                act.wait_ge(s_ns, b + 1)
                for k in range(GB):
                    m = act.activation(xrow[:, par, k, :, 0:D], x1[:, k:k + 1, :].to_broadcast([P, TOP, D]),
                                       ACT.Identity, scale=bv[:, 21, k:k + 1], bias=bv[:, 22, k:k + 1])
                m.then_inc(s_xl, 1)

            BAS, BCS = 10, 7

            def batch(b, par, log=True, exp=True, route=True):
                lst, est = Steps(act, s_bas, BAS * (b - 1)), Steps(act, s_bcs, BCS * (b - 2))
                if exp:
                    functions(est, s_rc, 2 * b - 3, s_rca, *root(bv[:, 11, :], bv[:, 10, :]))
                    functions(est, s_rc, 2 * b - 2, s_rca, (bv[:, 12, :], bv[:, 11, :], ACT.Exp, {}))
                if route:
                    copy_turned(b - 3)
                if log:
                    elu_exp(b - 1, 1 - par, lst)
                if exp:
                    square_x1(b - 2, est)
                if log:
                    square_y(b - 1)
                if route:
                    gate_exp(b - 3)
                if log:
                    functions(lst, s_r, 2 * b - 1, s_ra, *root(bv[:, 4:7, :], bv[:, 1:4, :]))
                if exp:
                    functions(est, s_var, b - 1, s_varr, *root(bv[:, 20, :], bv[:, 19, :]))
                if log:
                    functions(lst, s_r, 2 * b, s_ra, (bv[:, 7, :], bv[:, 7, :], ACT.Ln, {}))
                if exp:
                    normalise(b - 2, par)
                if log:
                    sigmoid(b - 1, 1 - par, lst)
                    assert lst.n == BAS, lst.n
                if exp:
                    assert est.n == BCS, est.n

            batch(1, 1, exp=False, route=False)
            batch(2, 0, route=False)
            batch(3, 1)
            with act.Fori(2, NB // 2) as o:
                for par in range(2):
                    batch(2 * o + par, par)
            batch(NB, 0)
            batch(NB + 1, 1, log=False)
            batch(NB + 2, 0, log=False, exp=False)

            act.preload_act_table(ACT.Gelu)

            def gelu(s, j):
                act.wait_ge(s_L1, s + 1)
                if not (isinstance(s, int) and s < 4):
                    act.wait_ge(s_L2, s - 3)
                for k in range(HK):
                    m = act.activation(hT[:, j % 4, k * P:(k + 1) * P], ps[j % 4][:, k * P:(k + 1) * P], ACT.Gelu,
                                       bias=b1c[:, j % 4, k:k + 1])
                m.then_inc(s_ge, 1)

            def weigh(s, j):
                act.wait_ge(s_ya, s + 1)
                if not (isinstance(s, int) and s < 4):
                    act.wait_ge(s_yp, s - 3)
                    act.wait_ge(s_yo[j % 4], 4 * (s - j % 4))
                act.activation(ys[:, j % 4, :], ya[:, j % 2, :], ACT.Copy, scale=xs[:, j, D:D + 1]).then_inc(s_ys, 1)

            gelu(0, 0)
            gelu(1, 1)

            def slot_step(s, j):
                if not isinstance(s, int) or s + 2 < SLOTS:
                    gelu(s + 2, (j + 2) % 8)
                weigh(s, j)

            for j in range(8):
                slot_step(j, j)
            with act.Fori(1, SLOTS // 8 - 1) as o:
                for j in range(8):
                    slot_step(8 * o + j, j)
            for j in range(8):
                slot_step(SLOTS - 8 + j, j)

        @block.vector
        def _(v):
            st = Steps(v, s_vs)
            TT, TS, STT = v.tensor_tensor, v.tensor_scalar, v.scalar_tensor_tensor

            def newton(st, u, val, tmp):
                st.step(v.reciprocal(tmp, u))
                st.step(STT(out=tmp, in0=val, scalar=0.5, in1=tmp, op0=ALU.mult, op1=ALU.mult))
                st.step(STT(out=u, in0=u, scalar=0.5, in1=tmp, op0=ALU.mult, op1=ALU.add))

            v.wait_ge(s_const, 1)
            TS(center[:], ident[:], -1.0 / D, None, ALU.add).then_inc(s_cdve, 1)
            v.wait_ge(s_pw, 1)
            v.tensor_copy(waq[0:DC, D:G], ps[0][0:DC, 0:1]).then_inc(s_pwc, 1)
            v.wait_ge(s_pw, 2)
            v.tensor_copy(vraw[:, DC:256], ps[0][:, 0:G]).then_inc(s_pwc, 1)
            v.wait_ge(s_pw, 3)
            v.tensor_copy(vc[:], ps[0][:, 0:256]).then_inc(s_pwc, 1)

            def take_features(i):
                v.wait_ge(s_ft, 2 * i + 2)
                v.tensor_copy(h3[:, 2 * i:2 * i + 2, :],
                              ps[i % 8][:].rearrange("p (a c) -> p a c", a=2)[:, :, DC:256]).then_inc(s_fcd, 1)

            EV, OD = D // 2, DC - D // 2
            for c in range(4):
                v.wait_ge(s_x[c], 16)
                for i in range(CH // 2):
                    for t in (CH * c + 2 * i, CH * c + 2 * i + 1):
                        st.did(v.bn_stats(bn[:, t, :], x[:, t, 1:D]))
                    if c < 3:
                        take_features(4 * c + i)
            st.settle()
            mean_e, m2_e, mean_o, m2_o = (bn[:, :, i] for i in (1, 2, 4, 5))
            st.did(TT(vec[:, 16, :], mean_e, mean_o, ALU.subtract))
            st.step(TT(vec[:, 18, :], m2_e, m2_o, ALU.add))
            st.did(STT(out=vec[:, 20, :], in0=vec[:, 16, :], scalar=EV * OD / DC, in1=vec[:, 16, :], op0=ALU.mult, op1=ALU.mult))
            st.step(STT(out=vec[:, 21, :], in0=vec[:, 16, :], scalar=EV / DC, in1=mean_o, op0=ALU.mult, op1=ALU.add))
            st.did(TT(vec[:, 18, :], vec[:, 18, :], vec[:, 20, :], ALU.add))
            st.step(TT(vec[:, 16, :], x[:, :, 0], vec[:, 21, :], ALU.subtract))
            st.did(TS(vec[:, 17, :], vec[:, 16, :], DC / D, None, ALU.mult))
            st.step(STT(out=vec[:, 21, :], in0=vec[:, 16, :], scalar=DC / D ** 2, in1=vec[:, 16, :], op0=ALU.mult, op1=ALU.mult))
            st.did(TT(vec[:, 18, :], vec[:, 18, :], vec[:, 21, :], ALU.add))
            st.step(TT(vec[:, 20, :], vec[:, 17, :], vec[:, 17, :], ALU.mult))
            st.step(TT(vec[:, 20, :], vec[:, 20, :], vec[:, 18, :], ALU.add))
            for i in range(12, 16):
                take_features(i)
            v.wait_ge(s_fca, NT)
            st.did(TS(vec[:, 0, :], vec[:, 20, :], 1.0 / D, LN_EPS, ALU.mult, ALU.add))
            st.did(TS(vec[:, 1, :], vec[:, 18, :], NORM2_MIN, None, ALU.max))
            st.settle()
            TS(vec[:, 2, :], vec[:, 19, :], NORM2_MIN, None, ALU.max).then_inc(s_va, 1)
            v.wait_ge(s_va, 1)
            v.wait_ge(s_av, 1)
            newton(st, vec[:, 3:6, :], vec[:, 0:3, :], vt[:])
            st.step(v.reciprocal(vec[:, 26, :], vec[:, 3:5, :][:, 0, :]))
            st.step(TT(vec[:, 24, :], vec[:, 17, :], vec[:, 26, :], ALU.mult))
            st.step(TS(vec[:, 24, :], vec[:, 24, :], THETA_MIN, None, ALU.max))
            st.step(TS(vec[:, 6, :], vec[:, 24, :], 1.0, None, ALU.add))
            STT(out=vec[:, 6, :], in0=vec[:, 24, :], scalar=-1.0, in1=vec[:, 6, :],
                op0=ALU.add, op1=ALU.mult).then_inc(s_va, 1)
            v.wait_ge(s_va, 2)
            v.wait_ge(s_av, 2)
            newton(st, vec[:, 7, :], vec[:, 6, :], vt[:, 0, :])
            TT(vec[:, 8, :], vec[:, 24, :], vec[:, 7, :], ALU.add).then_inc(s_va, 1)
            st.step(v.reciprocal(vec[:, 26, :], vec[:, 4, :]))
            v.wait_ge(s_av, 3)
            st.step(TT(vec[:, 15, :], vec[:, 8, :], vec[:, 26, :], ALU.mult))
            TT(vec[:, 9, :], vec[:, 15, :], vec[:, 5, :], ALU.mult).then_inc(s_va, 1)
            v.wait_ge(s_va, 4)
            v.wait_ge(s_av, 4)
            st.step(v.reciprocal(vec[:, 21, :], vec[:, 20, :]))
            st.did(TT(vec[:, 12, :], vec[:, 20, :], vec[:, 21, :], ALU.subtract))
            st.step(TT(vec[:, 13, :], vec[:, 20, :], vec[:, 21, :], ALU.add))
            st.did(TS(vec[:, 12, :], vec[:, 12, :], 0.5, ROOT_CL, ALU.mult, ALU.max))
            st.step(TS(vec[:, 13, :], vec[:, 13, :], 0.5, THETA_MIN, ALU.mult, ALU.max))
            TT(vec[:, 14, :], vec[:, 12, :], vec[:, 13, :], ALU.add).then_inc(s_va, 1)
            st.step(TS(vec[:, 25, :], vec[:, 9, :], 1e-15, None, ALU.max))
            st.step(v.reciprocal(vec[:, 25, :], vec[:, 25, :]))
            v.wait_ge(s_av, 5)
            st.step(TT(vec[:, 25, :], vec[:, 14, :], vec[:, 25, :], ALU.mult))
            TT(vec[:, 15, :], vec[:, 15, :], vec[:, 25, :], ALU.mult).then_inc(s_al, 1)
            v.wait_ge(s_al, 1)
            st.step(TT(vec[:, 22, :], h3[:, :, D], vec[:, 15, :], ALU.mult))
            st.did(v.reduce_max(mm[:, 0:1], vec[:, 22, :], AX_X))
            st.step(TS(vec[:, 21, :], vec[:, 22, :], -1.0, None, ALU.mult))
            v.reduce_max(mm[:, 1:2], vec[:, 21, :], AX_X).then_inc(s_mt, 1)
            v.wait_ge(s_mb, 1)
            st.step(v.reduce_max(mm[0:2, 2:3], ps[4][0:2, 0:P], AX_X))
            TS(mm[0:2, 4:6], ident[0:2, 0:2], mm[0:2, 2:3], None, ALU.mult).then_inc(s_md, 1)
            v.wait_ge(s_mb, 2)
            TS(mm[:, 6:7], ps[4][:, 128:129], -1.0, None, ALU.mult).then_inc(s_va, 1)
            st.step(v.tensor_copy(mm[:, 7:8], ps[4][:, 129:130]))
            st.step(TT(mm[:, 7:8], mm[:, 7:8], mm[:, 6:7], ALU.subtract))
            TS(flagi[:], mm[:, 7:8], SPREAD_MAX, None, ALU.is_gt).then_inc(s_flag, 1)

            def make_mask(b, k, half, first=False):
                if half == 0:
                    v.wait_ge(s_adj[k], 16 * b + 16)
                    if not first:
                        v.wait_ge(s_at, GB * b + k - GB + 1)
                    elif k == 2:
                        v.wait_ge(s_spare, 16)
                cols = slice(half * N // 2, (half + 1) * N // 2)
                ins = TS(mask[:, k, cols], raw[:, k, cols], 0, None, ALU.is_gt)
                if half == 1:
                    ins.then_inc(s_mask, 1)

            v.wait_ge(s_av, 6)
            st.step(TT(vec[:, 24, :], vec[:, 15, :], vec[:, 23, :], ALU.mult))

            def wide_softmax():
                st = Steps(v, s_wv)
                alpha = vec[:, 15, :].unsqueeze(2).to_broadcast([P, NT, D])
                st.did(TT(h3[:, :, 0:D], h3[:, :, 0:D], alpha, ALU.mult))
                st.step(v.tensor_scalar(vec[:, 22, :], vec[:, 22, :], ps[4][:, 129:130], 1.0, ALU.add, ALU.add))
                st.did(TS(h3[:, :, D], vec[:, 15, :], 0.0, 1.0, ALU.mult, ALU.add))
                for k in range(GB):
                    v.wait_ge(s_adj[k], 16)
                st.step(TS(onesf, ident[:], 0.0, 1.0, ALU.mult, ALU.add))
                v.tensor_copy(mm[:, 7:8], mm[:, 6:7]).then_inc(s_wp, 1)
                v.wait_ge(s_wo, 1)
                st.step(v.tensor_copy(tk[:, 0, :], ps[3][:, 0:G]))
                loop = Steps(v, s_wv, st.n)
                logits = vec[:, 22, :].unsqueeze(2).to_broadcast([P, NT, P])
                scores = sc_row.rearrange("p (j i) -> p j i", i=P)
                with v.Fori(0, NT) as t:
                    loop = Steps(v, s_wv, st.n + WIDE * t)
                    v.wait_ge(s_wa, 16 * t + 16)
                    loop.step(TS(sc_row, raw[:, 0, :], 0, None, ALU.is_gt))
                    loop.step(TT(scores, scores, logits, ALU.mult))
                    v.reduce_max(part_max, sc_row.rearrange("p (j i) -> p i j", i=P), AX_X).then_inc(s_wpm, 1)
                    v.wait_ge(s_wt, t + 1)
                    loop.step(v.reduce_max(ta[:, 0, 0:1], ps[0][:, 0:P], AX_X))
                    TS(diag, ident[:], ta[:, 0, 0:1], None, ALU.mult).then_inc(s_wd, 1)
                    v.wait_ge(s_wm, t + 1)
                    loop.step(v.tensor_copy(row_max, ps[1][:, 0:P]))
                    loop.step(TT(scores, scores, row_max.unsqueeze(1).to_broadcast([P, NT, P]), ALU.subtract))
                    TS(sc_row, sc_row, 0.0, None, ALU.min).then_inc(s_wx, 1)
                    v.wait_ge(s_we, t + 1)
                    loop.step(TS(sc_row, raw[:, 0, :], 0, None, ALU.is_gt))
                    TT(ex_row, ex_row, sc_row, ALU.mult).then_inc(s_wp, 1)
                    v.wait_ge(s_wo, t + 2)
                    loop.step(v.tensor_copy(tk[:, 1, :], ps[2][:, 0:G]))
                    loop.step(TS(ta[:, 0, 1:2], tk[:, 1, D:G], 0.0, None, ALU.is_equal))
                    loop.step(STT(out=tk[:, 1, :], in0=tk[:, 0, :], scalar=ta[:, 0, 1:2], in1=tk[:, 1, :],
                                  op0=ALU.mult, op1=ALU.add))
                    loop.step(v.reciprocal(ta[:, 0, 2:3], tk[:, 1, D:G]))
                    TS(gres[:, bass.ds(t, 1), :], tk[:, 1:2, 0:D], ta[:, 0, 2:3], None, ALU.mult).then_inc(s_wr, 1)
                    assert loop.n <= WIDE
                v.wait_ge(s_wr, NT)
                end = Steps(v, s_wv, st.n + WIDE * NT)
                with v.Fori(0, NT) as t:
                    TS(h3[:, bass.ds(NT - 1 - t, 1), 0:D], gres[:, bass.ds(t, 1), :], 1.0, None, ALU.mult).then_inc(s_wv, 1)
                end.n += NT
                for i in (23, 24):
                    end.did(TS(vec[:, i, :], vec[:, i, :], 0.0, 1.0, ALU.mult, ALU.add))
                end.did(TS(raw[:, 1, :], raw[:, 0, :], 0, None, ALU.mult))
                v.tensor_copy(raw[:, 2, 0:P], ident[:]).then_inc(s_wu, 1)
                end.settle()
                for k in range(GB):
                    v.wait_ge(s_ww[k], 16)

            WIDE = 10
            wide = v.value_load(flagi[0:1, 0:1], min_val=0, max_val=1)
            with v.If(wide > 0):
                wide_softmax()
            make_mask(0, 0, 0, True)
            make_mask(0, 0, 1, True)
            for n, (p, c) in enumerate(PARTS):
                cs = slice(CH * c, CH * c + CH)
                if p == 0:
                    st.step(TT(h3[:, cs, 0:D], h3[:, cs, 0:D], vec[:, 24, cs].unsqueeze(2).to_broadcast([P, CH, D]), ALU.mult))
                    v.tensor_copy(h3[:, cs, D], vec[:, 23, cs]).then_inc(s_gf, 1)
                else:
                    v.wait_ge(s_gc, PARTS.index((p - 1, c)) + 1)
                    TT(h3[:, cs, :], h3[:, cs, :], g[:, cs, p - 1, :], ALU.subtract).then_inc(s_gf, 1)
            v.wait_ge(s_u, 1)
            v.tensor_copy(ty[:, 0, :], ps[5][:, 0:1].to_broadcast([P, P])).then_inc(s_ub, 1)
            v.wait_ge(s_hp, 1)
            v.tensor_copy(hsum[:, 0:D], ps[5][:, 128:256]).then_inc(s_ub, 1)

            def take(b, k):
                st = Steps(v, s_tk, 2 * (GB * b + k))
                if k == 0 and not (isinstance(b, int) and b == 0):
                    v.wait_ge(s_e2, b)
                v.wait_ge(s_at, GB * b + k + 1)
                st.step(v.tensor_copy(tk[:, k, :], ps[k][:, 2 * G:3 * G]))
                st.step(TT(tk[:, k, :], tk[:, k, :], ps[k][:, G:2 * G], ALU.add))
                TT(tk[:, k, :], tk[:, k, :], ps[k][:, 0:G], ALU.add).then_inc(s_pf, 1)

            def divide(b, st):
                v.wait_ge(s_pf, GB * b + GB)
                st.step(TS(alone[:], tk[:, :, D:G], 0.0, None, ALU.is_equal))
                TS(carry[:], nhalf[:], 0.0, None, ALU.add)
                st.step(v.copy_predicated(tk[:], alone[:].to_broadcast([P, GB, G]),
                                          hsum[:].unsqueeze(1).to_broadcast([P, GB, G])))
                v.reciprocal(bv[:, 28, :], tk[:, :, D]).then_inc(s_e1, 1)

            def elu(b, par):
                v.wait_ge(s_e2, b + 1)
                STT(out=ty[:], in0=te[:, par], scalar=-1.0, in1=ta[:], op0=ALU.add, op1=ALU.add).then_inc(s_y1, 1)

            def log_bounds(b, st):
                v.wait_ge(s_y2, b + 1)
                st.did(TS(bv[:, 1, :], bv[:, 0, :], NORM2_MIN, None, ALU.max))
                st.step(TS(bv[:, 2, :], bv[:, 0, :], CL, None, ALU.max))
                TS(bv[:, 3, :], bv[:, 2, :], 1.0, None, ALU.add).then_inc(s_r, 1)

            def log_roots(b, st):
                v.wait_ge(s_r, 2 * b + 1)
                v.wait_ge(s_ra, 2 * b + 1)
                newton(st, bv[:, 4:7, :], bv[:, 1:4, :], bt[:, 0:3, :])
                TT(bv[:, 7, :], bv[:, 5, :], bv[:, 6, :], ALU.add).then_inc(s_r, 1)
                st.step(v.reciprocal(bv[:, 26, :], bv[:, 4, :]))

            def log_scale(b):
                v.wait_ge(s_ra, 2 * b + 2)
                TT(bv[:, 8, :], bv[:, 7, :], bv[:, 26, :], ALU.mult).then_inc(s_al2, 1)

            def exp_bound(b):
                v.wait_ge(s_sg2, b + 1)
                TS(bv[:, 10, :], bv[:, 9, :], NORM2_MIN, None, ALU.max).then_inc(s_rc, 1)

            def exp_root(b, st):
                v.wait_ge(s_rc, 2 * b + 1)
                v.wait_ge(s_rca, 2 * b + 1)
                st.step(v.reciprocal(bt[:, 3, :], bv[:, 11, :]))
                st.step(STT(out=bt[:, 3, :], in0=bv[:, 10, :], scalar=0.5, in1=bt[:, 3, :], op0=ALU.mult, op1=ALU.mult))
                STT(out=bv[:, 11, :], in0=bv[:, 11, :], scalar=0.5, in1=bt[:, 3, :], op0=ALU.mult, op1=ALU.add).then_inc(s_rc, 1)
                v.wait_ge(s_rc, 2 * b + 2)
                st.step(v.reciprocal(bv[:, 15, :], bv[:, 11, :]))

            def residual(b, par, st):
                v.wait_ge(s_rca, 2 * b + 2)
                st.step(v.reciprocal(bv[:, 13, :], bv[:, 12, :]))
                st.step(TT(bv[:, 16, :], bv[:, 12, :], bv[:, 13, :], ALU.subtract))
                st.did(TT(bv[:, 14, :], bv[:, 12, :], bv[:, 13, :], ALU.add))
                st.step(STT(out=bv[:, 15, :], in0=bv[:, 16, :], scalar=0.5, in1=bv[:, 15, :], op0=ALU.mult, op1=ALU.mult))
                if not (isinstance(b, int) and b == 0):
                    v.wait_ge(s_xl, b)
                for k in range(GB):
                    st.did(STT(out=x1[:, k:k + 1, 1:D], in0=te[:, par, k:k + 1, 1:D], scalar=bv[:, 15, k:k + 1],
                               in1=x[:, bass.ds(GB * b + k, 1), 1:D], op0=ALU.mult, op1=ALU.add))
                first = x[:, bass.ds(GB * b, GB), 0:1].rearrange("p t a -> p (t a)")
                STT(out=x1[:, :, 0], in0=bv[:, 14, :], scalar=0.5, in1=first, op0=ALU.mult, op1=ALU.add).then_inc(s_x1, 1)

            def variance(b):
                v.wait_ge(s_x2, b + 1)
                TS(bv[:, 19, :], bv[:, 18, :], 1.0 / D, LN_EPS, ALU.mult, ALU.add).then_inc(s_var, 1)

            def norm_scale(b, par, st):
                v.wait_ge(s_var, b + 1)
                v.wait_ge(s_varr, b + 1)
                newton(st, bv[:, 20, :], bv[:, 19, :], bt[:, 3, :])
                st.step(v.reciprocal(bv[:, 21, :], bv[:, 20, :]))
                if not (isinstance(b, int) and b < 2):
                    v.wait_ge(s_sc[par], 8 * TOP * GB * (b - par))
                TT(bv[:, 22, :], bv[:, 17, :], bv[:, 21, :], ALU.mult).then_inc(s_ns, 1)

            def choice1(b, par, st):
                v.wait_ge(s_lg, b + 1)
                st.did(TT(lg[:], ps[5][:, 0:GB * E].rearrange("p (k e) -> p k e", e=E),
                           bgb[:].unsqueeze(1).to_broadcast([P, GB, E]), ALU.add))
                st.settle()
                st.did(TS(xrow[:, par, :, 0, D + 1], tokid[:, bass.ds(GB * b, GB)], 0.0, None, ALU.add))
                for k in range(GB):
                    st.did(v.max(top[:, k, :], lg[:, k, :]))
                st.settle()
                st.did(TS(xrow[:, par, :, 1, D + 1], tokid[:, bass.ds(GB * b, GB)], float(N), None, ALU.add))
                for k in range(GB):
                    st.did(v.max_index(idx[:, k, :], top[:, k, :], lg[:, k, :]))
                TT(bv[:, 23, :], top[:, :, 1], top[:, :, 0], ALU.subtract).then_inc(s_dl, 1)

            def choice2(b, par, st):
                st.settle()
                st.step(v.tensor_copy(idxf[:], idx[:, :, 0:TOP].rearrange("p k c -> p c k")))
                st.did(TT(onehot[:].rearrange("p c k e -> p (c k) e"), iota8[:].unsqueeze(1).to_broadcast([P, TOP * GB, E]),
                          idxf[:].rearrange("p c k -> p (c k)").unsqueeze(2).to_broadcast([P, TOP * GB, E]), ALU.is_equal))
                st.settle()
                TT(both[:].rearrange("p (k e) -> p k e", e=E), onehot[:, 0], onehot[:, 1], ALU.add).then_inc(s_m, 1)
                v.wait_ge(s_de, b + 1)
                st.step(TS(bv[:, 23, :], bv[:, 24, :], 1.0, None, ALU.add))
                st.step(v.reciprocal(bv[:, 25, :], bv[:, 23, :]))
                st.did(v.tensor_copy(xrow[:, par, :, 0, D], bv[:, 25, :]))
                st.did(TT(xrow[:, par, :, 1, D], bv[:, 24, :], bv[:, 25, :], ALU.mult))

            def place(b, par, st):
                v.wait_ge(s_pr, b + 1)
                st.step(TT(rowid[:], ps[6][:, 0:GB * E].rearrange("p (k e) -> p k e", e=E),
                           run[:].unsqueeze(1).to_broadcast([P, GB, E]), ALU.add))
                st.did(TT(run[:], run[:], ps[6][:, GB * E:GB * E + E], ALU.add))
                st.step(TT(pick[:].rearrange("p (c k) e -> p c (k e)", c=TOP), onehot[:].rearrange("p c k e -> p c (k e)"),
                           rowid[:].rearrange("p k e -> p (k e)").unsqueeze(1).to_broadcast([P, TOP, GB * E]), ALU.mult))
                st.step(v.reduce_sum(slotf[:], pick[:], AX_X))
                if not (isinstance(b, int) and b == 0):
                    v.wait_ge(s_sp, b)
                    v.wait_ge(s_sc[1 - par], 8 * TOP * GB * (b - par) + (16 * TOP * GB if par else 0))
                v.tensor_copy(slot[:], slotf[:]).then_inc(s_sl, 1)

            EA, EB, EC, CHO, PL = 2, 6, 15, 17, 4
            ORDER = "m0 c1 t2 m1 c2 t3 a m2 c3 m3 b1 h1 c4 m4 b2 h2 c5 m5 t0 b3 m6 b4 p m7 t1".split()

            def batch(b, par, masks=True, log=True, exp=True, route=True, first=False, order=ORDER):
                a = Steps(v, s_ea, EA * (b - 1))
                bb = Steps(v, s_eb, EB * (b - 1))
                cc = Steps(v, s_ec, EC * (b - 2))
                hh = Steps(v, s_ch, CHO * (b - 3))
                pp = Steps(v, s_plc, PL * (b - 3))
                for o in order:
                    if o[0] == "m" and masks:
                        make_mask(b, int(o[1]) // 2, int(o[1]) % 2, first)
                    elif o in ("t0", "t1") and masks:
                        take(b, int(o[1]))
                    elif o in ("t2", "t3") and log:
                        take(b - 1, int(o[1]))
                    elif o == "a" and log:
                        divide(b - 1, a)
                    elif o == "b1" and log:
                        elu(b - 1, 1 - par)
                    elif o == "b2" and log:
                        log_bounds(b - 1, bb)
                    elif o == "b3" and log:
                        log_roots(b - 1, bb)
                    elif o == "b4" and log:
                        log_scale(b - 1)
                    elif o == "c1" and exp:
                        exp_bound(b - 2)
                    elif o == "c2" and exp:
                        exp_root(b - 2, cc)
                    elif o == "c3" and exp:
                        residual(b - 2, par, cc)
                    elif o == "c4" and exp:
                        variance(b - 2)
                    elif o == "c5" and exp:
                        norm_scale(b - 2, par, cc)
                    elif o == "h1" and route:
                        choice1(b - 3, 1 - par, hh)
                    elif o == "h2" and route:
                        choice2(b - 3, 1 - par, hh)
                    elif o == "p" and route:
                        place(b - 3, 1 - par, pp)
                if log:
                    assert a.n == EA and bb.n == EB, (a.n, bb.n)
                if exp:
                    assert cc.n == EC, cc.n
                if route:
                    assert hh.n == CHO and pp.n == PL, (hh.n, pp.n)

            batch(0, 0, first=True, log=False, exp=False, route=False, order=["m2", "m3", "m4", "m5", "t0", "m6", "m7", "t1"])
            batch(1, 1, exp=False, route=False)
            batch(2, 0, route=False)
            batch(3, 1)
            with v.Fori(2, NB // 2) as o:
                for par in range(2):
                    batch(2 * o + par, par)
            batch(NB, 0, masks=False)
            batch(NB + 1, 1, masks=False, log=False)
            batch(NB + 2, 0, masks=False, log=False, exp=False)

            v.wait_ge(s_sl, NB)
            v.tensor_copy(padrow[:], run[:]).then_inc(s_pad, 1)
            st.step(TT(cnt[:, 0, :], run[:], region0[:], ALU.subtract))
            st.step(TS(cnt[:, 0, :], cnt[:, 0, :], float(P - 1), None, ALU.add))
            st.step(v.tensor_copy(cnti[:, 0, :], cnt[:, 0, :]))
            st.step(TS(cnti[:, 1, :], cnti[:, 0, :], 7, None, ALU.arith_shift_right))
            st.step(v.tensor_copy(cnt[:, 1, :], cnti[:, 1, :]))
            st.step(v.tensor_copy(cnt[:, 2, :], cnt[:, 1, :]))
            for sh in (1, 2, 4):
                a, z = (2, 3) if sh != 2 else (3, 2)
                st.did(v.tensor_copy(cnt[:, z, 0:sh], cnt[:, a, 0:sh]))
                st.step(TT(cnt[:, z, sh:E], cnt[:, a, sh:E], cnt[:, a, 0:E - sh], ALU.add))
            slots = slotno[:].unsqueeze(2).to_broadcast([P, SLOTS, E])
            st.step(TT(cmpb, cnt[:, 3, :].unsqueeze(1).to_broadcast([P, SLOTS, E]), slots, ALU.is_le))
            st.step(v.reduce_sum(tabs[:, 0, :], cmpb, AX_X))
            st.step(TT(cmpb, cmpb, cnt[:, 1, :].unsqueeze(1).to_broadcast([P, SLOTS, E]), ALU.mult))
            st.step(v.reduce_sum(tabs[:, 1, :], cmpb, AX_X))
            st.step(TT(tabs[:, 1, :], slotno[:], tabs[:, 1, :], ALU.subtract))
            st.step(TS(tabs[:, 1, :], tabs[:, 1, :], float(P), None, ALU.mult))
            st.step(STT(out=tabs[:, 1, :], in0=tabs[:, 0, :], scalar=float(REGION), in1=tabs[:, 1, :],
                        op0=ALU.mult, op1=ALU.add))
            st.step(TS(tabs[:, 0, :], tabs[:, 0, :], float(E - 1), None, ALU.min))
            st.step(v.tensor_copy(tabi[:, 0, :], tabs[:, 1, :]))
            v.tensor_copy(tabi[:, 1, :], tabs[:, 0, :]).then_inc(s_tab, 1)
            v.wait_ge(s_tab, 1)

            def expert_of(s):
                return v.value_load(tabi[0:1, 1, bass.ds(s, 1)], min_val=0, max_val=E - 1)

            def fetch(s, j, e):
                if not (isinstance(s, int) and s < 4):
                    v.wait_ge(s_L1, s - 3)
                TS(w1c[:, j % 4, :], w1[:, bass.ds(e * H, H)], 1.0, None, ALU.mult)
                if not (isinstance(s, int) and s < 4):
                    v.wait_ge(s_ge, s - 3)
                TS(b1c[:, j % 4, :], b1t[:, bass.ds(e * HK, HK)], 1.0, None, ALU.mult)
                if not (isinstance(s, int) and s < 4):
                    v.wait_ge(s_L2, s - 3)
                TS(w2c[:, j % 4, :], w2[:, bass.ds(e * H, H)], 1.0, None, ALU.mult)
                if not (isinstance(s, int) and s < 8):
                    v.wait_ge(s_ya, s - 7)
                TS(b2c[:, j, :], b2b[:, bass.ds(e * D, D)], 1.0, None, ALU.mult).then_inc(s_wc, 1)

            def copy_rows(s, j):
                v.wait_ge(s_T, s + 1)
                if not (isinstance(s, int) and s < 4):
                    v.wait_ge(s_L1, s - 3)
                v.tensor_copy(xsT[:, j % 4, :], ps[(4, 7)[j % 2]][:, 0:P]).then_inc(s_Tc, 1)

            def result(s, j):
                v.wait_ge(s_L2, s + 1)
                if not (isinstance(s, int) and s < 2):
                    v.wait_ge(s_ys, s - 1)
                TT(ya[:, j % 2, :], ps[5 + j % 2][:, 0:D], b2c[:, j, :], ALU.add).then_inc(s_ya, 1)
                if not (isinstance(s, int) and s < 4):
                    v.wait_ge(s_yo[j % 4], 4 * (s - j % 4))
                v.tensor_copy(yid[:, j % 4:j % 4 + 1], xs[:, j, D + 1:D + 2]).then_inc(s_yi, 1)

            v.wait_ge(s_w, 64)
            for s in range(4):
                fetch(s, s, expert_of(s))
                copy_rows(s, s)

            def slot_steps(s0, tiles):
                for j in range(8):
                    s = s0 + j
                    if j + 4 < tiles:
                        if j % 2 == 0:
                            e = expert_of(s + 4), expert_of(s + 5)
                        fetch(s + 4, (j + 4) % 8, e[j % 2])
                        copy_rows(s + 4, (j + 4) % 8)
                    result(s, j)

            slot_steps(0, SLOTS)
            with v.Fori(1, SLOTS // 8 - 1) as o:
                slot_steps(8 * o, SLOTS)
            slot_steps(SLOTS - 8, 8)

            for c in range(4):
                cs = slice(CH * c, CH * c + CH)
                v.wait_ge(s_pl[c], 32)
                TT(x[:, cs, :], x[:, cs, :], yplane[0][:, cs, :], ALU.add).then_inc(s_fs, 1)
                v.wait_ge(s_fs, c + 1)
                TT(x[:, cs, :], x[:, cs, :], yplane[1][:, cs, :], ALU.add).then_inc(s_fin, 1)


def kernel(**inputs):
    import concourse.bacc as bacc
    from concourse.bass_utils import run_bass_kernel_spmd

    a = {k: np.asarray(v) for k, v in inputs.items()}
    x = a["x"]
    wg = np.zeros((D, DC), x.dtype)
    wg[1:, :] = a["L0_gnn_W_gcn"]
    wa = a["L0_gnn_W_att"][1:, :]
    arrays = {
        "x_rows": x.reshape(NT, P, D).transpose(1, 0, 2),
        "xT": x.T,
        "adjT": a["adj"].reshape(NT, P, NT, P).transpose(0, 3, 2, 1).reshape(NT, P, N),
        "w_gcn": wg,
        "w_gcnT": wg.T,
        "w_att": wa,
        "w_attT": wa.T,
        "a2": a["L0_gnn_a_att"][D:, :],
        "gate_w": a["L0_ffn_Wg"],
        "gate_b": a["L0_ffn_bg"],
        "w1": a["L0_ffn_W1"].transpose(1, 0, 2).reshape(D, E * H),
        "b1": a["L0_ffn_b1"].reshape(E * HK, P).T,
        "w2": a["L0_ffn_W2"].reshape(E, HK, P, D).transpose(2, 0, 1, 3).reshape(P, E * HK * D),
        "b2": a["L0_ffn_b2"].reshape(E * D),
    }
    arrays = {k: np.ascontiguousarray(v) for k, v in arrays.items()}
    nc = bacc.Bacc("TRN2", target_bir_lowering=False, num_devices=1)
    args = [nc.dram_tensor(f"in_{k}", v.shape, mybir.dt.from_np(v.dtype), kind="ExternalInput").ap() for k, v in arrays.items()]
    out = nc.dram_tensor("out", (N, D), F32, kind="ExternalOutput").ap()
    gnn_moe_kernel(nc, *args, out)
    result = run_bass_kernel_spmd(nc, [{f"in_{k}": v for k, v in arrays.items()}], core_ids=[0])
    return result.results[0]["out"]
```

```python
from contextlib import ExitStack

import numpy as np

import concourse.bass as bass
from concourse import mybir

F32 = mybir.dt.float32
BF16 = mybir.dt.bfloat16
I32 = mybir.dt.int32
U32 = mybir.dt.uint32
ALU = mybir.AluOpType
ACT = mybir.ActivationFunctionType
AX_X = mybir.AxisListType.X

P = 128
N = 4096
D = 128
NT = N // P
GB = 4
NB = NT // GB
DC = D - 1
G = D + 1
E = 8
H = 512
HK = H // P
TOP = 2
REGION = N + P
SLOTS = 72
SPARE = SLOTS - TOP * N // P
ROW = D + 2
LN_EPS = 1e-5
THETA_MIN = float(np.float32(1.0 + 1e-7))
CL = THETA_MIN ** 2 - 1.0
ROOT_CL = CL ** 0.5
NORM2_MIN = 1e-30
SPREAD_MAX = 50.0
LN_SCALE = 2.0 ** 36
HALF_LN_SCALE = 18.0 * float(np.log(2.0))
CH = NT // 4
PARTS = sorted(((p, c) for p in range(3) for c in range(4)), key=lambda pc: (pc[0] + pc[1], pc[0]))
CASTS = [pc for pc in PARTS if pc[0] < 2]


class Steps:

    def __init__(self, eng, sem, start=0):
        self.eng, self.sem, self.base, self.n = eng, sem, start, 0

    def value(self):
        return self.base + self.n

    def did(self, ins):
        ins.then_inc(self.sem, 1)
        self.n += 1

    def settle(self):
        self.eng.wait_ge(self.sem, self.base + self.n)

    def step(self, ins):
        self.did(ins)
        self.settle()



def gnn_moe_kernel(nc, x_rows, xT_in, adjT, wg_in, wgT_in, wa_in, waT_in, a2_in,
                   gate_in, bg_in, w1_in, b1_in, w2_in, b2_in, out):
    disp = nc.dram_tensor("disp", [E * REGION + SPARE * P, ROW], F32).ap()
    unit = nc.dram_tensor("unit", [P, (2 * NT - 1) * P], I32).ap()
    planes = nc.dram_tensor("planes", [TOP * N + (E + SPARE) * P, D], F32).ap()
    with ExitStack() as ctx:
        def sb(name, shape, dt=F32):
            return ctx.enter_context(nc.sbuf_tensor(name, shape, dt))

        def sem(name):
            return ctx.enter_context(nc.semaphore(name))

        x = sb("x", [P, NT, D])
        hb = sb("hb", [P, NT * G])
        h3 = hb[:].rearrange("p (t g) -> p t g", g=G)
        w2c = hb[:, 0:4 * H].rearrange("p (s r) -> p s r", r=H)
        b2c = hb[:, 4 * H:4 * H + 8 * D].rearrange("p (s r) -> p s r", r=D)
        gb = sb("gb", [P, NT * 3 * G], BF16)
        g = gb[:].rearrange("p (t a b) -> p t a b", a=3, b=G)
        b1t = sb("b1t", [P, E * HK])
        b2b = sb("b2b", [P, E * D])
        raw = sb("raw", [P, 4, N], I32)
        mask = sb("mask", [P, GB, N], BF16)
        maskf = mask[:].rearrange("p a n -> p (a n)").bitcast(F32)
        xT = maskf[:, 0:N]
        rawf = raw[:].bitcast(F32).rearrange("p a n -> p (a n)")
        ident = sb("ident", [P, P])
        ones = sb("ones", [2, P])
        center = sb("center", [P, P])
        ltri = sb("ltri", [P, P], BF16)
        onesb = sb("onesb", [P, P], BF16)
        gatew = sb("gatew", [P, E])
        bgb = sb("bgb", [P, E])
        iota8 = sb("iota8", [P, E])
        region0 = sb("region0", [P, E])
        tokid = sb("tokid", [P, NT])
        ia = sb("ia", [P, SLOTS], I32)
        slotno = sb("slotno", [P, SLOTS])
        nhalf = sb("nhalf", [P, 1])
        sqj = sb("sqj", [P, 4, D], BF16)
        tk = sb("tk", [P, GB, G])
        alone = sb("alone", [P, GB, 1], U32)
        ta = sb("ta", [P, GB, D])
        ty = sb("ty", [P, GB, D])
        te = sb("te", [P, 2, GB, D])
        x1 = sb("x1", [P, 2, GB, D])
        xlT = sb("xlT", [P, GB * P])
        xrow = sb("xrow", [P, 2, GB, TOP, ROW])
        hsum = sb("hsum", [P, G])
        vc = sb("vc", [P, 256])
        vec = sb("vec", [P, 28, NT])
        junk = vec[:].rearrange("p a t -> p (a t)").bitcast(BF16)[:, 0:2 * GB * D].rearrange("p (a k d) -> p a k d", a=2, d=D)
        bn = sb("bn", [P, NT, 6])
        vt = sb("vt", [P, 3, NT])
        bv = sb("bv", [P, 29, GB])
        bt = sb("bt", [P, 4, GB])
        lg = sb("lg", [P, GB, E])
        top = sb("top", [P, GB, 8])
        idx = sb("idx", [P, GB, 8], U32)
        idxf = sb("idxf", [P, TOP, GB])
        onehot = sb("onehot", [P, TOP, GB, E])
        both = sb("both", [P, GB * E], BF16)
        run = sb("run", [P, E])
        rowid = sb("rowid", [P, GB, E])
        pick = sb("pick", [P, TOP * GB, E])
        slotf = sb("slotf", [P, TOP * GB])
        slot = sb("slot", [P, 2, TOP * GB], U32)
        mm = sb("mm", [P, 8])
        flagi = sb("flagi", [P, 1], I32)
        padrow = sb("padrow", [P, E], I32)
        tabs = sb("tabs", [P, 3, SLOTS])
        tabi = sb("tabi", [P, 2, SLOTS], I32)
        cnt = sb("cnt", [P, 5, E])
        cnti = sb("cnti", [P, 2, E], I32)
        yid = sb("yid", [P, 4], U32)
        carry = sb("carry", [P, 1])
        still = sb("still", [P, 6])
        pre = rawf[:, 3 * N:4 * N]
        wgT, waq, waT, a2, vraw = pre[:, 0:128], pre[:, 128:257], pre[:, 257:384], pre[:, 384:385], pre[:, 385:641]
        cmpb = sb("cmpb", [P, SLOTS, E])[:]
        pad = sb("pad", [P, E, ROW])[:]
        w1, w2 = rawf[:, 2 * N:3 * N], rawf[:, 3 * N:4 * N]
        sc_row, ex_row = (rawf[:, k * N:(k + 1) * N] for k in (1, 2))
        grp = rawf[:, 3 * N:3 * N + 5 * P].rearrange("p (a i) -> p a i", i=P)
        onesf, part_max, diag, row_max, h_sum = (grp[:, i, :] for i in range(5))
        gres = gb[:].bitcast(F32)[:, 0:N].rearrange("p (t d) -> p t d", d=D)
        xs = rawf[:, 0:8 * ROW].rearrange("p (s r) -> p s r", r=ROW)
        xsT = rawf[:, 2048:2048 + 4 * P].rearrange("p (s r) -> p s r", r=P)
        w1c = rawf[:, 2560:2560 + 4 * H].rearrange("p (s r) -> p s r", r=H)
        hT = rawf[:, 4608:4608 + 4 * H].rearrange("p (s r) -> p s r", r=H)
        b1c = rawf[:, 6656:6656 + 4 * HK].rearrange("p (s r) -> p s r", r=HK)
        ya = rawf[:, 7168:7168 + 2 * D].rearrange("p (s r) -> p s r", r=D)
        ys = rawf[:, 7424:7424 + 4 * D].rearrange("p (s r) -> p s r", r=D)
        yplane = [rawf[:, k * N:(k + 1) * N].rearrange("p (t d) -> p t d", d=D) for k in range(TOP)]
        spare = maskf[:, N:N + SPARE * ROW].rearrange("p (e r) -> p e r", r=ROW)

        ps = [ctx.enter_context(nc.psum_tensor(f"ps{i}", [P, 512], F32)) for i in range(8)]

        s_small = sem("small_weights_in")
        s_x = [sem(f"x_in{c}") for c in range(4)]
        s_xT = [sem(f"xT_in{c}") for c in range(4)]
        s_adj = [sem(f"adj_in{i}") for i in range(4)]
        s_gw = sem("gate_weights_in")
        s_w = sem("expert_weights_in")
        s_const = sem("constants")
        s_cdve = sem("centre_matrix")
        s_pc = sem("pool_steps")
        s_vs = sem("dve_steps")
        s_as = sem("act_steps")
        s_pw = sem("weight_products")
        s_pwc = sem("weight_products_copied")
        s_ft = sem("feature_products")
        s_fcd = sem("feature_rows_copied")
        s_fca = sem("feature_squares")
        s_va = sem("vectors_for_act")
        s_av = sem("vectors_from_act")
        s_al = sem("alpha_ready")
        s_u = sem("u_product")
        s_ub = sem("u_copied")
        s_hp = sem("hsum_product")
        s_mt = sem("extremes_ready")
        s_mb = sem("extremes_products")
        s_md = sem("extremes_taken")
        s_flag = sem("spread_known")
        s_wa = sem("wide_adj_in")
        s_wpm = sem("wide_partition_max")
        s_wt = sem("wide_max_turned")
        s_wd = sem("wide_max_diagonal")
        s_wm = sem("wide_max_spread")
        s_wx = sem("wide_exponents")
        s_we = sem("wide_exp_done")
        s_wp = sem("wide_weights")
        s_wo = sem("wide_sums")
        s_wr = sem("wide_rows_taken")
        s_wv = sem("wide_dve_steps")
        s_wu = sem("wide_identity")
        s_wuo = sem("wide_identity_out")
        s_ww = [sem(f"wide_window_in{k}") for k in range(GB)]
        s_gf = sem("g_rest")
        s_gc = sem("g_cast")
        s_g3 = sem("g_third_part")
        s_mask = sem("mask_ready")
        s_at = sem("attention_done")
        s_pf = sem("attention_taken")
        s_tk = sem("take_dve_steps")
        s_e1 = sem("elu_operand")
        s_e2 = sem("elu_exp")
        s_y1 = sem("emb_ready")
        s_y2 = sem("emb_squared")
        s_al2 = sem("log_scale_ready")
        s_sg2 = sem("sigmoid_squared")
        s_r = sem("log_vectors_for_act")
        s_ra = sem("log_vectors_from_act")
        s_rc = sem("exp_vectors_for_act")
        s_rca = sem("exp_vectors_from_act")
        s_var = sem("variance")
        s_varr = sem("deviation")
        s_x1 = sem("x1_ready")
        s_x2 = sem("x1_squared")
        s_ns = sem("norm_scale_ready")
        s_xl = sem("xl_ready")
        s_bas = sem("log_act_steps")
        s_bcs = sem("exp_act_steps")
        s_tt = sem("xl_turned")
        s_ttc = sem("xl_turned_copied")
        s_lg = sem("logits")
        s_dl = sem("gate_difference")
        s_de = sem("gate_exp")
        s_m = sem("choice_ready")
        s_pr = sem("prefix_ready")
        s_sl = sem("rows_addressed")
        s_sp = sem("dispatch_begun")
        s_yp = sem("return_begun")
        s_spare = sem("spare_rows_out")
        s_sc = [sem(f"rows_dispatched{i}") for i in range(2)]
        s_pd = sem("padding_rows_out")
        s_ea = sem("elu_dve_steps")
        s_eb = sem("log_dve_steps")
        s_ec = sem("exp_dve_steps")
        s_ch = sem("choice_dve_steps")
        s_plc = sem("place_dve_steps")
        s_tab = sem("tables_ready")
        s_pad = sem("padding_addressed")
        s_xsw = [sem(f"slot_rows_in{i}") for i in range(8)]
        s_T = sem("slot_turned")
        s_Tc = sem("slot_turned_copied")
        s_L1 = sem("layer1")
        s_wc = sem("tile_weights_fetched")
        s_ge = sem("gelu_done")
        s_L2 = sem("layer2")
        s_ya = sem("layer2_biased")
        s_ys = sem("result_weighted")
        s_yi = sem("result_place")
        s_yo = [sem(f"result_out{i}") for i in range(4)]
        s_pl = [sem(f"planes_in{c}") for c in range(4)]
        s_fs = sem("final_steps")
        s_fin = sem("final_sum")
        s_out = sem("out_stored")

        block = ctx.enter_context(nc.Block())

        @block.sync
        def _(sp):
            sp.dma_start(wgT[0:DC, :], wgT_in).then_inc(s_small, 16)
            sp.dma_start(waq[0:DC, 0:D], wa_in).then_inc(s_small, 16)
            sp.dma_start(waT[:, 0:DC], waT_in).then_inc(s_small, 16)
            sp.dma_start(a2, a2_in).then_inc(s_small, 16)
            sp.dma_start(vraw[:, 0:DC], wg_in).then_inc(s_small, 16)
            for c in range(4):
                sp.dma_start(x[:, CH * c:CH * c + CH, :], x_rows[:, CH * c:CH * c + CH, :]).then_inc(s_x[c], 16)
                sp.dma_start(xT[:, 1024 * c:1024 * (c + 1)], xT_in[:, 1024 * c:1024 * (c + 1)]).then_inc(s_xT[c], 16)
            for t in range(3):
                sp.dma_start(raw[:, t, :], adjT[t]).then_inc(s_adj[t], 16)
            sp.dma_start(gatew[:], gate_in).then_inc(s_gw, 16)
            sp.dma_start(bgb[:], bg_in.partition_broadcast(P)).then_inc(s_gw, 16)
            sp.dma_start(b1t[:], b1_in).then_inc(s_w, 16)
            sp.dma_start(b2b[:], b2_in.partition_broadcast(P)).then_inc(s_w, 16)
            sp.wait_ge(s_pwc, 3)
            sp.dma_start(raw[:, 3, :], adjT[3]).then_inc(s_adj[3], 16)
            def stream(tile):
                with sp.Fori(1, NB) as q:
                    for k in range(GB):
                        src = tile(GB * q + k)
                        sp.wait_ge(s_mask, GB * q - GB + k + 1)
                        sp.dma_start(raw[:, k, :], src).then_inc(s_adj[k], 16)

            def window(t):
                return unit[:, bass.ds(t * P, N)]

            sp.wait_ge(s_flag, 1)
            wide = sp.value_load(flagi[0:1, 0:1], min_val=0, max_val=1)
            with sp.If(wide > 0):
                for k in range(GB):
                    sp.wait_ge(s_adj[k], 16)
                sp.dma_start(raw[:, 0, :], adjT[0]).then_inc(s_wa, 16)
                with sp.Fori(1, NT) as t:
                    sp.wait_ge(s_wr, t)
                    sp.dma_start(raw[:, 0, :], adjT[bass.ds(t, 1)].rearrange("a p n -> (a p) n")).then_inc(s_wa, 16)
                sp.wait_ge(s_wu, 1)
                sp.dma_start(unit[:, 0:(NT - 1) * P], raw[:, 1, 0:(NT - 1) * P]).then_inc(s_wuo, 16)
                sp.dma_start(unit[:, NT * P:], raw[:, 1, 0:(NT - 1) * P]).then_inc(s_wuo, 16)
                sp.dma_start(unit[:, (NT - 1) * P:NT * P], raw[:, 2, 0:P]).then_inc(s_wuo, 16)
                sp.wait_ge(s_wuo, 48)
                for k in range(GB):
                    sp.dma_start(raw[:, k, :], unit[:, k * P:k * P + N]).then_inc(s_ww[k], 16)
                stream(window)
            with sp.Else():
                stream(lambda t: adjT[bass.ds(t, 1)].rearrange("a p n -> (a p) n"))
            sp.wait_ge(s_mask, NT - 1)
            sp.dma_start(w1, w1_in).then_inc(s_w, 16)
            sp.wait_ge(s_mask, NT)
            sp.dma_start(w2, w2_in).then_inc(s_w, 16)
            sp.wait_ge(s_pad, 1)
            for e in range(E):
                last = sp.value_load(padrow[0:1, e:e + 1], min_val=0, max_val=E * REGION - P)
                sp.dma_start(disp[bass.ds(last, P), :], pad[:, e, :]).then_inc(s_pd, 16)
            sp.wait_ge(s_spare, 16)
            sp.wait_ge(s_tab, 1)
            for i in range(2):
                sp.wait_ge(s_sc[i], 16 * TOP * GB * NB // 2)
            sp.wait_ge(s_pd, 16 * E)

            def load(s, j):
                rb = sp.value_load(tabi[0:1, 0, bass.ds(s, 1)], min_val=0, max_val=E * REGION + (SPARE - 1) * P)
                sp.dma_start(xs[:, j, :], disp[bass.ds(rb, P), :]).then_inc(s_xsw[j], 16)

            for s in range(8):
                load(s, s)
            with sp.Fori(1, SLOTS // 8) as o:
                for j in range(8):
                    s = 8 * o + j
                    sp.wait_ge(s_T, s - 7)
                    sp.wait_ge(s_ys, s - 7)
                    sp.wait_ge(s_yi, s - 7)
                    load(s, j)
            for j in range(4):
                sp.wait_ge(s_yo[j], 16 * (SLOTS // 4))
            for c in range(4):
                for k in range(TOP):
                    src = planes[k * N + c * 1024:k * N + (c + 1) * 1024, :].rearrange("(t p) d -> p t d", p=P)
                    sp.dma_start(yplane[k][:, CH * c:CH * c + CH, :], src).then_inc(s_pl[c], 16)
            for c in range(4):
                sp.wait_ge(s_fin, c + 1)
                dst = out[c * 1024:(c + 1) * 1024, :].rearrange("(t p) d -> p t d", p=P)
                sp.dma_start(dst, x[:, CH * c:CH * c + CH, :]).then_inc(s_out, 16)
            sp.wait_ge(s_out, 64)

        @block.gpsimd
        def _(pool):
            st = Steps(pool, s_pc)
            st.did(pool.memset(ident[:], 0.0))
            st.did(pool.memset(ones[:], 1.0))
            st.did(pool.memset(onesb[:], 1.0))
            st.did(pool.memset(nhalf[:], -HALF_LN_SCALE))
            st.did(pool.memset(hsum[:, D:G], float(N)))
            st.did(pool.memset(spare, 0.0))
            st.did(pool.memset(pad, 0.0))
            st.did(pool.iota(ia[:, 0:NT], pattern=[[P, NT]], base=0, channel_multiplier=1))
            st.settle()
            pool.affine_select(out=ident[:], in_=ident[:], compare_op=ALU.not_equal, fill=1.0,
                               base=0, pattern=[[-1, P]], channel_multiplier=1).then_inc(s_const, 1)
            st.did(pool.affine_select(out=ltri[:], in_=onesb[:], compare_op=ALU.is_gt, fill=0.0,
                                      base=0, pattern=[[1, P]], channel_multiplier=-1))
            st.did(pool.tensor_copy(tokid[:], ia[:, 0:NT]))
            st.settle()
            st.step(pool.iota(ia[:, 0:SLOTS], pattern=[[1, SLOTS]], base=0, channel_multiplier=0))
            st.did(pool.tensor_copy(slotno[:], ia[:, 0:SLOTS]))
            st.did(pool.tensor_copy(iota8[:], ia[:, 0:E]))
            st.settle()
            st.step(pool.iota(ia[:, 0:E], pattern=[[REGION, E]], base=0, channel_multiplier=0))
            st.did(pool.tensor_copy(region0[:], ia[:, 0:E]))
            st.did(pool.tensor_copy(run[:], ia[:, 0:E]))
            st.settle()
            st.step(pool.iota(ia[:, 0:SPARE], pattern=[[P, SPARE]], base=TOP * N + E * P, channel_multiplier=1))
            st.step(pool.tensor_copy(spare[:, :, D + 1], ia[:, 0:SPARE]))
            st.step(pool.iota(ia[:, 0:E], pattern=[[P, E]], base=TOP * N, channel_multiplier=1))
            pool.tensor_copy(pad[:, :, D + 1], ia[:, 0:E]).then_inc(s_const, 1)
            pool.wait_ge(s_const, 2)
            pool.dma_start(disp[E * REGION:, :].rearrange("(e p) r -> p e r", p=P), spare).then_inc(s_spare, 16)

            def pass_wait(i, done):
                pool.tensor_tensor(out=still[:, i:i + 1], in0=nhalf[:], in1=nhalf[:], op=ALU.add).then_inc(done, 1)

            with pool.Fori(0, NB // 2) as o:
                for par in range(2):
                    pool.wait_ge(s_sl, 2 * o + par + 1)
                    pass_wait(par, s_sp)
                    for c in range(TOP):
                        for k in range(GB):
                            i = c * GB + k
                            pool.indirect_dma_start(disp, bass.IndirectOffsetOnAxis(slot[:, par, i:i + 1], axis=0),
                                                    xrow[:, par, k, c, :], None).then_inc(s_sc[par], 16)
            with pool.Fori(0, SLOTS // 4) as o:
                for j in range(4):
                    s = 4 * o + j
                    pool.wait_ge(s_ys, s + 1)
                    pool.wait_ge(s_yi, s + 1)
                    pass_wait(2 + j, s_yp)
                    pool.indirect_dma_start(planes, bass.IndirectOffsetOnAxis(yid[:, j:j + 1], axis=0),
                                            ys[:, j, :], None).then_inc(s_yo[j], 16)

        @block.tensor
        def _(pe):
            mmul = pe.matmul
            pe.wait_ge(s_small, 80)
            mmul(ps[0][0:DC, 0:1], waT[:, 0:DC], a2, start=True, stop=True).then_inc(s_pw, 1)
            pe.wait_ge(s_pwc, 1)
            mmul(ps[0][:, 0:G], wgT[0:DC, :], waq[0:DC, :], start=True, stop=True).then_inc(s_pw, 1)
            pe.wait_ge(s_pwc, 2)
            pe.wait_ge(s_cdve, 1)
            mmul(ps[0][:, 0:256], center[:], vraw, start=True, stop=True).then_inc(s_pw, 1)
            pe.wait_ge(s_pwc, 3)
            for t in range(NT):
                if t % CH == 0:
                    pe.wait_ge(s_xT[t // CH], 16)
                if t >= 16:
                    pe.wait_ge(s_fcd, t // 2 - 7)
                    pe.wait_ge(s_fca, t // 2 * 2 - 14)
                mmul(ps[t // 2 % 8][:, t % 2 * 256:t % 2 * 256 + 256], xT[:, t * P:(t + 1) * P], vc[:],
                     start=True, stop=True).then_inc(s_ft, 1)
            pe.wait_ge(s_fcd, NT // 2)
            pe.wait_ge(s_fca, NT)
            pe.wait_ge(s_mt, 1)
            pe.transpose(ps[4][0:2, 0:P], mm[:, 0:2], ident[:]).then_inc(s_mb, 1)
            pe.wait_ge(s_md, 1)
            mmul(ps[4][:, 128:130], ones[:], mm[0:2, 4:6], start=True, stop=True).then_inc(s_mb, 1)
            pe.wait_ge(s_flag, 1)
            wide = pe.value_load(flagi[0:1, 0:1], min_val=0, max_val=1)
            with pe.If(wide > 0):
                pe.wait_ge(s_wp, 1)
                for t in range(NT):
                    m = mmul(ps[3][:, 0:G], onesf, h3[:, t, :], start=(t == 0), stop=(t == NT - 1))
                m.then_inc(s_wo, 1)
                with pe.Fori(0, NT) as t:
                    pe.wait_ge(s_wpm, t + 1)
                    pe.transpose(ps[0][:, 0:P], part_max, ident[:]).then_inc(s_wt, 1)
                    pe.wait_ge(s_wd, t + 1)
                    mmul(ps[1][:, 0:P], onesf, diag, start=True, stop=True).then_inc(s_wm, 1)
                    pe.wait_ge(s_wp, t + 2)
                    for j in range(NT):
                        m = mmul(ps[2][:, 0:G], ex_row[:, j * P:(j + 1) * P], h3[:, j, :], start=(j == 0), stop=(j == NT - 1))
                    m.then_inc(s_wo, 1)
            for t in range(NT):
                m = mmul(ps[5][0:1, 0:D], vec[:, 15, t:t + 1], x[:, t, :], start=(t == 0), stop=(t == NT - 1))
            m.then_inc(s_u, 1)

            def spread_u():
                pe.wait_ge(s_ub, 1)
                mmul(ps[5][:, 128:256], ty[0:1, 1, :], ones[0:1, :], start=True, stop=True).then_inc(s_hp, 1)

            def sum_h():
                pe.wait_ge(s_ub, 2)
                mmul(ps[5][:, 256:384], ty[:, 0, :], vc[:, DC:DC + D], start=True, stop=True).then_inc(s_hp, 1)

            def attend(b, k, first=False):
                n = GB * b + k
                pe.wait_ge(s_mask, n + 1)
                if not first:
                    pe.wait_ge(s_pf, n - GB + 1)
                for j in range(NT):
                    if first and k == 0 and j % CH == 0:
                        pe.wait_ge(s_g3, j // CH + 1)
                    m = mmul(ps[k][:, 0:3 * G], mask[:, k, j * P:(j + 1) * P],
                             g[:, j, :, :].rearrange("p a b -> p (a b)"), start=(j == 0), stop=(j == NT - 1))
                m.then_inc(s_at, 1)

            def turn(b, par):
                pe.wait_ge(s_xl, b + 1)
                for k in range(GB):
                    m = pe.transpose(ps[4][:, k * P:(k + 1) * P], xrow[:, par, k, 0, 0:D], ident[:])
                m.then_inc(s_tt, 1)

            def gate(b):
                pe.wait_ge(s_ttc, b + 1)
                for k in range(GB):
                    m = mmul(ps[5][:, k * E:(k + 1) * E], xlT[:, k * P:(k + 1) * P], gatew[:], start=True, stop=True)
                m.then_inc(s_lg, 1)

            def places(b):
                pe.wait_ge(s_m, b + 1)
                for k in range(GB):
                    for i in range(k + 1):
                        mmul(ps[6][:, k * E:(k + 1) * E], (ltri if i == k else onesb)[:], both[:, i * E:(i + 1) * E],
                             start=(i == 0), stop=(i == k))
                for i in range(GB):
                    m = mmul(ps[6][:, GB * E:GB * E + E], onesb[:], both[:, i * E:(i + 1) * E],
                             start=(i == 0), stop=(i == GB - 1))
                m.then_inc(s_pr, 1)

            def batch(b, par, route=True):
                if route:
                    turn(b - 3, 1 - par)
                attend(b, 0)
                if route:
                    gate(b - 3)
                attend(b, 1)
                attend(b, 2)
                if route:
                    places(b - 3)
                attend(b, 3)

            attend(0, 0, True)
            spread_u()
            attend(0, 1, True)
            sum_h()
            attend(0, 2, True)
            attend(0, 3, True)
            batch(1, 1, False)
            batch(2, 0, False)
            pe.wait_ge(s_gw, 32)
            pe.wait_ge(s_ub, 3)
            batch(3, 1)
            with pe.Fori(2, NB // 2) as o:
                for par in range(2):
                    batch(2 * o + par, par)
            for b in (NB - 3, NB - 2, NB - 1):
                turn(b, b % 2)
                gate(b)
                places(b)

            def turn_rows(s, j):
                pe.wait_ge(s_xsw[j], 2 * (s - j) + 16)
                if not (isinstance(s, int) and s < 2):
                    pe.wait_ge(s_Tc, s - 1)
                pe.transpose(ps[(4, 7)[j % 2]][:, 0:P], xs[:, j, 0:D], ident[:]).then_inc(s_T, 1)

            def layer1(s, j):
                pe.wait_ge(s_Tc, s + 1)
                pe.wait_ge(s_wc, s + 1)
                if not (isinstance(s, int) and s < 4):
                    pe.wait_ge(s_ge, s - 3)
                for k in range(HK):
                    m = mmul(ps[j % 4][:, k * P:(k + 1) * P], w1c[:, j % 4, k * P:(k + 1) * P], xsT[:, j % 4, :],
                             start=True, stop=True)
                m.then_inc(s_L1, 1)

            def layer2(s, j):
                pe.wait_ge(s_ge, s + 1)
                if not (isinstance(s, int) and s < 2):
                    pe.wait_ge(s_ya, s - 1)
                for k in range(HK):
                    m = mmul(ps[5 + j % 2][:, 0:D], hT[:, j % 4, k * P:(k + 1) * P],
                             w2c[:, j % 4, k * P:(k + 1) * P], start=(k == 0), stop=(k == HK - 1))
                m.then_inc(s_L2, 1)

            pe.wait_ge(s_w, 64)
            pe.wait_ge(s_tab, 1)
            for s in range(4):
                turn_rows(s, s)
            layer1(0, 0)
            layer1(1, 1)

            def slot_step(s, j):
                if not isinstance(s, int) or s + 4 < SLOTS:
                    turn_rows(s + 4, (j + 4) % 8)
                if not isinstance(s, int) or s + 2 < SLOTS:
                    layer1(s + 2, (j + 2) % 8)
                layer2(s, j)

            for s in range(8):
                slot_step(s, s)
            with pe.Fori(1, SLOTS // 8 - 1) as o:
                for j in range(8):
                    slot_step(8 * o + j, j)
            for j in range(8):
                slot_step(SLOTS - 8 + j, j)

        @block.scalar
        def _(act):
            act.preload_act_table_set("natural_log_exp_and_others")
            st = Steps(act, s_as)
            if True:
                for t in range(NT):
                    act.wait_ge(s_fcd, t // 2 + 1)
                    if t >= 4:
                        act.wait_ge(s_fca, t - 3)
                    act.activation(sqj[:, t % 4, 0:DC], ps[t // 2 % 8][:, t % 2 * 256:t % 2 * 256 + DC], ACT.Square,
                                   accum_out=vec[:, 19, t:t + 1]).then_inc(s_fca, 1)

            def root(o, v):
                return ((o, v, ACT.Ln, dict(scale=LN_SCALE)), (o, o, ACT.Exp, dict(scale=0.5, bias=nhalf[:])))

            def functions(st, ready, n, done, *ops):
                act.wait_ge(ready, n)
                for i, (o, a, f, kw) in enumerate(ops):
                    ins = act.activation(o, a, f, **kw)
                    if i < len(ops) - 1:
                        st.step(ins)
                    else:
                        ins.then_inc(done, 1)

            functions(st, s_va, 1, s_av, *root(vec[:, 3:6, :], vec[:, 0:3, :]))
            functions(st, s_va, 2, s_av, *root(vec[:, 7, :], vec[:, 6, :]))
            functions(st, s_va, 3, s_av, (vec[:, 8, :], vec[:, 8, :], ACT.Ln, {}))
            functions(st, s_va, 4, s_av, (vec[:, 20, :], vec[:, 9, :], ACT.Exp, {}))
            functions(st, s_va, 5, s_av, (vec[:, 14, :], vec[:, 14, :], ACT.Ln, {}))
            functions(st, s_va, 6, s_av, (vec[:, 23, :], vec[:, 22, :], ACT.Exp, dict(bias=mm[:, 6:7])))
            act.wait_ge(s_flag, 1)
            wide = act.value_load(flagi[0:1, 0:1], min_val=0, max_val=1)
            with act.If(wide > 0):
                with act.Fori(0, NT) as t:
                    act.wait_ge(s_wx, t + 1)
                    act.activation(ex_row, sc_row, ACT.Exp).then_inc(s_we, 1)
            for n, (p, c) in enumerate(CASTS):
                act.wait_ge(s_gf, n + 1)
                act.activation(g[:, CH * c:CH * c + CH, p, :], h3[:, CH * c:CH * c + CH, :], ACT.Copy).then_inc(s_gc, 1)

            def copy_turned(b):
                act.wait_ge(s_tt, b + 1)
                act.activation(xlT[:], ps[4][:], ACT.Copy).then_inc(s_ttc, 1)

            def gate_exp(b):
                act.wait_ge(s_dl, b + 1)
                act.activation(bv[:, 24, :], bv[:, 23, :], ACT.Exp).then_inc(s_de, 1)

            def elu_exp(b, par, st):
                act.wait_ge(s_e1, b + 1)
                for k in range(GB):
                    st.did(act.activation(ta[:, k, :], tk[:, k, 0:D], ACT.Copy, scale=bv[:, 28, k:k + 1]))
                st.settle()
                st.step(act.activation(ty[:], ta[:], ACT.Relu, scale=-1.0))
                act.activation(te[:, par], ty[:], ACT.Exp, scale=-1.0)
                act.activation(ta[:], ta[:], ACT.Relu).then_inc(s_e2, 1)

            def square_y(b):
                act.wait_ge(s_y1, b + 1)
                for k in range(GB):
                    m = act.activation(sqj[:, k, 0:DC], ty[:, k, 1:D], ACT.Square, accum_out=bv[:, 0, k:k + 1])
                m.then_inc(s_y2, 1)

            def sigmoid(b, par, st):
                act.preload_act_table_set("sigmoid_and_others")
                act.wait_ge(s_al2, b + 1)
                for k in range(GB):
                    st.did(act.activation(te[:, par, k, :], ty[:, k, :], ACT.Sigmoid, scale=bv[:, 8, k:k + 1]))
                st.settle()
                for k in range(GB):
                    m = act.activation(junk[:, 1, k, 0:DC], te[:, par, k, 1:D], ACT.Square, accum_out=bv[:, 9, k:k + 1])
                m.then_inc(s_sg2, 1)
                act.preload_act_table_set("natural_log_exp_and_others")

            def square_x1(b, par, st):
                act.wait_ge(s_x1, b + 1)
                for k in range(GB):
                    st.did(act.activation(x[:, bass.ds(GB * b + k, 1), :], x1[:, par, k:k + 1, :], ACT.Copy,
                                          accum_out=bv[:, 18, k:k + 1]))
                st.settle()
                st.step(act.activation(bv[:, 17, :], bv[:, 18, :], ACT.Copy, scale=-1.0 / D))
                for k in range(GB):
                    m = act.activation(junk[:, 0, k, :], x1[:, par, k, :], ACT.Square, bias=bv[:, 17, k:k + 1],
                                       accum_out=bv[:, 18, k:k + 1])
                m.then_inc(s_x2, 1)

            def normalise(b, par):
                act.wait_ge(s_ns, b + 1)
                for k in range(GB):
                    m = act.activation(xrow[:, par, k, :, 0:D], x1[:, par, k:k + 1, :].to_broadcast([P, TOP, D]),
                                       ACT.Identity, scale=bv[:, 21, k:k + 1], bias=bv[:, 22, k:k + 1])
                m.then_inc(s_xl, 1)

            BAS, BCS = 10, 7

            def log_steps(b):
                return Steps(act, s_bas, BAS * b)

            def exp_steps(b):
                return Steps(act, s_bcs, BCS * b)

            def log_roots(b, st):
                functions(st, s_r, 2 * b + 1, s_ra, *root(bv[:, 4:7, :], bv[:, 1:4, :]))

            def log_theta(b):
                functions(None, s_r, 2 * b + 2, s_ra, (bv[:, 7, :], bv[:, 7, :], ACT.Ln, {}))

            def exp_norm(b, st):
                functions(st, s_rc, 2 * b + 1, s_rca, *root(bv[:, 11, :], bv[:, 10, :]))
                functions(st, s_rc, 2 * b + 2, s_rca, (bv[:, 12, :], bv[:, 11, :], ACT.Exp, {}))

            def deviation(b, st):
                functions(st, s_var, b + 1, s_varr, *root(bv[:, 20, :], bv[:, 19, :]))

            def batch(b, par, exp=True, route=True):
                lst, est = log_steps(b - 1), exp_steps(b - 2)
                if exp:
                    exp_norm(b - 2, est)
                if route:
                    copy_turned(b - 3)
                elu_exp(b - 1, 1 - par, lst)
                if exp:
                    square_x1(b - 2, par, est)
                square_y(b - 1)
                if route:
                    gate_exp(b - 3)
                log_roots(b - 1, lst)
                if exp:
                    deviation(b - 2, est)
                log_theta(b - 1)
                if exp:
                    normalise(b - 2, par)
                    assert est.n == BCS, est.n
                sigmoid(b - 1, 1 - par, lst)
                assert lst.n == BAS, lst.n

            batch(1, 1, exp=False, route=False)
            batch(2, 0, route=False)
            batch(3, 1)
            with act.Fori(2, NB // 2) as o:
                for par in range(2):
                    batch(2 * o + par, par)
            l, m, r = NB - 1, NB - 2, NB - 3
            lst, est, mst = log_steps(l), exp_steps(l), exp_steps(m)
            exp_norm(m, mst)
            copy_turned(r)
            elu_exp(l, l % 2, lst)
            gate_exp(r)
            square_y(l)
            log_roots(l, lst)
            log_theta(l)
            square_x1(m, m % 2, mst)
            deviation(m, mst)
            sigmoid(l, l % 2, lst)
            exp_norm(l, est)
            normalise(m, m % 2)
            square_x1(l, l % 2, est)
            deviation(l, est)
            gate_exp(m)
            normalise(l, l % 2)
            gate_exp(l)

            act.preload_act_table(ACT.Gelu)

            def gelu(s, j):
                act.wait_ge(s_L1, s + 1)
                if not (isinstance(s, int) and s < 4):
                    act.wait_ge(s_L2, s - 3)
                for k in range(HK):
                    m = act.activation(hT[:, j % 4, k * P:(k + 1) * P], ps[j % 4][:, k * P:(k + 1) * P], ACT.Gelu,
                                       bias=b1c[:, j % 4, k:k + 1])
                m.then_inc(s_ge, 1)

            def weigh(s, j):
                act.wait_ge(s_ya, s + 1)
                if not (isinstance(s, int) and s < 4):
                    act.wait_ge(s_yp, s - 3)
                    act.wait_ge(s_yo[j % 4], 4 * (s - j % 4))
                act.activation(ys[:, j % 4, :], ya[:, j % 2, :], ACT.Copy, scale=xs[:, j, D:D + 1]).then_inc(s_ys, 1)

            gelu(0, 0)
            gelu(1, 1)

            def slot_step(s, j):
                if not isinstance(s, int) or s + 2 < SLOTS:
                    gelu(s + 2, (j + 2) % 8)
                weigh(s, j)

            for j in range(8):
                slot_step(j, j)
            with act.Fori(1, SLOTS // 8 - 1) as o:
                for j in range(8):
                    slot_step(8 * o + j, j)
            for j in range(8):
                slot_step(SLOTS - 8 + j, j)

        @block.vector
        def _(v):
            st = Steps(v, s_vs)
            TT, TS, STT = v.tensor_tensor, v.tensor_scalar, v.scalar_tensor_tensor

            def newton(st, u, val, tmp):
                st.step(v.reciprocal(tmp, u))
                st.step(STT(out=tmp, in0=val, scalar=0.5, in1=tmp, op0=ALU.mult, op1=ALU.mult))
                st.step(STT(out=u, in0=u, scalar=0.5, in1=tmp, op0=ALU.mult, op1=ALU.add))

            v.wait_ge(s_const, 1)
            TS(center[:], ident[:], -1.0 / D, None, ALU.add).then_inc(s_cdve, 1)
            v.wait_ge(s_pw, 1)
            v.tensor_copy(waq[0:DC, D:G], ps[0][0:DC, 0:1]).then_inc(s_pwc, 1)
            v.wait_ge(s_pw, 2)
            v.tensor_copy(vraw[:, DC:256], ps[0][:, 0:G]).then_inc(s_pwc, 1)
            v.wait_ge(s_pw, 3)
            v.tensor_copy(vc[:], ps[0][:, 0:256]).then_inc(s_pwc, 1)

            def take_features(i):
                v.wait_ge(s_ft, 2 * i + 2)
                v.tensor_copy(h3[:, 2 * i:2 * i + 2, :],
                              ps[i % 8][:].rearrange("p (a c) -> p a c", a=2)[:, :, DC:256]).then_inc(s_fcd, 1)

            EV, OD = D // 2, DC - D // 2
            for c in range(4):
                v.wait_ge(s_x[c], 16)
                for i in range(CH // 2):
                    for t in (CH * c + 2 * i, CH * c + 2 * i + 1):
                        st.did(v.bn_stats(bn[:, t, :], x[:, t, 1:D]))
                    if c < 3:
                        take_features(4 * c + i)
            st.settle()
            mean_e, m2_e, mean_o, m2_o = (bn[:, :, i] for i in (1, 2, 4, 5))
            st.did(TT(vec[:, 16, :], mean_e, mean_o, ALU.subtract))
            st.step(TT(vec[:, 18, :], m2_e, m2_o, ALU.add))
            st.did(STT(out=vec[:, 20, :], in0=vec[:, 16, :], scalar=EV * OD / DC, in1=vec[:, 16, :], op0=ALU.mult, op1=ALU.mult))
            st.step(STT(out=vec[:, 21, :], in0=vec[:, 16, :], scalar=EV / DC, in1=mean_o, op0=ALU.mult, op1=ALU.add))
            st.did(TT(vec[:, 18, :], vec[:, 18, :], vec[:, 20, :], ALU.add))
            st.step(TT(vec[:, 16, :], x[:, :, 0], vec[:, 21, :], ALU.subtract))
            st.did(TS(vec[:, 17, :], vec[:, 16, :], DC / D, None, ALU.mult))
            st.step(STT(out=vec[:, 21, :], in0=vec[:, 16, :], scalar=DC / D ** 2, in1=vec[:, 16, :], op0=ALU.mult, op1=ALU.mult))
            st.did(TT(vec[:, 18, :], vec[:, 18, :], vec[:, 21, :], ALU.add))
            st.step(TT(vec[:, 20, :], vec[:, 17, :], vec[:, 17, :], ALU.mult))
            st.step(TT(vec[:, 20, :], vec[:, 20, :], vec[:, 18, :], ALU.add))
            for i in range(12, 16):
                take_features(i)
            v.wait_ge(s_fca, NT)
            st.did(TS(vec[:, 0, :], vec[:, 20, :], 1.0 / D, LN_EPS, ALU.mult, ALU.add))
            st.did(TS(vec[:, 1, :], vec[:, 18, :], NORM2_MIN, None, ALU.max))
            st.settle()
            TS(vec[:, 2, :], vec[:, 19, :], NORM2_MIN, None, ALU.max).then_inc(s_va, 1)
            v.wait_ge(s_va, 1)
            v.wait_ge(s_av, 1)
            newton(st, vec[:, 3:6, :], vec[:, 0:3, :], vt[:])
            st.step(v.reciprocal(vec[:, 26, :], vec[:, 3:5, :][:, 0, :]))
            st.step(TT(vec[:, 24, :], vec[:, 17, :], vec[:, 26, :], ALU.mult))
            st.step(TS(vec[:, 24, :], vec[:, 24, :], THETA_MIN, None, ALU.max))
            st.step(TS(vec[:, 6, :], vec[:, 24, :], 1.0, None, ALU.add))
            STT(out=vec[:, 6, :], in0=vec[:, 24, :], scalar=-1.0, in1=vec[:, 6, :],
                op0=ALU.add, op1=ALU.mult).then_inc(s_va, 1)
            v.wait_ge(s_va, 2)
            v.wait_ge(s_av, 2)
            newton(st, vec[:, 7, :], vec[:, 6, :], vt[:, 0, :])
            TT(vec[:, 8, :], vec[:, 24, :], vec[:, 7, :], ALU.add).then_inc(s_va, 1)
            st.step(v.reciprocal(vec[:, 26, :], vec[:, 4, :]))
            v.wait_ge(s_av, 3)
            st.step(TT(vec[:, 15, :], vec[:, 8, :], vec[:, 26, :], ALU.mult))
            TT(vec[:, 9, :], vec[:, 15, :], vec[:, 5, :], ALU.mult).then_inc(s_va, 1)
            v.wait_ge(s_va, 4)
            v.wait_ge(s_av, 4)
            st.step(v.reciprocal(vec[:, 21, :], vec[:, 20, :]))
            st.did(TT(vec[:, 12, :], vec[:, 20, :], vec[:, 21, :], ALU.subtract))
            st.step(TT(vec[:, 13, :], vec[:, 20, :], vec[:, 21, :], ALU.add))
            st.did(TS(vec[:, 12, :], vec[:, 12, :], 0.5, ROOT_CL, ALU.mult, ALU.max))
            st.step(TS(vec[:, 13, :], vec[:, 13, :], 0.5, THETA_MIN, ALU.mult, ALU.max))
            TT(vec[:, 14, :], vec[:, 12, :], vec[:, 13, :], ALU.add).then_inc(s_va, 1)
            st.step(TS(vec[:, 25, :], vec[:, 9, :], 1e-15, None, ALU.max))
            st.step(v.reciprocal(vec[:, 25, :], vec[:, 25, :]))
            v.wait_ge(s_av, 5)
            st.step(TT(vec[:, 25, :], vec[:, 14, :], vec[:, 25, :], ALU.mult))
            TT(vec[:, 15, :], vec[:, 15, :], vec[:, 25, :], ALU.mult).then_inc(s_al, 1)
            v.wait_ge(s_al, 1)
            st.step(TT(vec[:, 22, :], h3[:, :, D], vec[:, 15, :], ALU.mult))
            st.did(v.reduce_max(mm[:, 0:1], vec[:, 22, :], AX_X))
            st.step(TS(vec[:, 21, :], vec[:, 22, :], -1.0, None, ALU.mult))
            v.reduce_max(mm[:, 1:2], vec[:, 21, :], AX_X).then_inc(s_mt, 1)
            v.wait_ge(s_mb, 1)
            st.step(v.reduce_max(mm[0:2, 2:3], ps[4][0:2, 0:P], AX_X))
            TS(mm[0:2, 4:6], ident[0:2, 0:2], mm[0:2, 2:3], None, ALU.mult).then_inc(s_md, 1)
            v.wait_ge(s_mb, 2)
            TS(mm[:, 6:7], ps[4][:, 128:129], -1.0, None, ALU.mult).then_inc(s_va, 1)
            st.step(v.tensor_copy(mm[:, 7:8], ps[4][:, 129:130]))
            st.step(TT(mm[:, 7:8], mm[:, 7:8], mm[:, 6:7], ALU.subtract))
            TS(flagi[:], mm[:, 7:8], SPREAD_MAX, None, ALU.is_gt).then_inc(s_flag, 1)

            def make_mask(b, k, half, first=False):
                if half == 0:
                    v.wait_ge(s_adj[k], 16 * b + 16)
                    if not first:
                        v.wait_ge(s_at, GB * b + k - GB + 1)
                    elif k == 2:
                        v.wait_ge(s_spare, 16)
                cols = slice(half * N // 2, (half + 1) * N // 2)
                ins = TS(mask[:, k, cols], raw[:, k, cols], 0, None, ALU.is_gt)
                if half == 1:
                    ins.then_inc(s_mask, 1)

            v.wait_ge(s_av, 6)
            st.step(TT(vec[:, 24, :], vec[:, 15, :], vec[:, 23, :], ALU.mult))

            def wide_softmax():
                st = Steps(v, s_wv)
                alpha = vec[:, 15, :].unsqueeze(2).to_broadcast([P, NT, D])
                st.did(TT(h3[:, :, 0:D], h3[:, :, 0:D], alpha, ALU.mult))
                st.step(v.tensor_scalar(vec[:, 22, :], vec[:, 22, :], ps[4][:, 129:130], 1.0, ALU.add, ALU.add))
                st.did(TS(h3[:, :, D], vec[:, 15, :], 0.0, 1.0, ALU.mult, ALU.add))
                for k in range(GB):
                    v.wait_ge(s_adj[k], 16)
                st.step(TS(onesf, ident[:], 0.0, 1.0, ALU.mult, ALU.add))
                v.tensor_copy(mm[:, 7:8], mm[:, 6:7]).then_inc(s_wp, 1)
                v.wait_ge(s_wo, 1)
                st.step(v.tensor_copy(tk[:, 0, :], ps[3][:, 0:G]))
                loop = Steps(v, s_wv, st.n)
                logits = vec[:, 22, :].unsqueeze(2).to_broadcast([P, NT, P])
                scores = sc_row.rearrange("p (j i) -> p j i", i=P)
                with v.Fori(0, NT) as t:
                    loop = Steps(v, s_wv, st.n + WIDE * t)
                    v.wait_ge(s_wa, 16 * t + 16)
                    loop.step(TS(sc_row, raw[:, 0, :], 0, None, ALU.is_gt))
                    loop.step(TT(scores, scores, logits, ALU.mult))
                    v.reduce_max(part_max, sc_row.rearrange("p (j i) -> p i j", i=P), AX_X).then_inc(s_wpm, 1)
                    v.wait_ge(s_wt, t + 1)
                    loop.step(v.reduce_max(ta[:, 0, 0:1], ps[0][:, 0:P], AX_X))
                    TS(diag, ident[:], ta[:, 0, 0:1], None, ALU.mult).then_inc(s_wd, 1)
                    v.wait_ge(s_wm, t + 1)
                    loop.step(v.tensor_copy(row_max, ps[1][:, 0:P]))
                    loop.step(TT(scores, scores, row_max.unsqueeze(1).to_broadcast([P, NT, P]), ALU.subtract))
                    TS(sc_row, sc_row, 0.0, None, ALU.min).then_inc(s_wx, 1)
                    v.wait_ge(s_we, t + 1)
                    loop.step(TS(sc_row, raw[:, 0, :], 0, None, ALU.is_gt))
                    TT(ex_row, ex_row, sc_row, ALU.mult).then_inc(s_wp, 1)
                    v.wait_ge(s_wo, t + 2)
                    loop.step(v.tensor_copy(tk[:, 1, :], ps[2][:, 0:G]))
                    loop.step(TS(ta[:, 0, 1:2], tk[:, 1, D:G], 0.0, None, ALU.is_equal))
                    loop.step(STT(out=tk[:, 1, :], in0=tk[:, 0, :], scalar=ta[:, 0, 1:2], in1=tk[:, 1, :],
                                  op0=ALU.mult, op1=ALU.add))
                    loop.step(v.reciprocal(ta[:, 0, 2:3], tk[:, 1, D:G]))
                    TS(gres[:, bass.ds(t, 1), :], tk[:, 1:2, 0:D], ta[:, 0, 2:3], None, ALU.mult).then_inc(s_wr, 1)
                    assert loop.n <= WIDE
                v.wait_ge(s_wr, NT)
                end = Steps(v, s_wv, st.n + WIDE * NT)
                with v.Fori(0, NT) as t:
                    TS(h3[:, bass.ds(NT - 1 - t, 1), 0:D], gres[:, bass.ds(t, 1), :], 1.0, None, ALU.mult).then_inc(s_wv, 1)
                end.n += NT
                for i in (23, 24):
                    end.did(TS(vec[:, i, :], vec[:, i, :], 0.0, 1.0, ALU.mult, ALU.add))
                end.did(TS(raw[:, 1, :], raw[:, 0, :], 0, None, ALU.mult))
                v.tensor_copy(raw[:, 2, 0:P], ident[:]).then_inc(s_wu, 1)
                end.settle()
                for k in range(GB):
                    v.wait_ge(s_ww[k], 16)

            WIDE = 10
            wide = v.value_load(flagi[0:1, 0:1], min_val=0, max_val=1)
            with v.If(wide > 0):
                wide_softmax()
            make_mask(0, 0, 0, True)
            make_mask(0, 0, 1, True)
            for n, (p, c) in enumerate(PARTS):
                cs = slice(CH * c, CH * c + CH)
                if p == 0:
                    st.step(TT(h3[:, cs, 0:D], h3[:, cs, 0:D], vec[:, 24, cs].unsqueeze(2).to_broadcast([P, CH, D]), ALU.mult))
                    v.tensor_copy(h3[:, cs, D], vec[:, 23, cs]).then_inc(s_gf, 1)
                else:
                    v.wait_ge(s_gc, CASTS.index((p - 1, c)) + 1)
                    if p == 1:
                        TT(h3[:, cs, :], h3[:, cs, :], g[:, cs, 0, :], ALU.subtract).then_inc(s_gf, 1)
                    else:
                        TT(g[:, cs, 2, :], h3[:, cs, :], g[:, cs, 1, :], ALU.subtract).then_inc(s_g3, 1)
            v.wait_ge(s_u, 1)
            v.tensor_copy(ty[0:1, 1, :], ps[5][0:1, 0:D]).then_inc(s_ub, 1)

            def take(b, k):
                if k == 0 and not (isinstance(b, int) and b == 0):
                    v.wait_ge(s_e2, b)
                v.wait_ge(s_at, GB * b + k + 1)
                v.reduce_sum(tk[:, k, :], ps[k][:, 0:3 * G].rearrange("p (a g) -> p g a", g=G), AX_X).then_inc(s_pf, 1)

            def divide(b, st):
                v.wait_ge(s_pf, GB * b + GB)
                st.step(TS(alone[:], tk[:, :, D:G], 0.0, None, ALU.is_equal))
                TS(carry[:], nhalf[:], 0.0, None, ALU.add)
                st.step(v.copy_predicated(tk[:], alone[:].to_broadcast([P, GB, G]),
                                          hsum[:].unsqueeze(1).to_broadcast([P, GB, G])))
                v.reciprocal(bv[:, 28, :], tk[:, :, D]).then_inc(s_e1, 1)

            def elu(b, par):
                v.wait_ge(s_e2, b + 1)
                STT(out=ty[:], in0=te[:, par], scalar=-1.0, in1=ta[:], op0=ALU.add, op1=ALU.add).then_inc(s_y1, 1)

            def log_bounds(b, st):
                v.wait_ge(s_y2, b + 1)
                st.did(TS(bv[:, 1, :], bv[:, 0, :], NORM2_MIN, None, ALU.max))
                st.step(TS(bv[:, 2, :], bv[:, 0, :], CL, None, ALU.max))
                TS(bv[:, 3, :], bv[:, 2, :], 1.0, None, ALU.add).then_inc(s_r, 1)

            def log_roots(b, st):
                v.wait_ge(s_r, 2 * b + 1)
                v.wait_ge(s_ra, 2 * b + 1)
                newton(st, bv[:, 4:7, :], bv[:, 1:4, :], bt[:, 0:3, :])
                TT(bv[:, 7, :], bv[:, 5, :], bv[:, 6, :], ALU.add).then_inc(s_r, 1)
                st.step(v.reciprocal(bv[:, 26, :], bv[:, 4, :]))

            def log_scale(b):
                v.wait_ge(s_ra, 2 * b + 2)
                TT(bv[:, 8, :], bv[:, 7, :], bv[:, 26, :], ALU.mult).then_inc(s_al2, 1)

            def exp_bound(b):
                v.wait_ge(s_sg2, b + 1)
                TS(bv[:, 10, :], bv[:, 9, :], NORM2_MIN, None, ALU.max).then_inc(s_rc, 1)

            def exp_root(b, st):
                v.wait_ge(s_rc, 2 * b + 1)
                v.wait_ge(s_rca, 2 * b + 1)
                st.step(v.reciprocal(bt[:, 3, :], bv[:, 11, :]))
                st.step(STT(out=bt[:, 3, :], in0=bv[:, 10, :], scalar=0.5, in1=bt[:, 3, :], op0=ALU.mult, op1=ALU.mult))
                STT(out=bv[:, 11, :], in0=bv[:, 11, :], scalar=0.5, in1=bt[:, 3, :], op0=ALU.mult, op1=ALU.add).then_inc(s_rc, 1)
                v.wait_ge(s_rc, 2 * b + 2)
                st.step(v.reciprocal(bv[:, 15, :], bv[:, 11, :]))

            def residual(b, par, st):
                v.wait_ge(s_rca, 2 * b + 2)
                st.step(v.reciprocal(bv[:, 13, :], bv[:, 12, :]))
                st.step(TT(bv[:, 16, :], bv[:, 12, :], bv[:, 13, :], ALU.subtract))
                st.did(TT(bv[:, 14, :], bv[:, 12, :], bv[:, 13, :], ALU.add))
                st.step(STT(out=bv[:, 15, :], in0=bv[:, 16, :], scalar=0.5, in1=bv[:, 15, :], op0=ALU.mult, op1=ALU.mult))
                if not (isinstance(b, int) and b < 2):
                    v.wait_ge(s_xl, b - 1)
                for k in range(GB):
                    st.did(STT(out=x1[:, par, k:k + 1, 1:D], in0=te[:, par, k:k + 1, 1:D], scalar=bv[:, 15, k:k + 1],
                               in1=x[:, bass.ds(GB * b + k, 1), 1:D], op0=ALU.mult, op1=ALU.add))
                first = x[:, bass.ds(GB * b, GB), 0:1].rearrange("p t a -> p (t a)")
                STT(out=x1[:, par, :, 0], in0=bv[:, 14, :], scalar=0.5, in1=first, op0=ALU.mult, op1=ALU.add).then_inc(s_x1, 1)

            def variance(b):
                v.wait_ge(s_x2, b + 1)
                TS(bv[:, 19, :], bv[:, 18, :], 1.0 / D, LN_EPS, ALU.mult, ALU.add).then_inc(s_var, 1)

            def norm_scale(b, par, st):
                v.wait_ge(s_var, b + 1)
                v.wait_ge(s_varr, b + 1)
                newton(st, bv[:, 20, :], bv[:, 19, :], bt[:, 3, :])
                st.step(v.reciprocal(bv[:, 21, :], bv[:, 20, :]))
                if not (isinstance(b, int) and b < 2):
                    v.wait_ge(s_sc[par], 8 * TOP * GB * (b - par))
                TT(bv[:, 22, :], bv[:, 17, :], bv[:, 21, :], ALU.mult).then_inc(s_ns, 1)

            def copy_turned(b):
                v.wait_ge(s_tt, b + 1)
                v.tensor_copy(xlT[:], ps[4][:]).then_inc(s_ttc, 1)

            def choice1(b, par, st):
                v.wait_ge(s_lg, b + 1)
                st.did(TT(lg[:], ps[5][:, 0:GB * E].rearrange("p (k e) -> p k e", e=E),
                           bgb[:].unsqueeze(1).to_broadcast([P, GB, E]), ALU.add))
                st.settle()
                st.did(TS(xrow[:, par, :, 0, D + 1], tokid[:, bass.ds(GB * b, GB)], 0.0, None, ALU.add))
                for k in range(GB):
                    st.did(v.max(top[:, k, :], lg[:, k, :]))
                st.settle()
                st.did(TS(xrow[:, par, :, 1, D + 1], tokid[:, bass.ds(GB * b, GB)], float(N), None, ALU.add))
                for k in range(GB):
                    st.did(v.max_index(idx[:, k, :], top[:, k, :], lg[:, k, :]))
                TT(bv[:, 23, :], top[:, :, 1], top[:, :, 0], ALU.subtract).then_inc(s_dl, 1)

            def choice2(b, par, st):
                st.settle()
                st.step(v.tensor_copy(idxf[:], idx[:, :, 0:TOP].rearrange("p k c -> p c k")))
                st.did(TT(onehot[:].rearrange("p c k e -> p (c k) e"), iota8[:].unsqueeze(1).to_broadcast([P, TOP * GB, E]),
                          idxf[:].rearrange("p c k -> p (c k)").unsqueeze(2).to_broadcast([P, TOP * GB, E]), ALU.is_equal))
                st.settle()
                TT(both[:].rearrange("p (k e) -> p k e", e=E), onehot[:, 0], onehot[:, 1], ALU.add).then_inc(s_m, 1)
                v.wait_ge(s_de, b + 1)
                st.step(TS(bv[:, 23, :], bv[:, 24, :], 1.0, None, ALU.add))
                st.step(v.reciprocal(bv[:, 25, :], bv[:, 23, :]))
                st.did(v.tensor_copy(xrow[:, par, :, 0, D], bv[:, 25, :]))
                st.did(TT(xrow[:, par, :, 1, D], bv[:, 24, :], bv[:, 25, :], ALU.mult))

            def place(b, par, st):
                v.wait_ge(s_pr, b + 1)
                st.step(TT(rowid[:], ps[6][:, 0:GB * E].rearrange("p (k e) -> p k e", e=E),
                           run[:].unsqueeze(1).to_broadcast([P, GB, E]), ALU.add))
                st.did(TT(run[:], run[:], ps[6][:, GB * E:GB * E + E], ALU.add))
                st.step(TT(pick[:].rearrange("p (c k) e -> p c (k e)", c=TOP), onehot[:].rearrange("p c k e -> p c (k e)"),
                           rowid[:].rearrange("p k e -> p (k e)").unsqueeze(1).to_broadcast([P, TOP, GB * E]), ALU.mult))
                st.step(v.reduce_sum(slotf[:], pick[:], AX_X))
                if not (isinstance(b, int) and b < 2):
                    v.wait_ge(s_sp, b - 1)
                    v.wait_ge(s_sc[par], 8 * TOP * GB * (b - par))
                v.tensor_copy(slot[:, par], slotf[:]).then_inc(s_sl, 1)

            EA, EB, EC, CHO, PL = 2, 6, 15, 17, 4
            def elu_steps(b):
                return Steps(v, s_ea, EA * b)

            def log_steps(b):
                return Steps(v, s_eb, EB * b)

            def exp_steps(b):
                return Steps(v, s_ec, EC * b)

            def choice_steps(b):
                return Steps(v, s_ch, CHO * b)

            def place_steps(b):
                return Steps(v, s_plc, PL * b)

            def batch(b, par, exp=True, route=True):
                lst, est, cst = log_steps(b - 1), exp_steps(b - 2), choice_steps(b - 3)
                make_mask(b, 0, 0)
                if exp:
                    exp_bound(b - 2)
                take(b - 1, 2)
                make_mask(b, 0, 1)
                if exp:
                    exp_root(b - 2, est)
                take(b - 1, 3)
                divide(b - 1, elu_steps(b - 1))
                make_mask(b, 1, 0)
                make_mask(b, 1, 1)
                if exp:
                    residual(b - 2, par, est)
                elu(b - 1, 1 - par)
                make_mask(b, 2, 0)
                make_mask(b, 2, 1)
                if route:
                    choice1(b - 3, 1 - par, cst)
                if exp:
                    variance(b - 2)
                log_bounds(b - 1, lst)
                if route:
                    choice2(b - 3, 1 - par, cst)
                if exp:
                    norm_scale(b - 2, par, est)
                take(b, 0)
                log_roots(b - 1, lst)
                make_mask(b, 3, 0)
                log_scale(b - 1)
                make_mask(b, 3, 1)
                take(b, 1)
                if route:
                    place(b - 3, 1 - par, place_steps(b - 3))
                assert lst.n == EB and (not exp or est.n == EC) and (not route or cst.n == CHO)

            for k in range(1, GB):
                make_mask(0, k, 0, True)
                make_mask(0, k, 1, True)
            take(0, 0)
            v.wait_ge(s_hp, 1)
            v.tensor_copy(ty[:, 0, :], ps[5][:, 128:256]).then_inc(s_ub, 1)
            take(0, 1)
            v.wait_ge(s_hp, 2)
            v.tensor_copy(hsum[:, 0:D], ps[5][:, 256:384]).then_inc(s_ub, 1)
            batch(1, 1, exp=False, route=False)
            batch(2, 0, route=False)
            batch(3, 1)
            with v.Fori(2, NB // 2) as o:
                for par in range(2):
                    batch(2 * o + par, par)
            l, m, r = NB - 1, NB - 2, NB - 3
            lst, est, mst = log_steps(l), exp_steps(l), exp_steps(m)
            rch, mch, lch = choice_steps(r), choice_steps(m), choice_steps(l)
            exp_bound(m)
            take(l, 2)
            exp_root(m, mst)
            take(l, 3)
            divide(l, elu_steps(l))
            residual(m, m % 2, mst)
            choice1(r, r % 2, rch)
            elu(l, l % 2)
            choice2(r, r % 2, rch)
            log_bounds(l, lst)
            log_roots(l, lst)
            log_scale(l)
            place(r, r % 2, place_steps(r))
            variance(m)
            norm_scale(m, m % 2, mst)
            exp_bound(l)
            exp_root(l, est)
            residual(l, l % 2, est)
            copy_turned(m)
            choice1(m, m % 2, mch)
            variance(l)
            choice2(m, m % 2, mch)
            norm_scale(l, l % 2, est)
            place(m, m % 2, place_steps(m))
            copy_turned(l)
            choice1(l, l % 2, lch)
            choice2(l, l % 2, lch)
            place(l, l % 2, place_steps(l))

            v.wait_ge(s_sl, NB)
            v.tensor_copy(padrow[:], run[:]).then_inc(s_pad, 1)
            st.step(TT(cnt[:, 0, :], run[:], region0[:], ALU.subtract))
            st.step(TS(cnt[:, 0, :], cnt[:, 0, :], float(P - 1), None, ALU.add))
            st.step(v.tensor_copy(cnti[:, 0, :], cnt[:, 0, :]))
            st.step(TS(cnti[:, 1, :], cnti[:, 0, :], 7, None, ALU.arith_shift_right))
            st.step(v.tensor_copy(cnt[:, 1, :], cnti[:, 1, :]))
            st.step(v.tensor_copy(cnt[:, 2, :], cnt[:, 1, :]))
            for sh in (1, 2, 4):
                a, z = (2, 3) if sh != 2 else (3, 2)
                st.did(v.tensor_copy(cnt[:, z, 0:sh], cnt[:, a, 0:sh]))
                st.step(TT(cnt[:, z, sh:E], cnt[:, a, sh:E], cnt[:, a, 0:E - sh], ALU.add))
            slots = slotno[:].unsqueeze(2).to_broadcast([P, SLOTS, E])
            st.step(TT(cmpb, cnt[:, 3, :].unsqueeze(1).to_broadcast([P, SLOTS, E]), slots, ALU.is_le))
            st.step(v.reduce_sum(tabs[:, 0, :], cmpb, AX_X))
            st.step(TT(cmpb, cmpb, cnt[:, 1, :].unsqueeze(1).to_broadcast([P, SLOTS, E]), ALU.mult))
            st.step(v.reduce_sum(tabs[:, 1, :], cmpb, AX_X))
            st.step(TT(tabs[:, 1, :], slotno[:], tabs[:, 1, :], ALU.subtract))
            st.step(TS(tabs[:, 1, :], tabs[:, 1, :], float(P), None, ALU.mult))
            st.step(STT(out=tabs[:, 1, :], in0=tabs[:, 0, :], scalar=float(REGION), in1=tabs[:, 1, :],
                        op0=ALU.mult, op1=ALU.add))
            st.step(TS(tabs[:, 0, :], tabs[:, 0, :], float(E - 1), None, ALU.min))
            st.step(v.tensor_copy(tabi[:, 0, :], tabs[:, 1, :]))
            v.tensor_copy(tabi[:, 1, :], tabs[:, 0, :]).then_inc(s_tab, 1)
            v.wait_ge(s_tab, 1)

            def expert_of(s):
                return v.value_load(tabi[0:1, 1, bass.ds(s, 1)], min_val=0, max_val=E - 1)

            def fetch(s, j, e):
                if not (isinstance(s, int) and s < 4):
                    v.wait_ge(s_L1, s - 3)
                TS(w1c[:, j % 4, :], w1[:, bass.ds(e * H, H)], 1.0, None, ALU.mult)
                if not (isinstance(s, int) and s < 4):
                    v.wait_ge(s_ge, s - 3)
                TS(b1c[:, j % 4, :], b1t[:, bass.ds(e * HK, HK)], 1.0, None, ALU.mult)
                if not (isinstance(s, int) and s < 4):
                    v.wait_ge(s_L2, s - 3)
                TS(w2c[:, j % 4, :], w2[:, bass.ds(e * H, H)], 1.0, None, ALU.mult)
                if not (isinstance(s, int) and s < 8):
                    v.wait_ge(s_ya, s - 7)
                TS(b2c[:, j, :], b2b[:, bass.ds(e * D, D)], 1.0, None, ALU.mult).then_inc(s_wc, 1)

            def copy_rows(s, j):
                v.wait_ge(s_T, s + 1)
                if not (isinstance(s, int) and s < 4):
                    v.wait_ge(s_L1, s - 3)
                v.tensor_copy(xsT[:, j % 4, :], ps[(4, 7)[j % 2]][:, 0:P]).then_inc(s_Tc, 1)

            def result(s, j):
                v.wait_ge(s_L2, s + 1)
                if not (isinstance(s, int) and s < 2):
                    v.wait_ge(s_ys, s - 1)
                TT(ya[:, j % 2, :], ps[5 + j % 2][:, 0:D], b2c[:, j, :], ALU.add).then_inc(s_ya, 1)
                if not (isinstance(s, int) and s < 4):
                    v.wait_ge(s_yo[j % 4], 4 * (s - j % 4))
                v.tensor_copy(yid[:, j % 4:j % 4 + 1], xs[:, j, D + 1:D + 2]).then_inc(s_yi, 1)

            v.wait_ge(s_w, 64)
            for s in range(4):
                fetch(s, s, expert_of(s))
                copy_rows(s, s)

            def slot_steps(s0, tiles):
                for j in range(8):
                    s = s0 + j
                    if j + 4 < tiles:
                        if j % 2 == 0:
                            e = expert_of(s + 4), expert_of(s + 5)
                        fetch(s + 4, (j + 4) % 8, e[j % 2])
                        copy_rows(s + 4, (j + 4) % 8)
                    result(s, j)

            slot_steps(0, SLOTS)
            with v.Fori(1, SLOTS // 8 - 1) as o:
                slot_steps(8 * o, SLOTS)
            slot_steps(SLOTS - 8, 8)

            for c in range(4):
                cs = slice(CH * c, CH * c + CH)
                v.wait_ge(s_pl[c], 32)
                TT(x[:, cs, :], x[:, cs, :], yplane[0][:, cs, :], ALU.add).then_inc(s_fs, 1)
                v.wait_ge(s_fs, c + 1)
                TT(x[:, cs, :], x[:, cs, :], yplane[1][:, cs, :], ALU.add).then_inc(s_fin, 1)


def kernel(**inputs):
    import concourse.bacc as bacc
    from concourse.bass_utils import run_bass_kernel_spmd

    a = {k: np.asarray(v) for k, v in inputs.items()}
    x = a["x"]
    wg = np.zeros((D, DC), x.dtype)
    wg[1:, :] = a["L0_gnn_W_gcn"]
    wa = a["L0_gnn_W_att"][1:, :]
    arrays = {
        "x_rows": x.reshape(NT, P, D).transpose(1, 0, 2),
        "xT": x.T,
        "adjT": a["adj"].reshape(NT, P, NT, P).transpose(0, 3, 2, 1).reshape(NT, P, N),
        "w_gcn": wg,
        "w_gcnT": wg.T,
        "w_att": wa,
        "w_attT": wa.T,
        "a2": a["L0_gnn_a_att"][D:, :],
        "gate_w": a["L0_ffn_Wg"],
        "gate_b": a["L0_ffn_bg"],
        "w1": a["L0_ffn_W1"].transpose(1, 0, 2).reshape(D, E * H),
        "b1": a["L0_ffn_b1"].reshape(E * HK, P).T,
        "w2": a["L0_ffn_W2"].reshape(E, HK, P, D).transpose(2, 0, 1, 3).reshape(P, E * HK * D),
        "b2": a["L0_ffn_b2"].reshape(E * D),
    }
    arrays = {k: np.ascontiguousarray(v) for k, v in arrays.items()}
    nc = bacc.Bacc("TRN2", target_bir_lowering=False, num_devices=1)
    args = [nc.dram_tensor(f"in_{k}", v.shape, mybir.dt.from_np(v.dtype), kind="ExternalInput").ap() for k, v in arrays.items()]
    out = nc.dram_tensor("out", (N, D), F32, kind="ExternalOutput").ap()
    gnn_moe_kernel(nc, *args, out)
    result = run_bass_kernel_spmd(nc, [{f"in_{k}": v for k, v in arrays.items()}], core_ids=[0])
    return result.results[0]["out"]
```
